# Optimizing a Trainium2 kernel written in Bass

```python
import numpy as np
import jax
import jax.numpy as jnp

def _softmax(x, axis=-1):
    return jax.nn.softmax(x, axis=axis)

def _gelu(x):
    return jax.nn.gelu(x, approximate=True)

def _silu(x):
    return jax.nn.silu(x)

def _sigmoid(x):
    return jax.nn.sigmoid(x)

def _layernorm(x, axis=-1, eps=1e-05):
    m = jnp.mean(x, axis=axis, keepdims=True)
    v = jnp.var(x, axis=axis, keepdims=True)
    return (x - m) / jnp.sqrt(v + eps)

def _scatter_add(tgt, idx, src, axis=0):
    return tgt.at[idx].add(src)

def _segment_sum(src, seg, n):
    return jax.ops.segment_sum(src, seg, n)
kernel_name = 'mk_gnn_ffn_d2_gnn_r8_39edf8'

def setup_inputs(seed: int=0):
    np.random.seed(seed)
    _w = jnp.asarray

    def _rec_inputs():
        import jax
        import jax.numpy as jnp
        _gk = jax.random.key(seed)
        x = 3.789e-05 + 1 * jax.random.normal(jax.random.fold_in(_gk, 1), (6250, 256), jnp.float32)
        _s = jax.random.randint(jax.random.fold_in(_gk, 2), (50000,), 0, 6250, jnp.int32)
        _d = jax.random.randint(jax.random.fold_in(_gk, 3), (50000,), 0, 6250, jnp.int32)
        _loop = jnp.arange(6250, dtype=jnp.int32)
        src = jnp.concatenate([_s, _d, _loop])
        dst = jnp.concatenate([_d, _s, _loop])
        _o = jnp.argsort(dst, stable=True)
        src = src[_o]
        dst = dst[_o]
        edge_attr3_1x1 = jax.random.uniform(jax.random.fold_in(_gk, 12), (106250, 1, 1), jnp.float32, 0.0, 0.999998)
        return (x, src, dst, edge_attr3_1x1)
    x, src, dst, edge_attr3_1x1 = _rec_inputs()

    def _L0_gnn_setup():
        import jax, jax.numpy as jnp
        import numpy as np
        N, F_IN, H, OUT, E = (4000, 256, 4, 64, 64000)
        NEG_SLOPE = 0.2
        key = jax.random.key(seed)
        ks = jax.random.split(key, 7)
        return {'feat': jax.random.normal(ks[0], (N, F_IN), dtype=jnp.float32), 'dist': jax.random.uniform(ks[1], (E, 1, 1), dtype=jnp.float32), 'W': jax.random.normal(ks[2], (F_IN, H * OUT), dtype=jnp.float32) * (1.0 / np.sqrt(F_IN)), 'w_att_src': jax.random.normal(ks[3], (1, H, OUT), dtype=jnp.float32) * 0.1, 'w_att_dst': jax.random.normal(ks[4], (1, H, OUT), dtype=jnp.float32) * 0.1, 'src': jax.random.randint(ks[5], (E,), 0, N, dtype=jnp.int32), 'dst': jax.random.randint(ks[6], (E,), 0, N, dtype=jnp.int32)}
    _L0_gnn_all = _L0_gnn_setup()
    _L0_gnn_in = {k: v for k, v in _L0_gnn_all.items() if k in ('W', 'w_att_src', 'w_att_dst')}
    del _L0_gnn_all

    def _L0_ffn_setup():
        import jax, jax.numpy as jnp
        import numpy as np
        E = 8
        K = 2
        D = 256
        H = 512
        DOUT = 256
        EPS = 1e-05
        key = jax.random.key(seed)
        ks = jax.random.split(key, 9)
        s = 0.02
        return {'x': jax.random.normal(ks[0], (4, 1024, D), jnp.float32), 'gamma': 1.0 + 0.05 * jax.random.normal(ks[1], (D,), jnp.float32), 'beta': 0.05 * jax.random.normal(ks[2], (D,), jnp.float32), 'Wr': 0.01 * jax.random.normal(ks[3], (D, E), jnp.float32), 'br': jnp.zeros((E,), jnp.float32), 'W1': s * jax.random.normal(ks[4], (E, D, H), jnp.float32), 'b1': s * jax.random.normal(ks[5], (E, H), jnp.float32), 'W2': s * jax.random.normal(ks[6], (E, H, DOUT), jnp.float32), 'b2': s * jax.random.normal(ks[7], (E, DOUT), jnp.float32)}
    _L0_ffn_all = _L0_ffn_setup()
    _L0_ffn_in = {k: v for k, v in _L0_ffn_all.items() if k in ('gamma', 'beta', 'Wr', 'br', 'W1', 'b1', 'W2', 'b2')}
    del _L0_ffn_all

    def _L1_gnn_setup():
        import jax, jax.numpy as jnp
        import numpy as np
        N, E, IN_DIM, H, D = (6250, 100000, 256, 8, 32)
        ALPHA = 0.2
        key = jax.random.key(seed)
        ks = jax.random.split(key, 6)
        feat = jax.random.normal(ks[0], (N, IN_DIM), dtype=jnp.float32)
        src = jax.random.randint(ks[1], (E,), 0, N, dtype=jnp.int32)
        dst = jax.random.randint(ks[2], (E,), 0, N, dtype=jnp.int32)
        W = jax.random.normal(ks[3], (IN_DIM, H * D), dtype=jnp.float32) * 0.05
        attn_l = jax.random.normal(ks[4], (H, D), dtype=jnp.float32)
        attn_r = jax.random.normal(ks[5], (H, D), dtype=jnp.float32)
        return {'feat': feat, 'src': src, 'dst': dst, 'W': W, 'attn_l': attn_l, 'attn_r': attn_r}
    _L1_gnn_all = _L1_gnn_setup()
    _L1_gnn_in = {k: v for k, v in _L1_gnn_all.items() if k in ('W', 'attn_l', 'attn_r')}
    del _L1_gnn_all

    def _L1_ffn_setup():
        import math
        import jax, jax.numpy as jnp
        import numpy as np
        CAPACITY_FACTOR = 1.25
        TOP_K = 2
        LN_EPS = 1e-05

        def _layer_norm(x, gamma, beta):
            mu = jnp.mean(x, axis=-1, keepdims=True)
            var = jnp.var(x, axis=-1, keepdims=True)
            return (x - mu) * jax.lax.rsqrt(var + LN_EPS) * gamma + beta
        key = jax.random.key(seed)
        ks = jax.random.split(key, 4)
        B, S, D, F, E = (8, 512, 256, 512, 8)
        x = jax.random.normal(ks[0], (B, S, D), dtype=jnp.float32)
        Wr = jax.random.normal(ks[1], (D, E), dtype=jnp.float32) / np.sqrt(D)
        br = jnp.zeros((E,), jnp.float32)
        W1 = jax.random.normal(ks[2], (E, D, F), dtype=jnp.float32) / np.sqrt(D)
        b1 = jnp.zeros((E, F), jnp.float32)
        W2 = jax.random.normal(ks[3], (E, F, D), dtype=jnp.float32) / np.sqrt(F)
        b2 = jnp.zeros((E, D), jnp.float32)
        gamma = jnp.ones((D,), jnp.float32)
        beta = jnp.zeros((D,), jnp.float32)
        return {'x': x, 'Wr': Wr, 'br': br, 'W1': W1, 'b1': b1, 'W2': W2, 'b2': b2, 'gamma': gamma, 'beta': beta}
    _L1_ffn_all = _L1_ffn_setup()
    _L1_ffn_in = {k: v for k, v in _L1_ffn_all.items() if k in ('Wr', 'br', 'W1', 'b1', 'W2', 'b2', 'gamma', 'beta')}
    del _L1_ffn_all
    return {'x': x, 'src': src, 'dst': dst, 'edge_attr3_1x1': edge_attr3_1x1, 'L0_gnn_W': _L0_gnn_in['W'], 'L0_gnn_w_att_src': _L0_gnn_in['w_att_src'], 'L0_gnn_w_att_dst': _L0_gnn_in['w_att_dst'], 'L0_ffn_gamma': _L0_ffn_in['gamma'], 'L0_ffn_beta': _L0_ffn_in['beta'], 'L0_ffn_Wr': _L0_ffn_in['Wr'], 'L0_ffn_br': _L0_ffn_in['br'], 'L0_ffn_W1': _L0_ffn_in['W1'], 'L0_ffn_b1': _L0_ffn_in['b1'], 'L0_ffn_W2': _L0_ffn_in['W2'], 'L0_ffn_b2': _L0_ffn_in['b2'], 'L1_gnn_W': _L1_gnn_in['W'], 'L1_gnn_attn_l': _L1_gnn_in['attn_l'], 'L1_gnn_attn_r': _L1_gnn_in['attn_r'], 'L1_ffn_Wr': _L1_ffn_in['Wr'], 'L1_ffn_br': _L1_ffn_in['br'], 'L1_ffn_W1': _L1_ffn_in['W1'], 'L1_ffn_b1': _L1_ffn_in['b1'], 'L1_ffn_W2': _L1_ffn_in['W2'], 'L1_ffn_b2': _L1_ffn_in['b2'], 'L1_ffn_gamma': _L1_ffn_in['gamma'], 'L1_ffn_beta': _L1_ffn_in['beta']}

def reference(x, src, dst, edge_attr3_1x1, L0_gnn_W, L0_gnn_w_att_src, L0_gnn_w_att_dst, L0_ffn_gamma, L0_ffn_beta, L0_ffn_Wr, L0_ffn_br, L0_ffn_W1, L0_ffn_b1, L0_ffn_W2, L0_ffn_b2, L1_gnn_W, L1_gnn_attn_l, L1_gnn_attn_r, L1_ffn_Wr, L1_ffn_br, L1_ffn_W1, L1_ffn_b1, L1_ffn_W2, L1_ffn_b2, L1_ffn_gamma, L1_ffn_beta):
    import jax
    import jax.numpy as jnp

    def _L0_gnn_ref(feat, dist, W, w_att_src, w_att_dst, src, dst):
        import jax, jax.numpy as jnp
        import numpy as np
        N, F_IN, H, OUT, E = (4000, 256, 4, 64, 64000)
        NEG_SLOPE = 0.2
        n = feat.shape[0]
        ft = (feat @ W).reshape(n, H, OUT)
        e_src = jnp.sum(ft * w_att_src, axis=-1, keepdims=True)
        e_dst = jnp.sum(ft * w_att_dst, axis=-1, keepdims=True)
        e = e_src[src] + e_dst[dst]
        e = jnp.where(e >= 0, e, NEG_SLOPE * e)
        emax = jax.ops.segment_max(e, dst, num_segments=n)
        ex = jnp.exp(e - emax[dst])
        denom = jax.ops.segment_sum(ex, dst, num_segments=n)
        a = ex / denom[dst] * dist
        m = ft[src] * a
        out = jax.ops.segment_sum(m, dst, num_segments=n)
        return out.reshape(n, H * OUT)

    def _L0_ffn_ref(x, gamma, beta, Wr, br, W1, b1, W2, b2):
        import jax, jax.numpy as jnp
        import numpy as np
        E = 8
        K = 2
        D = 256
        H = 512
        DOUT = 256
        EPS = 1e-05
        mu = jnp.mean(x, axis=-1, keepdims=True)
        var = jnp.mean(jnp.square(x - mu), axis=-1, keepdims=True)
        xn = (x - mu) * jax.lax.rsqrt(var + EPS) * gamma + beta
        logits = jnp.einsum('bsd,de->bse', xn, Wr) + br
        top_vals, top_idx = jax.lax.top_k(logits, K)
        w = jax.nn.softmax(top_vals, axis=-1)
        w_full = jnp.einsum('bsk,bske->bse', w, jax.nn.one_hot(top_idx, E, dtype=w.dtype))
        y = jnp.zeros(x.shape[:-1] + (DOUT,), x.dtype)
        for e in range(E):
            h = jax.nn.gelu(jnp.einsum('bsd,dh->bsh', xn, W1[e]) + b1[e], approximate=False)
            y_e = jnp.einsum('bsh,hd->bsd', h, W2[e]) + b2[e]
            y = y + y_e * w_full[..., e, None]
        return y

    def _L1_gnn_ref(feat, src, dst, W, attn_l, attn_r):
        import jax, jax.numpy as jnp
        import numpy as np
        N, E, IN_DIM, H, D = (6250, 100000, 256, 8, 32)
        ALPHA = 0.2
        n = feat.shape[0]
        ft = (feat @ W).reshape(n, H, D)
        a1 = jnp.einsum('nhd,hd->nh', ft, attn_l)
        a2 = jnp.einsum('nhd,hd->nh', ft, attn_r)
        e = jax.nn.leaky_relu(a1[src] + a2[dst], negative_slope=ALPHA)
        m = jax.ops.segment_max(e, dst, num_segments=n)
        ex = jnp.exp(e - m[dst])
        s = jax.ops.segment_sum(ex, dst, num_segments=n)
        alpha = ex / s[dst]
        msg = ft[src] * alpha[:, :, None]
        out = jax.ops.segment_sum(msg, dst, num_segments=n)
        return jax.nn.elu(out.reshape(n, H * D))

    def _L1_ffn_ref(x, Wr, br, W1, b1, W2, b2, gamma, beta):
        import math
        import jax, jax.numpy as jnp
        import numpy as np
        CAPACITY_FACTOR = 1.25
        TOP_K = 2
        LN_EPS = 1e-05

        def _layer_norm(x, gamma, beta):
            mu = jnp.mean(x, axis=-1, keepdims=True)
            var = jnp.var(x, axis=-1, keepdims=True)
            return (x - mu) * jax.lax.rsqrt(var + LN_EPS) * gamma + beta
        B, S, D = x.shape
        E = Wr.shape[1]
        N = B * S
        K = TOP_K
        logits = jnp.mean(x, axis=1) @ Wr + br
        routing_weights = jax.nn.softmax(logits, axis=-1)
        capacity = float(math.ceil(N * CAPACITY_FACTOR / E))
        expected_loads = routing_weights.sum(axis=0) * (N / B)
        scale = jnp.where(expected_loads > capacity, capacity / expected_loads, 1.0)
        routing_weights = jax.nn.softmax(routing_weights * scale, axis=-1)
        rw_tok = jnp.broadcast_to(routing_weights[:, None, :], (B, S, E)).reshape(N, E)
        top_w, top_i = jax.lax.top_k(rw_tok, K)
        top_w = jax.nn.softmax(top_w, axis=-1)
        xf = x.reshape(N, D)
        h = jax.nn.gelu(jnp.einsum('nd,edf->enf', xf, W1) + b1[:, None, :], approximate=False)
        y = jnp.einsum('enf,efd->end', h, W2) + b2[:, None, :]
        w_dense = jnp.zeros((N, E), x.dtype).at[jnp.arange(N)[:, None], top_i].add(top_w)
        out = jnp.einsum('ne,end->nd', w_dense, y).reshape(B, S, D)
        out = _layer_norm(out + x, gamma, beta)
        return out
    x = x + _L0_gnn_ref(_layernorm(x, axis=-1), edge_attr3_1x1, L0_gnn_W, L0_gnn_w_att_src, L0_gnn_w_att_dst, src, dst)
    x = x + _L0_ffn_ref(_layernorm(x, axis=-1)[None], L0_ffn_gamma, L0_ffn_beta, L0_ffn_Wr, L0_ffn_br, L0_ffn_W1, L0_ffn_b1, L0_ffn_W2, L0_ffn_b2)[0]
    x = x + _L1_gnn_ref(_layernorm(x, axis=-1), src, dst, L1_gnn_W, L1_gnn_attn_l, L1_gnn_attn_r)
    x = x + _L1_ffn_ref(_layernorm(x, axis=-1)[None], L1_ffn_Wr, L1_ffn_br, L1_ffn_W1, L1_ffn_b1, L1_ffn_W2, L1_ffn_b2, L1_ffn_gamma, L1_ffn_beta)[0]
    return x

_drawn_inputs = setup_inputs


def setup_inputs(seed=0):
    import zlib

    import numpy as np

    out = dict(_drawn_inputs(seed))
    spreads = {'L0_ffn_br': (0.0, 0.1),
     'L1_ffn_br': (0.0, 0.8),
     'L1_ffn_b1': (0.0, 0.356),
     'L1_ffn_b2': (0.0, 0.28),
     'L1_ffn_gamma': (1.0, 0.2),
     'L1_ffn_beta': (0.0, 0.1)}
    factors = {'L0_ffn_gamma': 5.058,
     'L0_ffn_beta': 4.049,
     'L0_ffn_b1': 8.0,
     'L0_ffn_b2': 3.488,
     'L1_ffn_Wr': 8.0}
    for name, (base, spread) in spreads.items():
        noise = np.random.default_rng([zlib.crc32(name.encode()), seed]).standard_normal(out[name].shape)
        drawn = base * np.exp(spread * noise) if base else spread * noise
        out[name] = jnp.asarray(drawn.astype(out[name].dtype))
    for name, factor in factors.items():
        out[name] = (out[name] * factor).astype(out[name].dtype)
    return out
```

```python
import concourse.bass as bass
from concourse import mybir
from contextlib import ExitStack, contextmanager

F32 = mybir.dt.float32
BF16 = mybir.dt.bfloat16
I32 = mybir.dt.int32
U32 = mybir.dt.uint32
ALU = mybir.AluOpType
ACT = mybir.ActivationFunctionType
AX = mybir.AxisListType
ENGINE = mybir.EngineType

N = 6250
D = 256
NE = 106250
P = 128
KD = D // P
TILES = 832
CH = 16
CHUNKS = TILES // CH
RING = 3
TB = 125
NB = N // TB
PADN = N + P
NSLOT = 4
G = 104
GT = TILES // G
GTOK = 2 * TB
NG = N // GTOK
E = 8
HID = 512
KH = HID // P
BIG = 1.0e30
EPS = 1e-5
SLOPE = 0.2
CAPACITY = 977.0
HEADS = (4, 8)


class Kernel:

    def __init__(self, nc, a):
        self.nc, self.a, self.sems = nc, a, {}
        self.root = ExitStack()
        self.stack = self.root

    def sem(self, name):
        if name not in self.sems:
            self.sems[name] = self.nc.alloc_semaphore(name=name)
        return self.sems[name]

    def sb(self, name, shape, dt=F32):
        return self.stack.enter_context(self.nc.sbuf_tensor(name, shape, dt))

    def stage(self, run, *args):
        run(self, *args)
        self.nc.clear_and_free_semaphores(list(self.sems.values()))
        self.nc.all_engine_barrier()
        self.sems = {}

    def dram(self, name, shape, dt=F32):
        return self.nc.dram_tensor(name, shape, dt, kind="Internal").ap()

    @contextmanager
    def phase(self):
        outer = self.stack
        with ExitStack() as self.stack:
            yield
        self.stack = outer


def emit(nc, a):
    k = Kernel(nc, a)
    with k.root:
        k.ps = k.root.enter_context(nc.psum_tensor("ps", [P, 8, 512], F32))
        k.acc = k.sb("acc", [P, 3, PADN])
        k.ident = k.sb("ident", [P, P])
        k.iota = k.sb("iota", [P, P])
        k.negpart = k.sb("negpart", [P, 1])
        k.ones = k.sb("ones", [P, 1])
        k.eps = k.sb("eps", [P, 1])
        k.seg = k.dram("seg_start_penalty", [TILES, P])
        k.segr = k.dram("seg_end_penalty", [TILES, P])
        k.reld = k.dram("rel_rows", [TILES, P], BF16)
        k.single = k.dram("single_segment", [1, TILES])
        k.first = k.dram("first_penalty", [1, TILES])
        k.x1 = k.dram("x1", [N, D])
        k.x2 = k.dram("x2", [N, D])
        k.x3 = k.dram("x3", [N, D])
        k.y3 = k.dram("y3", [N, D])
        with k.phase():
            k.srcE = k.sb("srcE", [P, TILES], I32)
            k.relE = k.sb("relE", [P, TILES])
            k.distE = k.sb("distE", [P, TILES])
            k.n0 = k.sb("n0", [1, TILES], I32)
            k.single_row = k.sb("single_row", [1, TILES])
            k.first_row = k.sb("first_row", [1, TILES])
            k.stage(prepare)
            k.stage(table, 0, a["x"], a["L0_gnn_W"], a["att0"])
            k.stage(edges, 0)
        with k.phase():
            k.logits = k.sb("logits", [TB, NB, E])
            k.stage(nodes, 0, a["x"], k.x1)
            k.stage(ffn0)
        with k.phase():
            k.srcE = k.sb("srcE1", [P, TILES], I32)
            k.relE = k.sb("relE1", [P, TILES])
            k.distE = None
            k.n0 = k.sb("n0_1", [1, TILES], I32)
            k.single_row = k.sb("single_row1", [1, TILES])
            k.first_row = k.sb("first_row1", [1, TILES])
            k.stage(reload)
            k.stage(table, 1, k.x2, a["L1_gnn_W"], a["att1"])
            k.stage(edges, 1)
        with k.phase():
            k.ysum = k.sb("ysum", [TB, D])
            k.stage(nodes, 1, k.x2, k.x3)
            with k.phase():
                k.stage(ffn1)


def prepare(k):
    nc, a = k.nc, k.a
    with k.phase():
        dT = k.sb("dT", [G, GT, P], I32)
        prevT = k.sb("prevT", [G, GT, P], I32)
        nextT = k.sb("nextT", [G, GT, P], I32)
        firstT = k.sb("firstT", [G, GT, 1])
        pen = k.sb("pen", [G, GT, P])
        penr = k.sb("penr", [G, GT, P])
        relT = k.sb("relT", [G, GT, P], BF16)
        lone = k.sb("lone", [G, GT])
        dE = k.sb("dE", [P, TILES], I32)
        n0E = k.sb("n0E", [P, TILES], I32)
        n0f = k.sb("n0f", [P, TILES])
        n0raw = k.sb("n0raw", [1, TILES], I32)
        loaded, step, stored = k.sem("prep_loaded"), k.sem("prep_step"), k.sem("prep_stored")
        rows_loaded = k.sem("prep_rows")
        view = lambda ap: ap.rearrange("(g p) e -> p g e", p=G)
        loads = [(dT[:, :, :], view(a["dst_t"])), (prevT[:, :, :], view(a["dst_prev_t"])),
                 (nextT[:, :, :], view(a["dst_next_t"])), (dE[:, :], a["dst_e"]),
                 (n0E[:, :], a["n0"].to_broadcast([P, TILES])), (n0raw[:, :], a["n0"]),
                 (k.srcE[:, :], a["src_e"]), (k.distE[:, :], a["dist_e"]),
                 (k.ident[:, :], a["ident"]), (k.iota[:, :], a["iota"]), (k.negpart[:, :], a["negpart"])]
        with nc.Block() as block:
            @block.sync
            def _(sp):
                for dst, src in loads:
                    sp.dma_start(dst, src).then_inc(loaded, 16)
                sp.wait_ge(step, 11)
                sp.dma_start(view(k.seg), pen[:, :, :]).then_inc(stored, 16)
                sp.dma_start(view(k.segr), penr[:, :, :]).then_inc(stored, 16)
                sp.dma_start(view(k.reld), relT[:, :, :]).then_inc(stored, 16)
                with nc.allow_non_contiguous_dma("832 words of each, once"):
                    sp.dma_start(k.single.rearrange("o (g p) -> p (o g)", p=G), lone[:, :]).then_inc(stored, 16)
                    sp.dma_start(k.first.rearrange("o (g p) -> p (o g)", p=G), pen[:, :, 0]).then_inc(stored, 16)
                sp.wait_ge(stored, 16 * 5)
                sp.dma_start(k.single_row[:, :], k.single).then_inc(rows_loaded, 16)
                sp.dma_start(k.first_row[:, :], k.first).then_inc(rows_loaded, 16)
                sp.wait_ge(rows_loaded, 32)

            @block.vector
            def _(dve):
                done = [0]

                def link(ins):
                    done[0] += 1
                    ins.then_inc(step, 1)
                    dve.wait_ge(step, done[0])

                link(nc.vector.memset(k.ones[:, :], 1.0))
                link(nc.vector.memset(k.eps[:, :], EPS))
                dve.wait_ge(loaded, 16 * len(loads))
                link(nc.vector.tensor_scalar(firstT[:, :, :], dT[:, :, 0:1], 0.0, None, ALU.max))
                link(nc.vector.tensor_tensor(relT[:, :, :], dT[:, :, :], firstT[:, :, :].to_broadcast([G, GT, P]), ALU.subtract))
                link(nc.vector.tensor_tensor(pen[:, :, :], dT[:, :, :], prevT[:, :, :], ALU.not_equal))
                link(nc.vector.tensor_scalar(pen[:, :, :], pen[:, :, :], -BIG, None, ALU.mult))
                link(nc.vector.tensor_tensor(penr[:, :, :], dT[:, :, :], nextT[:, :, :], ALU.not_equal))
                link(nc.vector.tensor_scalar(penr[:, :, :], penr[:, :, :], -BIG, None, ALU.mult))
                link(nc.vector.tensor_reduce(lone[:, :], pen[:, :, :], AX.X, ALU.min))
                link(nc.vector.tensor_scalar(k.n0[:, :], n0raw[:, :], 0.0, None, ALU.max))
                link(nc.vector.tensor_scalar(n0f[:, :], n0E[:, :], 0.0, None, ALU.max))
                link(nc.vector.tensor_tensor(k.relE[:, :], dE[:, :], n0f[:, :], ALU.subtract))


def reload(k):
    nc, a = k.nc, k.a
    with k.phase():
        dE = k.sb("dE1", [P, TILES], I32)
        n0E = k.sb("n0E1", [P, TILES], I32)
        n0f = k.sb("n0f1", [P, TILES])
        n0raw = k.sb("n0raw1", [1, TILES], I32)
        loaded, step = k.sem("reload_loaded"), k.sem("reload_step")
        loads = [(dE[:, :], a["dst_e"]), (n0E[:, :], a["n0"].to_broadcast([P, TILES])),
                 (n0raw[:, :], a["n0"]), (k.srcE[:, :], a["src_e"]),
                 (k.single_row[:, :], k.single), (k.first_row[:, :], k.first)]
        with nc.Block() as block:
            @block.sync
            def _(sp):
                for dst, src in loads:
                    sp.dma_start(dst, src).then_inc(loaded, 16)

            @block.vector
            def _(dve):
                dve.wait_ge(loaded, 16 * len(loads))
                nc.vector.tensor_scalar(k.n0[:, :], n0raw[:, :], 0.0, None, ALU.max)
                nc.vector.tensor_scalar(n0f[:, :], n0E[:, :], 0.0, None, ALU.max).then_inc(step, 1)
                dve.wait_ge(step, 1)
                nc.vector.tensor_tensor(k.relE[:, :], dE[:, :], n0f[:, :], ALU.subtract)


def norm_steps(k, tag, dve, act_wait, x, stats, mv, out, n):
    nc = k.nc
    nc.vector.bn_stats(stats, x).then_inc(k.sem(tag + "_stats"), 1)
    dve.wait_ge(k.sem(tag + "_stats"), n)
    dve.sem_inc(k.sem(tag + "_pause"), 1)
    nc.vector.bn_aggr(mv, stats).then_inc(k.sem(tag + "_var"), 1)
    dve.wait_ge(k.sem(tag + "_root"), n)
    nc.vector.reciprocal(mv[:, 1:2], mv[:, 1:2]).then_inc(k.sem(tag + "_rstd"), 1)
    dve.wait_ge(k.sem(tag + "_rstd"), n)
    return nc.vector.tensor_scalar(out, x, mv[:, 0:1], mv[:, 1:2], ALU.subtract, ALU.mult)


def root_step(k, tag, act, mv, n):
    act.wait_ge(k.sem(tag + "_var"), n)
    k.nc.scalar.activation(mv[:, 1:2], mv[:, 1:2], ACT.Sqrt, bias=k.eps[0:TB, :]).then_inc(k.sem(tag + "_root"), 1)


def table(k, layer, x, w, att):
    nc, H = k.nc, HEADS[layer]
    W = D + 2 * H
    t = f"tab{layer}"
    k.rows = k.dram(f"rows{layer}", [N, D + H])
    k.edst = k.dram(f"edst{layer}", [PADN, H])
    S = lambda name: k.sem(f"{t}_{name}")
    with k.phase():
        wsb = k.sb(t + "w", [P, KD, D])
        attsb = k.sb(t + "att", [P, KD, 2 * H])
        wT = k.sb(t + "wT", [P, KD, D])
        wext = k.sb(t + "wext", [P, KD, W])
        zpad = k.sb(t + "zpad", [P, H])
        xb = k.sb(t + "x", [TB, 2, D])
        xn = k.sb(t + "xn", [TB, 2, D])
        xt = k.sb(t + "xt", [P, 2, KD, TB])
        tb = k.sb(t + "tb", [TB, 2, W])
        st = k.sb(t + "st", [TB, 2, 6])
        mv = k.sb(t + "mv", [TB, 2, 2])
        psT = [k.ps[:, u, 0:KD * TB].rearrange("p (h n) -> p h n", h=KD) for u in range(2)]
        psO = [k.ps[0:TB, 2 + u, 0:W] for u in range(2)]
        psW, psA = k.ps[:, 4, 0:512].rearrange("p (h n) -> p h n", h=KD), k.ps[:, 5, 0:KD * 2 * H].rearrange("p (h n) -> p h n", h=KD)
        with nc.Block() as block:
            @block.sync
            def _(sp):
                sp.dma_start(wsb[:, :, :], w.rearrange("(h p) n -> p h n", p=P)).then_inc(S("w"), 16)
                sp.dma_start(attsb[:, :, :], att.rearrange("(h p) n -> p h n", p=P)).then_inc(S("w"), 16)

                def load(i, n, u, first=False):
                    if not first:
                        sp.wait_ge(S("normed"), n - 2)
                    sp.dma_start(xb[:, u, :], x[bass.ds(i, TB), :]).then_inc(S(f"x{u}"), 16)

                for u in range(2):
                    load(u * TB, u + 1, u, first=True)
                with sp.Fori(0, NB // 2 - 1) as i:
                    for u in range(2):
                        load(i * (2 * TB) + (2 + u) * TB, i * 2 + 3 + u, u)

            @block.vector
            def _(dve):
                nc.vector.memset(zpad[:, :], 0.0).then_inc(S("zpad"), 1)
                dve.wait_ge(S("wTp"), 1)
                nc.vector.tensor_copy(wT[:, :, :], psW).then_inc(S("wT"), 1)
                dve.wait_ge(S("w"), 32)
                nc.vector.tensor_copy(wext[:, :, 0:D], wsb[:, :, :]).then_inc(S("wext"), 1)
                dve.wait_ge(S("attp"), 1)
                nc.vector.tensor_copy(wext[:, :, D:W], psA).then_inc(S("wext"), 1)
                with dve.Fori(0, NB // 2) as i:
                    for u in range(2):
                        n = i * 2 + 1 + u
                        dve.wait_ge(S(f"x{u}"), i * 16 + 16)
                        last = norm_steps(k, t, dve, None, xb[:, u, :], st[:, u, :], mv[:, u, :], xn[:, u, :], n)
                        last.then_inc(S("normed"), 1)
                        dve.wait_ge(S("product"), n)
                        nc.vector.tensor_copy(tb[:, u, :], psO[u]).then_inc(S("row"), 1)

            @block.tensor
            def _(pe):
                pe.wait_ge(S("w"), 32)
                for m in range(KD):
                    for h in range(KD):
                        last = nc.tensor.transpose(psW[:, m, h * P:(h + 1) * P], wsb[:, h, m * P:(m + 1) * P], k.ident[:, :])
                last.then_inc(S("wTp"), 1)
                pe.wait_ge(S("wT"), 1)
                for h in range(KD):
                    for m in range(KD):
                        last = nc.tensor.matmul(psA[:, h, :], wT[:, m, h * P:(h + 1) * P], attsb[:, m, :],
                                                start=(m == 0), stop=(m == KD - 1))
                last.then_inc(S("attp"), 1)
                pe.wait_ge(S("wext"), 2)
                with pe.Fori(0, NB // 2) as i:
                    for u in range(2):
                        n = i * 2 + 1 + u
                        pe.wait_ge(S("normed"), n)
                        for h in range(KD):
                            last = nc.tensor.transpose(psT[u][:, h, :], xn[:, u, h * P:(h + 1) * P], k.ident[0:TB, 0:TB])
                        last.then_inc(S("turned"), 1)
                        pe.wait_ge(S("xt"), n)
                        for h in range(KD):
                            last = nc.tensor.matmul(psO[u], xt[:, u, h, :], wext[:, h, :], start=(h == 0), stop=(h == KD - 1))
                        last.then_inc(S("product"), 1)

            @block.gpsimd
            def _(pool):
                nc.gpsimd.memset(k.acc[:, :, :], 0.0).then_inc(S("cleared"), 1)

            @block.scalar
            def _(act):
                act.wait_ge(S("zpad"), 1)
                act.dma_start(k.edst[N:PADN, :], zpad[:, :]).then_inc(S("pad"), 16)
                act.wait_ge(S("pad"), 16)

                def block_steps(i, n, u, first=False):
                    root_step(k, t, act, mv[:, u, :], n)
                    act.wait_ge(S("turned"), n)
                    nc.scalar.copy(xt[:, u, :, :], psT[u]).then_inc(S("xt"), 1)
                    act.wait_ge(S("row"), n)
                    act.dma_start(k.rows[bass.ds(i, TB), :], tb[:, u, 0:D + H]).then_inc(S(f"stored{u}"), 16)
                    act.dma_start(k.edst[bass.ds(i, TB), :], tb[:, u, D + H:W]).then_inc(S(f"stored{u}"), 16)

                with act.Fori(0, NB // 2) as i:
                    for u in range(2):
                        block_steps(i * (2 * TB) + u * TB, i * 2 + 1 + u, u)
                        act.wait_ge(S(f"stored{u}"), i * 32 + 32)
                        act.sem_inc(S(f"free{u}"), 1)


def edges(k, layer):
    nc, a, H = k.nc, k.a, HEADS[layer]
    t = f"e{layer}"
    R = H * CH
    DH = D // H
    W = D + H
    S = lambda name: k.sem(f"edge{layer}_{name}")
    heads_of = [[h for h in range(H) if h * DH // P == s] for s in range(KD)] + [list(range(H))]
    with k.phase():
        g = k.sb(t + "g", [P, RING, CH, W])
        idx = k.sb(t + "idx", [P, RING, CH], I32)
        relc = k.sb(t + "relc", [P, RING, CH])
        relrow = k.sb(t + "relrow", [P, RING, CH * P], BF16)
        pen = k.sb(t + "pen", [R, RING, P])
        penr = k.sb(t + "penr", [R, RING, P])
        edw = k.sb(t + "edw", [P, RING, CH, H])
        absd = k.sb(t + "absd", [P, CH * P], BF16)
        pt = k.sb(t + "pt", [P, CH * P])
        zz = k.sb(t + "zz", [P, 2, R])
        ad = k.sb(t + "ad", [P, R])
        ll = k.sb(t + "ll", [P, 2, R])
        dd = k.sb(t + "dd", [P, R])
        wt = k.sb(t + "wt", [P, RING, R])
        wd = k.sb(t + "wd", [P, RING, R]) if layer == 0 else None
        scan1 = k.sb(t + "scan1", [R, P])
        scan2 = k.sb(t + "scan2", [R, P])
        scan3 = k.sb(t + "scan3", [R, P])
        cin = k.sb(t + "cin", [R, 1])
        cval = k.sb(t + "cval", [1, H, CH + 1])
        cpen = k.sb(t + "cpen", [1, H, CH + 1])
        carry = k.sb(t + "carry", [1, H, CH + 1])
        brought = k.sb(t + "brought", [1, R])
        ce = k.sb(t + "ce", [1, R])
        frow = k.sb(t + "frow", [1, R])
        fac = k.sb(t + "fac", [P, RING, 3, CH])
        mask = k.sb(t + "mask", [1, H * 3 * P])
        onehot = k.sb(t + "onehot", [P, NSLOT, P])
        msg = k.sb(t + "msg", [P, NSLOT, D])
        ps = k.ps
        psX, psR, psA, psF = ps[0:R, 4, 0:P], ps[:, 5, 0:R], ps[:, 6, 0:R], ps[:, 7, 0:3 * CH]
        psC, psC2 = ps[0:1, 7, 128:128 + R], ps[0:R, 4, 256:257]
        hj = lambda ap: ap.rearrange("p (h j) -> p h j", h=H)
        aggr = [ps[:, q, 0:3 * P].rearrange("p (s n) -> p s n", s=3) for q in range(NSLOT)]
        mk = mask[:, :].rearrange("o (h s p) -> o h s p", h=H, s=3)

        with nc.Block() as block:
            @block.gpsimd
            def _(pool):
                def gather(c, u, used=True):
                    if used:
                        pool.wait_ge(S("chunk_done"), c - (RING - 1))
                        pool.sem_inc(S("slot_taken"), 1)
                    nc.gpsimd.tensor_copy(idx[:, u, :], k.srcE[:, bass.ds(c * CH, CH)]).then_inc(S("idx"), 1)
                    pool.wait_ge(S("idx"), c + 1)
                    pool.sem_inc(S("idx_seen"), 1)
                    for j in range(CH):
                        nc.gpsimd.indirect_dma_start(
                            g[:, u, j, :], None, k.rows,
                            bass.IndirectOffsetOnAxis(ap=idx[:, u, j:j + 1].bitcast(U32), axis=0),
                        ).then_inc(S(f"gathered{u}"), 16)

                for c in range(RING):
                    gather(c, c, used=False)
                with pool.Fori(0, CHUNKS // RING - 1) as i:
                    for u in range(RING):
                        gather(i * RING + (RING + u), u)
                gather(CHUNKS - 1, 0)

            def gathered(eng, c, i, u):
                eng.wait_ge(S(f"gathered{u}"), i * (16 * CH) + 16 * CH)

            @block.sync
            def _(sp):
                sp.dma_start(mask[:, :], a[f"mask{layer}"]).then_inc(S("mask"), 16)

                def load(c, i, u, used=True):
                    _, at0 = nc.values_load_multi_w_load_instructions(
                        k.n0[0:1, bass.ds(c * CH, CH)], engines=[ENGINE.SP], min_val=0, max_val=N - 1,
                        skip_runtime_bounds_check_because="destinations are nodes, clamped at zero on the chip")
                    rows = nc.sync.snap(c * CH) if not isinstance(c, int) else c * CH
                    if used:
                        sp.wait_ge(S("weights"), c - (RING - 1))
                        sp.sem_inc(S("loads_free"), 1)
                    sem = S(f"loaded{u}")
                    sp.dma_start(relrow[:, u, :].rearrange("p (o n) -> p o n", o=1),
                                 k.reld[bass.ds(rows, CH), :].rearrange("(o t) e -> o (t e)", o=1).rearrange("(z o) n -> z o n", z=1).to_broadcast([P, 1, CH * P])).then_inc(sem, 16)
                    for h in range(H):
                        sp.dma_start(pen[h * CH:(h + 1) * CH, u, :], k.seg[bass.ds(rows, CH), :]).then_inc(sem, 16)
                        sp.dma_start(penr[h * CH:(h + 1) * CH, u, :], k.segr[bass.ds(rows, CH), :]).then_inc(sem, 16)
                    for j in range(CH):
                        sp.dma_start(edw[:, u, j, :], k.edst[bass.ds(at0[j], P), :]).then_inc(sem, 16)

                for c in range(RING):
                    load(c, 0, c, used=False)
                with sp.Fori(0, CHUNKS // RING - 1) as i:
                    for u in range(RING):
                        load(i * RING + (RING + u), i, u)
                load(CHUNKS - 1, 0, 0)

            LOADS = 16 * (1 + 2 * H + CH)

            def loaded(eng, i, u):
                eng.wait_ge(S(f"loaded{u}"), i * LOADS + LOADS)

            def act_scores(act, c, i, u):
                n = c + 1

                def first():
                    gathered(act, c, i, u)
                    act.wait_ge(S("diff"), n)
                    nc.scalar.copy(hj(zz[:, 0, :]), g[:, u, :, D:W].rearrange("p j h -> p h j")).then_inc(S("esrc"), 1)
                    nc.scalar.copy(relc[:, u, :], k.relE[:, bass.ds(c * CH, CH)]).then_inc(S("relc"), 1)
                    nc.scalar.copy(cpen[:, :, 1:CH + 1],
                                   k.single_row[0:1, bass.ds(c * CH, CH)].rearrange("o (z j) -> o z j", z=1).to_broadcast([1, H, CH])).then_inc(S("cpen"), 1)

                def onehots():
                    loaded(act, i, u)
                    nc.scalar.activation(absd[:, :], relrow[:, u, :], ACT.Abs, bias=k.negpart[:, :]).then_inc(S("absd"), 1)
                    act.wait_ge(S("absd"), n)
                    act.wait_ge(S("expanded"), n)
                    nc.scalar.activation(pt[:, :], absd[:, :], ACT.Relu, bias=k.ones[:, :], scale=-1.0).then_inc(S("pt"), 1)

                def to_column():
                    act.wait_ge(S("cin_ps"), n)
                    nc.scalar.copy(cin[:, :], psC2).then_inc(S("cin"), 1)

                def expand():
                    act.wait_ge(S("expanded"), n + 1)
                    act.wait_ge(S("frow_ready"), n)
                    nc.scalar.copy(hj(ad[:, :]), psA.rearrange("p (j h) -> p h j", h=H)).then_inc(S("ad"), 1)

                def running():
                    act.wait_ge(S("max_ps"), n)
                    nc.scalar.copy(zz[:, 1, :], psR).then_inc(S("maxed"), 1)

                def exps():
                    act.wait_ge(S("diff"), n + 1)
                    nc.scalar.activation(wt[:, u, :], dd[:, :], ACT.Exp).then_inc(S("exp"), 1)
                    act.wait_ge(S("frow_ready"), n + 1)
                    nc.scalar.activation(frow[:, :], ce[:, :], ACT.Exp).then_inc(S("frow"), 1)

                def facs():
                    act.wait_ge(S("fac_ps"), n)
                    nc.scalar.copy(fac[:, u, :, :], psF.rearrange("p (s j) -> p s j", s=3)).then_inc(S("fac"), 1)

                return [first, onehots, to_column, expand, running, exps, facs]

            def pe_scores(pe, c, i, u):
                n = c + 1

                def turn():
                    pe.wait_ge(S("esrc"), n)
                    pe.sem_inc(S("pause"), 1)
                    nc.tensor.transpose(psX, zz[:, 0, :], k.ident[:, :]).then_inc(S("esrc_t"), 1)

                def last_row():
                    pe.wait_ge(S("scan1"), n)
                    pe.sem_inc(S("pause"), 1)
                    nc.tensor.transpose(psC, scan1[:, P - 1:P], k.ident[0:R, 0:R]).then_inc(S("last_ps"), 1)

                def column():
                    pe.wait_ge(S("brought"), n)
                    nc.tensor.matmul(psC2, brought[:, :], k.ones[0:1, :], start=True, stop=True).then_inc(S("cin_ps"), 1)

                def expand():
                    pe.wait_ge(S("pt"), n)
                    for j in range(CH):
                        last = nc.tensor.matmul(psA[:, j * H:(j + 1) * H], pt[:, j * P:(j + 1) * P], edw[:, u, j, :],
                                                start=True, stop=True)
                    last.then_inc(S("expanded"), 1)

                def running():
                    pe.wait_ge(S("scan3"), n)
                    pe.sem_inc(S("pause"), 1)
                    nc.tensor.transpose(psR, scan3[:, :], k.ident[0:R, 0:R]).then_inc(S("max_ps"), 1)

                def facs():
                    pe.wait_ge(S("frow"), n + 1)
                    for s in range(3):
                        for h in heads_of[s]:
                            last = nc.tensor.matmul(psF[:, s * CH:(s + 1) * CH], mk[:, h, s, :], frow[:, h * CH:(h + 1) * CH],
                                                    start=(h == heads_of[s][0]), stop=(h == heads_of[s][-1]))
                    last.then_inc(S("fac_ps"), 1)

                return [turn, expand, last_row, column, running, facs]

            def dve_scores(dve, c, i, u):
                n = c + 1

                def local_max():
                    loaded(dve, i, u)
                    dve.wait_ge(S("esrc_t"), n)
                    nc.vector.tensor_tensor_scan(scan1[:, :], pen[:, u, :], psX, -BIG, ALU.add, ALU.max).then_inc(S("scan1"), 1)

                def carries():
                    dve.wait_ge(S("last_ps"), n)
                    dve.wait_ge(S("cpen"), n)
                    nc.vector.tensor_copy(cval[:, :, 1:CH + 1], hj(psC)).then_inc(S("cval"), 1)
                    dve.wait_ge(S("cval"), n)
                    nc.vector.tensor_tensor_scan(carry[:, :, :].rearrange("o h j -> o (h j)"), cpen[:, :, :].rearrange("o h j -> o (h j)"),
                                                 cval[:, :, :].rearrange("o h j -> o (h j)"), -BIG, ALU.add, ALU.max).then_inc(S("carry"), 1)
                    dve.wait_ge(S("carry"), n)
                    nc.vector.tensor_copy(hj(brought[:, :]), carry[:, :, 0:CH]).then_inc(S("brought"), 1)
                    nc.vector.tensor_copy(cval[:, :, 0:1], carry[:, :, CH:CH + 1]).then_inc(S("clast"), 1)

                def running_max():
                    dve.wait_ge(S("cin"), n)
                    nc.vector.tensor_tensor_scan(scan2[:, :], pen[:, u, :], psX, cin[:, :], ALU.add, ALU.max).then_inc(S("scan2"), 1)
                    dve.wait_ge(S("scan2"), n)
                    nc.vector.tensor_tensor_scan(scan3[:, ::-1], penr[:, u, ::-1], scan2[:, ::-1], -BIG, ALU.add, ALU.max).then_inc(S("scan3"), 1)

                def scores():
                    dve.wait_ge(S("ad"), n)
                    dve.wait_ge(S("maxed"), n)
                    nc.vector.tensor_tensor(zz[:, :, :], zz[:, :, :], ad[:, :].rearrange("p (z r) -> p z r", z=1).to_broadcast([P, 2, R]), ALU.add).then_inc(S("zz"), 1)
                    dve.wait_ge(S("zz"), n)
                    nc.vector.scalar_tensor_tensor(ll[:, :, :], zz[:, :, :], SLOPE, zz[:, :, :], ALU.mult, ALU.max).then_inc(S("ll"), 1)
                    dve.wait_ge(S("ll"), n)
                    dve.wait_ge(S("exp"), n)
                    nc.vector.tensor_tensor(dd[:, :], ll[:, 0, :], ll[:, 1, :], ALU.subtract).then_inc(S("diff"), 1)

                def factors():
                    dve.wait_ge(S("clast"), n)
                    dve.wait_ge(S("frow"), n)
                    first = k.first_row[0:1, bass.ds(c * CH, CH)].rearrange("o (z j) -> o z j", z=1).to_broadcast([1, H, CH])
                    nc.vector.tensor_tensor(hj(ce[:, :]), hj(brought[:, :]), first, ALU.add).then_inc(S("ce"), 1)
                    dve.wait_ge(S("ce"), (n - 1) * 4 + 1)
                    nc.vector.tensor_tensor(ce[:, :], ce[:, :], ad[0:1, :], ALU.add).then_inc(S("ce"), 1)
                    dve.wait_ge(S("ce"), (n - 1) * 4 + 2)
                    nc.vector.scalar_tensor_tensor(ce[:, :], ce[:, :], SLOPE, ce[:, :], ALU.mult, ALU.max).then_inc(S("ce"), 1)
                    dve.wait_ge(S("ce"), (n - 1) * 4 + 3)
                    nc.vector.tensor_tensor(ce[:, :], ce[:, :], ll[0:1, 1, :], ALU.subtract).then_inc(S("ce"), 1)
                    dve.wait_ge(S("ce"), (n - 1) * 4 + 4)
                    nc.vector.tensor_scalar(ce[:, :], ce[:, :], -200.0, None, ALU.max).then_inc(S("frow_ready"), 1)

                def weights():
                    dve.wait_ge(S("exp"), n + 1)
                    if layer == 0:
                        dist = k.distE[:, bass.ds(c * CH, CH)].rearrange("p (z j) -> p z j", z=1).to_broadcast([P, H, CH])
                        nc.vector.tensor_tensor(hj(wd[:, u, :]), hj(wt[:, u, :]), dist, ALU.mult).then_inc(S("weights"), 1)
                    else:
                        dve.sem_inc(S("weights"), 1)

                return [local_max, carries, running_max, scores, factors, weights]

            def dve_tile(dve, c, i, u, j, at0):
                n = c * CH + (j + 1)
                q = j % NSLOT
                w = (wd if layer == 0 else wt)

                def operands(j2):
                    m, q2 = c * CH + (j2 + 1), j2 % NSLOT
                    dve.wait_ge(S("summed"), m)
                    nc.vector.tensor_scalar(onehot[:, q2, :], k.iota[:, :], relc[:, u, j2:j2 + 1], None, ALU.is_equal).then_inc(S("operands"), 1)
                    nc.vector.tensor_tensor(msg[:, q2, :].rearrange("p (h d) -> p h d", h=H), g[:, u, j2, 0:D].rearrange("p (h d) -> p h d", h=H),
                                            hj(w[:, u, :])[:, :, j2:j2 + 1].to_broadcast([P, H, DH]), ALU.mult).then_inc(S("operands"), 1)

                if j == 0:
                    operands(0)
                    operands(1)
                window = k.acc[:, :, bass.ds(at0[j], P)]
                dve.wait_ge(S("added"), n + (NSLOT - 1))
                nc.vector.tensor_tensor(k.acc[:, :, bass.ds(at0[j], 1)], k.acc[:, :, bass.ds(at0[j], 1)], fac[:, u, :, j:j + 1], ALU.mult).then_inc(S("rescaled"), 1)
                if j + 2 < CH:
                    operands(j + 2)
                dve.wait_ge(S("summed"), n + NSLOT)
                dve.wait_ge(S("rescaled"), n)
                last = nc.vector.tensor_tensor(window, window, aggr[q], ALU.add)
                last.then_inc(S("added"), 1)
                if j == CH - 1:
                    dve.sem_inc(S("chunk_operands"), 1)

            def pe_tile(pe, c, i, u, j):
                n = c * CH + (j + 1)
                q = j % NSLOT
                pe.wait_ge(S("added"), n)
                pe.wait_ge(S("operands"), n * 2)
                for s in range(KD):
                    nc.tensor.matmul(aggr[q][:, s, :], msg[:, q, s * P:(s + 1) * P], onehot[:, q, :], start=True, stop=True)
                nc.tensor.matmul(aggr[q][0:H, KD, :], hj(wt[:, u, :])[:, :, j], onehot[:, q, :], start=True, stop=True).then_inc(S("summed"), 1)

            SCORE_AT = {"dve": {1: [0], 3: [1], 5: [2], 8: [3], 10: [4], 13: [5]},
                        "pe": {0: [0], 2: [1], 3: [2], 4: [3], 7: [4], 12: [5]}}

            @block.vector
            def _(dve):
                for q in range(NSLOT):
                    nc.vector.memset(ps[:, q, :], 0.0).then_inc(S("added"), 1)
                nc.vector.memset(cpen[:, :, :], -BIG).then_inc(S("carry_init"), 1)
                nc.vector.memset(cval[:, :, :], -BIG).then_inc(S("carry_init"), 1)
                dve.wait_ge(S("carry_init"), 2)
                dve.sem_inc(S("diff"), 1)
                dve.sem_inc(S("frow_ready"), 1)
                for step in dve_scores(dve, 0, 0, 0):
                    step()

                def turn(c, i, u, following=None):
                    _, at0 = nc.values_load_multi_w_load_instructions(
                        k.n0[0:1, bass.ds(c * CH, CH)], engines=[ENGINE.DVE], min_val=0, max_val=N - 1,
                        skip_runtime_bounds_check_because="destinations are nodes, clamped at zero on the chip")
                    dve.wait_ge(S("fac"), c + 1)
                    dve.wait_ge(S("relc"), c + 1)
                    dve.wait_ge(S("weights"), c + 1)
                    gathered(dve, c, i, u)
                    steps = dve_scores(dve, *following) if following else []
                    for j in range(CH):
                        dve_tile(dve, c, i, u, j, at0)
                        for s in SCORE_AT["dve"].get(j, []):
                            if steps:
                                steps[s]()
                    dve.wait_ge(S("added"), c * CH + (CH + NSLOT))
                    dve.sem_inc(S("chunk_done"), 1)

                with dve.Fori(0, CHUNKS // RING) as i:
                    for u in range(RING):
                        c = i * RING + u
                        u1 = (u + 1) % RING
                        turn(c, i, u, (i * RING + (u + 1), i + 1 if u1 == 0 else i, u1))
                turn(CHUNKS - 1, CHUNKS // RING, 0)

            @block.tensor
            def _(pe):
                pe.sem_inc(S("summed"), NSLOT)
                pe.sem_inc(S("expanded"), 1)
                pe.wait_ge(S("mask"), 16)
                for step in pe_scores(pe, 0, 0, 0):
                    step()

                def turn(c, i, u, following=None):
                    steps = pe_scores(pe, *following) if following else []
                    for j in range(CH):
                        pe_tile(pe, c, i, u, j)
                        for s in SCORE_AT["pe"].get(j, []):
                            if steps:
                                steps[s]()

                with pe.Fori(0, CHUNKS // RING) as i:
                    for u in range(RING):
                        u1 = (u + 1) % RING
                        turn(i * RING + u, i, u, (i * RING + (u + 1), i + 1 if u1 == 0 else i, u1))
                turn(CHUNKS - 1, CHUNKS // RING, 0)

            @block.scalar
            def _(act):
                act.sem_inc(S("exp"), 1)
                act.sem_inc(S("frow"), 1)
                act.wait_ge(S("carry_init"), 2)
                for step in act_scores(act, 0, 0, 0):
                    step()
                with act.Fori(0, CHUNKS // RING) as i:
                    for u in range(RING):
                        u1 = (u + 1) % RING
                        for step in act_scores(act, i * RING + (u + 1), i + 1 if u1 == 0 else i, u1):
                            step()


def nodes(k, layer, xin, xout):
    nc, a, H = k.nc, k.a, HEADS[layer]
    t = f"n{layer}"
    S = lambda name: k.sem(f"{t}_{name}")
    with k.phase():
        xb = k.sb(t + "x", [TB, 2, D])
        rden = k.sb(t + "rden", [H, 2, TB])
        spread = k.sb(t + "spread", [H, KD, P])
        onT = k.sb(t + "onT", [P, 2, KD, TB])
        x1 = k.sb(t + "x1", [TB, 2, D])
        y = k.sb(t + "y", [TB, 2, D])
        yt = k.sb(t + "yt", [P, 2, KD, TB])
        st = k.sb(t + "st", [TB, 2, 6])
        mv = k.sb(t + "mv", [TB, 2, 2])
        if layer == 0:
            st2 = k.sb(t + "st2", [TB, 2, 6])
            mv2 = k.sb(t + "mv2", [TB, 2, 2])
            y2 = k.sb(t + "y2", [TB, 2, D])
            gamma = k.sb(t + "gamma", [TB, D])
            beta = k.sb(t + "beta", [TB, D])
            wr = k.sb(t + "wr", [P, KD, E])
            br = k.sb(t + "br", [TB, E])
        else:
            neg = k.sb(t + "neg", [TB, 2, D])
            ex = k.sb(t + "ex", [TB, 2, D])
        ps = k.ps
        psB = [ps[:, u, 0:KD * TB].rearrange("p (h n) -> p h n", h=KD) for u in range(2)]
        psX = [ps[0:TB, 2 + u, 0:D] for u in range(2)]
        psY = [ps[:, 4 + u, 0:KD * TB].rearrange("p (h n) -> p h n", h=KD) for u in range(2)]
        psL = [ps[0:TB, 6 + u, 0:E] for u in range(2)]
        consts = [(spread[:, :, :], a[f"spread{layer}"])]
        if layer == 0:
            consts += [(gamma[:, :], a["L0_ffn_gamma"].to_broadcast([TB, D])), (beta[:, :], a["L0_ffn_beta"].to_broadcast([TB, D])),
                       (wr[:, :, :], a["L0_ffn_Wr"].rearrange("(h p) e -> p h e", p=P)), (br[:, :], a["L0_ffn_br"].to_broadcast([TB, E]))]
        ready = 16 * len(consts)
        with nc.Block() as block:
            @block.sync
            def _(sp):
                for dst, src in consts:
                    sp.dma_start(dst, src).then_inc(S("consts"), 16)

                def load(row, n, u, first=False):
                    if not first:
                        sp.wait_ge(S("sum"), n - 2)
                    sp.dma_start(xb[:, u, :], xin[bass.ds(row, TB), :]).then_inc(S(f"x{u}"), 16)

                for u in range(2):
                    load(u * TB, u + 1, u, first=True)
                with sp.Fori(0, NB // 2 - 1) as i:
                    for u in range(2):
                        load(i * (2 * TB) + (2 + u) * TB, i * 2 + 3 + u, u)

            @block.scalar
            def _(act):
                with act.Fori(0, NB // 2) as i:
                    for u in range(2):
                        n, row = i * 2 + 1 + u, i * (2 * TB) + u * TB
                        if layer == 1:
                            act.wait_ge(S("neg"), n)
                            nc.scalar.activation(ex[:, u, :], neg[:, u, :], ACT.Exp).then_inc(S("ex"), 1)
                        act.wait_ge(S("sum"), n)
                        act.dma_start(xout[bass.ds(row, TB), :], x1[:, u, :]).then_inc(S(f"xs{u}"), 16)
                        root_step(k, t, act, mv[:, u, :], n)
                        if layer == 0:
                            root_step(k, t + "b", act, mv2[:, u, :], n)
                        else:
                            act.wait_ge(S("y"), n)
                            act.dma_start(k.y3[bass.ds(row, TB), :], y[:, u, :]).then_inc(S(f"ys{u}"), 16)
                        act.wait_ge(S("yt_ps"), n)
                        act.wait_ge(S(f"placed"), n)
                        nc.scalar.copy(yt[:, u, :, :], psY[u]).then_inc(S("yt"), 1)
                        act.wait_ge(S(f"xs{u}"), i * 16 + 16)
                        act.sem_inc(S("x_stored"), 1)
                        if layer == 1:
                            act.wait_ge(S(f"ys{u}"), i * 16 + 16)
                            act.sem_inc(S("y_stored"), 1)

            @block.gpsimd
            def _(pool):
                pool.sem_inc(S("placed"), 2)
                if layer == 1:
                    nc.gpsimd.memset(k.ysum[:, :], 0.0).then_inc(S("ysum"), 1)
                with pool.Fori(0, NB // 2) as i:
                    for u in range(2):
                        n, row = i * 2 + 1 + u, i * (2 * TB) + u * TB
                        if layer == 1:
                            pool.wait_ge(S("y"), n)
                            pool.wait_ge(S("ysum"), n)
                            nc.gpsimd.tensor_tensor(k.ysum[:, :], k.ysum[:, :], y[:, u, :], ALU.add).then_inc(S("ysum"), 1)
                        pool.wait_ge(S("yt"), n)
                        pool.sem_inc(S("yt_seen"), 1)
                        nc.gpsimd.tensor_copy(k.acc[:, 0:KD, bass.ds(row, TB)], yt[:, u, :, :]).then_inc(S("placed"), 1)

            @block.tensor
            def _(pe):
                pe.wait_ge(S("consts"), ready)
                with pe.Fori(0, NB // 2) as i:
                    for u in range(2):
                        n = i * 2 + 1 + u
                        pe.wait_ge(S("rden"), n)
                        for h in range(KD):
                            last = nc.tensor.matmul(psB[u][:, h, :], spread[:, h, :], rden[:, u, :], start=True, stop=True)
                        last.then_inc(S("spread"), 1)
                        pe.wait_ge(S("onT"), n)
                        for h in range(KD):
                            last = nc.tensor.transpose(psX[u][:, h * P:(h + 1) * P], onT[:, u, h, :], k.ident[:, :])
                        last.then_inc(S("msg"), 1)
                        pe.wait_ge(S("y"), n)
                        src = y2 if layer == 0 else y
                        for h in range(KD):
                            last = nc.tensor.transpose(psY[u][:, h, :], src[:, u, h * P:(h + 1) * P], k.ident[0:TB, 0:TB])
                        last.then_inc(S("yt_ps"), 1)
                        if layer == 0:
                            pe.wait_ge(S("yt"), n)
                            for h in range(KD):
                                last = nc.tensor.matmul(psL[u], yt[:, u, h, :], wr[:, h, :], start=(h == 0), stop=(h == KD - 1))
                            last.then_inc(S("logit_ps"), 1)

            @block.vector
            def _(dve):
                dve.wait_ge(S("consts"), ready)
                dve.sem_inc(S("ready"), 1)
                with dve.Fori(0, NB // 2) as i:
                    for u in range(2):
                        n, row = i * 2 + 1 + u, i * (2 * TB) + u * TB
                        nc.vector.reciprocal(rden[:, u, :], k.acc[0:H, KD, bass.ds(row, TB)]).then_inc(S("rden"), 1)
                        dve.wait_ge(S("spread"), n)
                        nc.vector.tensor_tensor(onT[:, u, :, :], k.acc[:, 0:KD, bass.ds(row, TB)], psB[u], ALU.mult).then_inc(S("onT"), 1)
                        dve.wait_ge(S(f"x{u}"), i * 16 + 16)
                        dve.wait_ge(S("msg"), n)
                        if layer == 0:
                            nc.vector.tensor_tensor(x1[:, u, :], xb[:, u, :], psX[u], ALU.add).then_inc(S("sum"), 1)
                        else:
                            nc.vector.tensor_scalar(neg[:, u, :], psX[u], 0.0, None, ALU.min).then_inc(S("neg"), 1)
                            nc.vector.scalar_tensor_tensor(x1[:, u, :], psX[u], 0.0, xb[:, u, :], ALU.max, ALU.add).then_inc(S("pos"), 1)
                            dve.wait_ge(S("pos"), n)
                            dve.wait_ge(S("ex"), n)
                            nc.vector.scalar_tensor_tensor(x1[:, u, :], ex[:, u, :], -1.0, x1[:, u, :], ALU.add, ALU.add).then_inc(S("sum"), 1)
                        dve.wait_ge(S("sum"), n)
                        last = norm_steps(k, t, dve, None, x1[:, u, :], st[:, u, :], mv[:, u, :], y[:, u, :], n)
                        if layer == 0:
                            last.then_inc(S("y1"), 1)
                            dve.wait_ge(S("y1"), n)
                            norm_steps(k, t + "b", dve, None, y[:, u, :], st2[:, u, :], mv2[:, u, :], y2[:, u, :], n).then_inc(S("yn"), 1)
                            dve.wait_ge(S("yn"), n)
                            nc.vector.tensor_tensor(y2[:, u, :], y2[:, u, :], gamma[:, :], ALU.mult).then_inc(S("yg"), 1)
                            dve.wait_ge(S("yg"), n)
                            nc.vector.tensor_tensor(y2[:, u, :], y2[:, u, :], beta[:, :], ALU.add).then_inc(S("y"), 1)
                            dve.wait_ge(S("logit_ps"), n)
                            nc.vector.tensor_tensor(k.logits[:, bass.ds(i * 2 + u, 1), :].rearrange("p o e -> p (o e)"), psL[u], br[:, :], ALU.add).then_inc(S("logit"), 1)
                        else:
                            last.then_inc(S("y"), 1)
                        dve.wait_ge(S("x_stored"), n)
                        dve.sem_inc(S("free"), 1)
                        if layer == 1:
                            dve.wait_ge(S("y_stored"), n)
                            dve.wait_ge(S("ysum"), n + 1)
                            dve.sem_inc(S("free"), 1)


def ffn0(k):
    nc, a = k.nc, k.a
    S = lambda name: k.sem(f"f0_{name}")
    with k.phase():
        w1 = k.sb("f0w1", [P, E, KD, HID])
        w2 = k.sb("f0w2", [P, E, KH, D])
        b1 = k.sb("f0b1", [P, E, KH])
        b2 = k.sb("f0b2", [E, D])
        iota8 = k.sb("f0iota8", [TB, E])
        top = k.sb("f0top", [TB, NB, E])
        topi = k.sb("f0topi", [TB, NB, E], U32)
        idxf = k.sb("f0idxf", [TB, NB, 2])
        gap = k.sb("f0gap", [TB, NB, 1])
        e2 = k.sb("f0e2", [TB, NB, 1])
        p = k.sb("f0p", [TB, NB, 2])
        den = k.sb("f0den", [TB, NB, 1])
        hit = k.sb("f0hit", [TB, NB, E])
        wf = k.sb("f0wf", [TB, NB, E])
        ws = k.sb("f0ws", [TB, 2, E])
        wsT = k.sb("f0wsT", [E, 2, TB])
        xg = k.sb("f0xg", [TB, 2, D])
        yacc = k.sb("f0yacc", [TB, 2, D])
        hT = k.sb("f0hT", [P, 2, KH, GTOK])
        ps = k.ps
        psH = [[ps[:, 2 * q + c // 2, (c % 2) * 256:(c % 2) * 256 + GTOK] for c in range(KH)] for q in range(2)]
        psY = [ps[0:TB, 4 + q, :].rearrange("p (t d) -> p t d", t=2) for q in range(2)]
        psT = ps[0:E, 6, 0:2 * TB].rearrange("p (t n) -> p t n", t=2)
        psB = ps[0:TB, 7, :].rearrange("p (t d) -> p t d", t=2)
        with nc.Block() as block:
            @block.sync
            def _(sp):
                sp.dma_start(iota8[:, :], a["iota"][0:TB, 0:E]).then_inc(S("small"), 16)
                sp.dma_start(b1[:, :, :], a["L0_ffn_b1"].rearrange("e p c -> p e c")).then_inc(S("small"), 16)
                sp.dma_start(b2[:, :], a["L0_ffn_b2"]).then_inc(S("small"), 16)
                for e in range(E):
                    sp.dma_start(w1[:, e, :, :], a["L0_ffn_W1"][e].rearrange("(h p) n -> p h n", p=P)).then_inc(S("w"), 16)
                    sp.dma_start(w2[:, e, :, :], a["L0_ffn_W2"][e].rearrange("(c p) n -> p c n", p=P)).then_inc(S("w"), 16)
                with sp.Fori(0, NG) as i:
                    sp.wait_ge(S("xg_used"), i + 1)
                    sp.dma_start(xg[:, :, :], k.x1[bass.ds(i * GTOK, GTOK), :].rearrange("(t p) d -> p t d", p=TB)).then_inc(S("xg"), 16)
                    sp.wait_ge(S("summed"), i * E + (E + 1))
                    sp.dma_start(k.x2[bass.ds(i * GTOK, GTOK), :].rearrange("(t p) d -> p t d", p=TB), yacc[:, :, :]).then_inc(S("stored"), 16)
                    sp.wait_ge(S("stored"), i * 16 + 16)
                    sp.sem_inc(S("yacc_free"), 1)

            @block.gpsimd
            def _(pool):
                with pool.Fori(0, NG) as i:
                    pool.wait_ge(S("wf"), 1)
                    pool.wait_ge(S("summed"), i * E + 1)
                    pool.sem_inc(S("ws_free"), 1)
                    nc.gpsimd.tensor_copy(ws[:, :, :], wf[:, bass.ds(i * 2, 2), :]).then_inc(S("ws"), 1)

            @block.tensor
            def _(pe):
                pe.wait_ge(S("small"), 48)
                pe.wait_ge(S("w"), 32 * E)

                pe.sem_inc(S("down"), 2)

                def up(i, e):
                    m, q = i * E + (e + 1), e % 2
                    pe.wait_ge(S("gelu"), m)
                    for c in range(KH):
                        for h in range(KD):
                            last = nc.tensor.matmul(psH[q][c], w1[:, e, h, c * P:(c + 1) * P], k.acc[:, h, bass.ds(i * GTOK, GTOK)],
                                                    start=(h == 0), stop=(h == KD - 1))
                    last.then_inc(S("up"), 1)

                def down(i, e):
                    m, q = i * E + (e + 1), e % 2
                    pe.wait_ge(S("gelu"), m + 2)
                    pe.wait_ge(S("down_read"), m)
                    for tt in range(2):
                        for c in range(KH):
                            last = nc.tensor.matmul(psY[q][:, tt, :], hT[:, q, c, tt * TB:(tt + 1) * TB], w2[:, e, c, :],
                                                    start=(c == 0), stop=(c == KH - 1))
                    last.then_inc(S("down"), 1)

                with pe.Fori(0, NG) as i:
                    up(i, 0)
                    pe.wait_ge(S("ws"), i + 1)
                    pe.sem_inc(S("pause"), 1)
                    for tt in range(2):
                        last = nc.tensor.transpose(psT[:, tt, :], ws[:, tt, :], k.ident[0:TB, 0:TB])
                    last.then_inc(S("wsT_ps"), 1)
                    up(i, 1)
                    pe.wait_ge(S("wsT"), i + 1)
                    for tt in range(2):
                        last = nc.tensor.matmul(psB[:, tt, :], wsT[:, tt, :], b2[:, :], start=True, stop=True)
                    last.then_inc(S("bias"), 1)
                    for e in range(2, E):
                        down(i, e - 2)
                        up(i, e)
                    down(i, E - 2)
                    down(i, E - 1)

            @block.scalar
            def _(act):
                act.wait_ge(S("gap"), 1)
                nc.scalar.activation(e2[:, :, :], gap[:, :, :], ACT.Exp).then_inc(S("e2"), 1)
                act.sem_inc(S("gelu"), 2)
                act.wait_ge(S("small"), 48)
                with act.Fori(0, NG) as i:
                    for e in range(E):
                        m, q = i * E + (e + 1), e % 2
                        act.wait_ge(S("down"), m)
                        act.wait_ge(S("up"), m)
                        for c in range(KH):
                            last = nc.scalar.activation(hT[:, q, c, :], psH[q][c], ACT.Gelu, bias=b1[:, e, c:c + 1])
                        last.then_inc(S("gelu"), 1)

            @block.vector
            def _(dve):
                for b in range(NB):
                    nc.vector.max(top[:, b, :], k.logits[:, b, :]).then_inc(S("top"), 1)
                dve.wait_ge(S("top"), NB)
                for b in range(NB):
                    nc.vector.max_index(topi[:, b, :], top[:, b, :], k.logits[:, b, :]).then_inc(S("topi"), 1)
                nc.vector.tensor_tensor(gap[:, :, :], top[:, :, 1:2], top[:, :, 0:1], ALU.subtract).then_inc(S("gap"), 1)
                dve.wait_ge(S("topi"), NB)
                nc.vector.tensor_copy(idxf[:, :, :], topi[:, :, 0:2]).then_inc(S("idxf"), 1)
                dve.wait_ge(S("e2"), 1)
                nc.vector.tensor_scalar(den[:, :, :], e2[:, :, :], 1.0, None, ALU.add).then_inc(S("den"), 1)
                dve.wait_ge(S("den"), 1)
                nc.vector.reciprocal(p[:, :, 0:1], den[:, :, :]).then_inc(S("p"), 1)
                dve.wait_ge(S("p"), 1)
                nc.vector.tensor_tensor(p[:, :, 1:2], p[:, :, 0:1], e2[:, :, :], ALU.mult).then_inc(S("p"), 1)
                dve.wait_ge(S("p"), 2)
                dve.wait_ge(S("idxf"), 1)
                dve.wait_ge(S("small"), 48)
                each = iota8[:, :].rearrange("p (z e) -> p z e", z=1).to_broadcast([TB, NB, E])
                chain = [0]

                def link(ins):
                    chain[0] += 1
                    ins.then_inc(S("route"), 1)
                    dve.wait_ge(S("route"), chain[0])

                link(nc.vector.tensor_tensor(wf[:, :, :], each, idxf[:, :, 0:1].to_broadcast([TB, NB, E]), ALU.is_equal))
                link(nc.vector.tensor_tensor(wf[:, :, :], wf[:, :, :], p[:, :, 0:1].to_broadcast([TB, NB, E]), ALU.mult))
                link(nc.vector.tensor_tensor(hit[:, :, :], each, idxf[:, :, 1:2].to_broadcast([TB, NB, E]), ALU.is_equal))
                link(nc.vector.tensor_tensor(hit[:, :, :], hit[:, :, :], p[:, :, 1:2].to_broadcast([TB, NB, E]), ALU.mult))
                nc.vector.tensor_tensor(wf[:, :, :], wf[:, :, :], hit[:, :, :], ALU.add).then_inc(S("wf"), 1)
                dve.sem_inc(S("yacc_free"), 1)
                dve.sem_inc(S("xg_used"), 1)
                dve.sem_inc(S("summed"), 1)
                dve.sem_inc(S("down_read"), 2)
                with dve.Fori(0, NG) as i:
                    dve.wait_ge(S("wsT_ps"), i + 1)
                    nc.vector.tensor_copy(wsT[:, :, :], psT).then_inc(S("wsT"), 1)
                    dve.wait_ge(S("xg"), i * 16 + 16)
                    dve.wait_ge(S("bias"), i + 1)
                    dve.wait_ge(S("yacc_free"), i + 1)
                    nc.vector.tensor_tensor(yacc[:, :, :], xg[:, :, :], psB, ALU.add).then_inc(S("xg_used"), 1)
                    for e in range(E):
                        m, q = i * E + (e + 1), e % 2
                        dve.wait_ge(S("down"), m + 2)
                        dve.wait_ge(S("xg_used"), i + 2)
                        dve.wait_ge(S("summed"), m)
                        nc.vector.scalar_tensor_tensor(yacc[:, 0, :], psY[q][:, 0, :], ws[:, 0, e:e + 1], yacc[:, 0, :], ALU.mult, ALU.add)
                        nc.vector.scalar_tensor_tensor(yacc[:, 1, :], psY[q][:, 1, :], ws[:, 1, e:e + 1], yacc[:, 1, :], ALU.mult, ALU.add).then_inc(S("summed"), 1)
                        dve.wait_ge(S("summed"), m + 1)
                        dve.sem_inc(S("down_read"), 1)


def ffn1(k):
    nc, a = k.nc, k.a
    S = lambda name: k.sem(f"f1_{name}")
    K = 2
    w1 = k.sb("f1w1", [P, K, KD, HID])
    w2 = k.sb("f1w2", [P, K, KH, D])
    w2s = k.sb("f1w2s", [P, K, KH, D])
    b1 = k.sb("f1b1", [P, K, KH])
    b2 = k.sb("f1b2", [1, K, D])
    b2m = k.sb("f1b2m", [1, K, D])
    bias = k.sb("f1bias", [TB, D])
    gamma = k.sb("f1gamma", [TB, D])
    beta = k.sb("f1beta", [TB, D])
    wr = k.sb("f1wr", [P, KD, E])
    br = k.sb("f1br", [1, E])
    ones = k.sb("f1ones", [1, P])
    mean = k.sb("f1mean", [P, KD])
    row = k.sb("f1row", [1, 8, E])
    best = k.sb("f1best", [1, 8])
    besti = k.sb("f1besti", [1, 8], U32)
    pair = k.sb("f1pair", [1, 4])
    pcol = k.sb("f1pcol", [P, K])
    xg = k.sb("f1xg", [TB, 2, 2, D])
    yg = k.sb("f1yg", [TB, 2, 2, D])
    res = k.sb("f1res", [TB, 2, 2, D])
    st = k.sb("f1st", [TB, 2, 6])
    mv = k.sb("f1mv", [TB, 2, 2])
    hT = k.sb("f1hT", [P, 2, KH, GTOK])
    ps = k.ps
    psH = [[ps[:, 2 * q + c // 2, (c % 2) * 256:(c % 2) * 256 + GTOK] for c in range(KH)] for q in range(2)]
    psY = [ps[0:TB, 4 + tt, 0:D] for tt in range(2)]
    with nc.Block() as block:
        @block.sync
        def _(sp):
            for dst, src in [(gamma[:, :], a["L1_ffn_gamma"].to_broadcast([TB, D])), (beta[:, :], a["L1_ffn_beta"].to_broadcast([TB, D])),
                             (wr[:, :, :], a["L1_ffn_Wr"].rearrange("(h p) e -> p h e", p=P)), (br[:, :], a["L1_ffn_br"])]:
                sp.dma_start(dst, src).then_inc(S("small"), 16)
            sp.wait_ge(S("besti"), 1)
            _, which = nc.values_load_multi_w_load_instructions(
                besti[0:1, 0:K].bitcast(I32), engines=[ENGINE.SP], min_val=0, max_val=E - 1,
                skip_runtime_bounds_check_because="a place in a row of eight")
            for j in range(K):
                sp.dma_start(w1[:, j, :, :], a["L1_ffn_W1"][bass.ds(which[j], 1), :, :].rearrange("o (h p) n -> p (o h) n", p=P)).then_inc(S("w"), 16)
                sp.dma_start(w2[:, j, :, :], a["L1_ffn_W2"][bass.ds(which[j], 1), :, :].rearrange("o (c p) n -> p (o c) n", p=P)).then_inc(S("w"), 16)
                sp.dma_start(b1[:, j, :], a["L1_ffn_b1"][bass.ds(which[j], 1), :, :].rearrange("o p c -> p (o c)")).then_inc(S("w"), 16)
                sp.dma_start(b2[:, j, :], a["L1_ffn_b2"][bass.ds(which[j], 1), :]).then_inc(S("w"), 16)

        @block.tensor
        def _(pe):
            for h in range(KD):
                last = nc.tensor.matmul(ps[:, 0, h:h + 1], k.ysum[:, h * P:(h + 1) * P], k.ones[0:TB, :], start=True, stop=True)
            last.then_inc(S("mean_ps"), 1)
            pe.wait_ge(S("small"), 64)
            pe.wait_ge(S("mean"), 1)
            for h in range(KD):
                last = nc.tensor.matmul(ps[0:1, 1, 0:E], mean[:, h:h + 1], wr[:, h, :], start=(h == 0), stop=(h == KD - 1))
            last.then_inc(S("logit_ps"), 1)
            pe.wait_ge(S("pair"), 1)
            nc.tensor.matmul(ps[:, 2, 0:K], ones[:, :], pair[:, 0:K], start=True, stop=True).then_inc(S("pcol_ps"), 1)
            pe.wait_ge(S("b2m"), 1)
            for j in range(K):
                last = nc.tensor.matmul(ps[0:TB, 3, 0:D], ones[:, 0:TB], b2m[:, j, :], start=(j == 0), stop=(j == K - 1))
            last.then_inc(S("bias_ps"), 1)

        @block.scalar
        def _(act):
            act.wait_ge(S("mean_ps"), 1)
            nc.scalar.mul(mean[:, :], ps[:, 0, 0:KD], 1.0 / N).then_inc(S("mean"), 1)
            for n in range(2):
                act.wait_ge(S("shifted"), n + 1)
                nc.scalar.activation(row[:, 2, :], row[:, 1, :], ACT.Exp).then_inc(S("ex"), 1)
            act.wait_ge(S("gap"), 1)
            nc.scalar.activation(pair[:, 3:4], pair[:, 2:3], ACT.Exp).then_inc(S("ex"), 1)

        @block.vector
        def _(dve):
            done = [0]

            def link(ins):
                done[0] += 1
                ins.then_inc(S("chain"), 1)
                dve.wait_ge(S("chain"), done[0])

            link(nc.vector.memset(ones[:, :], 1.0))
            dve.wait_ge(S("logit_ps"), 1)
            link(nc.vector.tensor_tensor(row[:, 0, :], ps[0:1, 1, 0:E], br[:, :], ALU.add))

            def softmax(n):
                link(nc.vector.tensor_reduce(row[:, 4, 0:1], row[:, 0, :], AX.X, ALU.max))
                nc.vector.tensor_scalar(row[:, 1, :], row[:, 0, :], row[:, 4, 0:1], None, ALU.subtract).then_inc(S("shifted"), 1)
                dve.wait_ge(S("ex"), n)
                link(nc.vector.tensor_reduce(row[:, 4, 1:2], row[:, 2, :], AX.X, ALU.add))
                link(nc.vector.reciprocal(row[:, 4, 2:3], row[:, 4, 1:2]))
                link(nc.vector.tensor_scalar(row[:, 3, :], row[:, 2, :], row[:, 4, 2:3], None, ALU.mult))

            softmax(1)
            link(nc.vector.tensor_scalar(row[:, 5, :], row[:, 3, :], float(N), CAPACITY, ALU.mult, ALU.max))
            link(nc.vector.reciprocal(row[:, 5, :], row[:, 5, :]))
            link(nc.vector.tensor_scalar(row[:, 5, :], row[:, 5, :], CAPACITY, None, ALU.mult))
            link(nc.vector.tensor_tensor(row[:, 0, :], row[:, 3, :], row[:, 5, :], ALU.mult))
            softmax(2)
            link(nc.vector.max(best[:, :], row[:, 3, :]))
            nc.vector.max_index(besti[:, :], best[:, :], row[:, 3, :]).then_inc(S("besti"), 1)
            nc.vector.tensor_tensor(pair[:, 2:3], best[:, 1:2], best[:, 0:1], ALU.subtract).then_inc(S("gap"), 1)
            dve.wait_ge(S("ex"), 3)
            link(nc.vector.tensor_scalar(row[:, 6, 0:1], pair[:, 3:4], 1.0, None, ALU.add))
            link(nc.vector.reciprocal(pair[:, 0:1], row[:, 6, 0:1]))
            nc.vector.tensor_tensor(pair[:, 1:2], pair[:, 0:1], pair[:, 3:4], ALU.mult).then_inc(S("pair"), 1)
            dve.wait_ge(S("pcol_ps"), 1)
            link(nc.vector.tensor_copy(pcol[:, :], ps[:, 2, 0:K]))
            dve.wait_ge(S("w"), 16 * 4 * K)
            for j in range(K):
                link(nc.vector.tensor_scalar(w2s[:, j, :, :], w2[:, j, :, :], pcol[:, j:j + 1], None, ALU.mult))
            link(nc.vector.tensor_scalar(b2m[:, 0, :], b2[:, 0, :], pcol[0:1, 0:1], None, ALU.mult))
            nc.vector.tensor_scalar(b2m[:, 1, :], b2[:, 1, :], pcol[0:1, 1:2], None, ALU.mult).then_inc(S("b2m"), 1)
            dve.wait_ge(S("bias_ps"), 1)
            nc.vector.tensor_copy(bias[:, :], ps[0:TB, 3, 0:D])

    with nc.Block() as block:
        @block.sync
        def _(sp):
            with sp.Fori(0, NG) as i:
                sp.wait_ge(S("taken"), i + 1)
                sp.dma_start(yg[:, 0, :, :], k.y3[bass.ds(i * GTOK, GTOK), :].rearrange("(t p) d -> p t d", p=TB)).then_inc(S("in"), 16)
                sp.dma_start(xg[:, 0, :, :], k.x3[bass.ds(i * GTOK, GTOK), :].rearrange("(t p) d -> p t d", p=TB)).then_inc(S("in"), 16)

        @block.tensor
        def _(pe):
            pe.sem_inc(S("down"), 2)
            with pe.Fori(0, NG) as i:
                for j in range(K):
                    pe.wait_ge(S("gelu"), i * K + (j + 1))
                    for c in range(KH):
                        for h in range(KD):
                            last = nc.tensor.matmul(psH[j][c], w1[:, j, h, c * P:(c + 1) * P], k.acc[:, h, bass.ds(i * GTOK, GTOK)],
                                                    start=(h == 0), stop=(h == KD - 1))
                    last.then_inc(S("up"), 1)
                pe.wait_ge(S("read"), i * 2 + 2)
                pe.wait_ge(S("gelu"), i * K + (K + 2))
                for tt in range(2):
                    for j in range(K):
                        for c in range(KH):
                            last = nc.tensor.matmul(psY[tt], hT[:, j, c, tt * TB:(tt + 1) * TB], w2s[:, j, c, :],
                                                    start=(j == 0 and c == 0), stop=(j == K - 1 and c == KH - 1))
                    last.then_inc(S("down"), 1)

        @block.scalar
        def _(act):
            act.sem_inc(S("gelu"), 2)
            with act.Fori(0, NG) as i:
                for j in range(K):
                    act.wait_ge(S("down"), i * 2 + 2)
                    act.wait_ge(S("up"), i * K + (j + 1))
                    for c in range(KH):
                        last = nc.scalar.activation(hT[:, j, c, :], psH[j][c], ACT.Gelu, bias=b1[:, j, c:c + 1])
                    last.then_inc(S("gelu"), 1)
                for tt in range(2):
                    root_step(k, "f1", act, mv[:, tt, :], i * 2 + (tt + 1))
                act.wait_ge(S("out"), i * 2 + 2)
                act.dma_start(a["out"][bass.ds(i * GTOK, GTOK), :].rearrange("(t p) d -> p t d", p=TB), res[:, 0, :, :]).then_inc(S("stored"), 16)
                act.wait_ge(S("stored"), i * 16 + 16)
                act.sem_inc(S("out_free"), 1)
            act.wait_ge(S("stored"), 16 * NG)

        @block.vector
        def _(dve):
            dve.sem_inc(S("taken"), 1)
            dve.sem_inc(S("read"), 2)
            dve.sem_inc(S("out_free"), 1)
            with dve.Fori(0, NG) as i:
                dve.wait_ge(S("in"), i * 32 + 32)
                for tt in range(2):
                    n = i * 2 + (tt + 1)
                    nc.vector.tensor_tensor(yg[:, 0, tt, :], yg[:, 0, tt, :], bias[:, :], ALU.add).then_inc(S("biased"), 1)
                    dve.wait_ge(S("biased"), n)
                    dve.wait_ge(S("down"), n + 2)
                    nc.vector.tensor_tensor(yg[:, 0, tt, :], psY[tt], yg[:, 0, tt, :], ALU.add).then_inc(S("read"), 1)
                    dve.wait_ge(S("read"), n + 2)
                    last = norm_steps(k, "f1", dve, None, yg[:, 0, tt, :], st[:, tt, :], mv[:, tt, :], yg[:, 1, tt, :], n)
                    last.then_inc(S("normed"), 1)
                    dve.wait_ge(S("normed"), n)
                    nc.vector.tensor_tensor(yg[:, 1, tt, :], yg[:, 1, tt, :], gamma[:, :], ALU.mult).then_inc(S("scaled"), 1)
                    dve.wait_ge(S("scaled"), n)
                    nc.vector.tensor_tensor(yg[:, 1, tt, :], yg[:, 1, tt, :], beta[:, :], ALU.add).then_inc(S("shift"), 1)
                    dve.wait_ge(S("shift"), n)
                    dve.wait_ge(S("out_free"), i + 1)
                    nc.vector.tensor_tensor(res[:, 0, tt, :], yg[:, 1, tt, :], xg[:, 0, tt, :], ALU.add).then_inc(S("out"), 1)
                dve.wait_ge(S("out"), i * 2 + 2)
                dve.sem_inc(S("taken"), 1)


_PLAIN = ["x", "L0_gnn_W", "L1_gnn_W", "L0_ffn_Wr", "L0_ffn_W1", "L0_ffn_W2", "L0_ffn_b2",
          "L1_ffn_Wr", "L1_ffn_W1", "L1_ffn_W2", "L1_ffn_b2"]
_ROWS = ["L0_ffn_gamma", "L0_ffn_beta", "L0_ffn_br", "L1_ffn_gamma", "L1_ffn_beta", "L1_ffn_br"]


def laid_out(inputs):
    import numpy as np

    out = {n: np.ascontiguousarray(inputs[n]) for n in _PLAIN}
    out.update({n: np.ascontiguousarray(inputs[n]).reshape(1, -1) for n in _ROWS})
    for n in ("L0_ffn_b1", "L1_ffn_b1"):
        out[n] = np.ascontiguousarray(np.asarray(inputs[n]).reshape(E, KH, P).transpose(0, 2, 1))
    pad = TILES * P - NE
    src, dst = np.asarray(inputs["src"]), np.asarray(inputs["dst"])
    dist = np.asarray(inputs["edge_attr3_1x1"]).reshape(-1)
    nodest = np.full(pad, -1, dst.dtype)
    dstp = np.concatenate([dst, nodest])
    edge_major = lambda v: np.ascontiguousarray(v.reshape(TILES, P).T)
    out["src_e"] = edge_major(np.concatenate([src, np.zeros(pad, src.dtype)]))
    out["dst_e"] = edge_major(dstp)
    out["dist_e"] = edge_major(np.concatenate([dist, np.zeros(pad, dist.dtype)]))
    out["dst_t"] = dstp.reshape(TILES, P)
    out["dst_prev_t"] = np.concatenate([np.full(1, -2, dst.dtype), dstp[:-1]]).reshape(TILES, P)
    out["dst_next_t"] = np.concatenate([dstp[1:], np.full(1, -2, dst.dtype)]).reshape(TILES, P)
    out["n0"] = np.ascontiguousarray(dstp[::P]).reshape(1, TILES)
    for layer, (left, right) in enumerate([("L0_gnn_w_att_src", "L0_gnn_w_att_dst"), ("L1_gnn_attn_l", "L1_gnn_attn_r")]):
        H = HEADS[layer]
        DH = D // H
        att = np.zeros((D, 2 * H), np.float32)
        for side, name in enumerate((left, right)):
            v = np.asarray(inputs[name]).reshape(H, DH)
            for h in range(H):
                att[h * DH:(h + 1) * DH, side * H + h] = v[h]
        out[f"att{layer}"] = att
        f = np.arange(D)
        spread = np.zeros((H, KD, P), np.float32)
        spread[f // DH, f // P, f % P] = 1
        out[f"spread{layer}"] = spread
        mask = np.zeros((H, 3, P), np.float32)
        mask[:, 0:KD, :] = spread
        mask[np.arange(H), KD, np.arange(H)] = 1
        out[f"mask{layer}"] = mask.reshape(1, -1)
    out["ident"] = np.eye(P, dtype=np.float32)
    out["iota"] = np.tile(np.arange(P, dtype=np.float32), (P, 1))
    out["negpart"] = -np.arange(P, dtype=np.float32).reshape(P, 1)
    return out


def kernel(**inputs):
    from concourse import bacc
    from concourse.bass_utils import run_bass_kernel_spmd as run

    nc = bacc.Bacc("TRN2", target_bir_lowering=False, num_devices=1)
    arrays = laid_out(inputs)
    aps = {n: nc.dram_tensor("in_" + n, v.shape, mybir.dt.from_np(v.dtype), kind="ExternalInput").ap() for n, v in arrays.items()}
    aps["out"] = nc.dram_tensor("out_0", (N, D), F32, kind="ExternalOutput").ap()
    emit(nc, aps)
    r = run(nc, [{"in_" + n: v for n, v in arrays.items()}], core_ids=[0])
    return r.results[0]["out_0"]
```

```python
import concourse.bass as bass
from concourse import mybir
from contextlib import ExitStack, contextmanager

F32 = mybir.dt.float32
BF16 = mybir.dt.bfloat16
I32 = mybir.dt.int32
U32 = mybir.dt.uint32
ALU = mybir.AluOpType
ACT = mybir.ActivationFunctionType
AX = mybir.AxisListType
ENGINE = mybir.EngineType

N = 6250
D = 256
NE = 106250
P = 128
KD = D // P
TILES = 832
CH = 16
CHUNKS = TILES // CH
RING = 3
TB = 125
NB = N // TB
BATCH = 5
ROWS = BATCH * TB
NBATCH = NB // BATCH
PADN = N + P
NSLOT = 4
AHEAD = 3
G = 104
GT = TILES // G
GTOK = 2 * TB
NG = N // GTOK
E = 8
HID = 512
KH = HID // P
BIG = 1.0e30
EPS = 1e-5
SLOPE = 0.2
CAPACITY = 977.0
ROWS_OF_TILE = 256
NT = (2 * N + E * (ROWS_OF_TILE - 1)) // ROWS_OF_TILE
MOST = -(-N // ROWS_OF_TILE)
HEADS = (4, 8)
ACT_TILES = ([1, 3, 5, 7, 9, 11, 13, 15], [3, 7, 11, 15])
SCHEDULE = {
    "dve": {0: ["scan_1"], 2: ["carries"], 3: ["bring", "carry_on"], 5: ["scan_2", "ce_1"], 6: ["scan_3"],
            8: ["backward", "sum_0"], 9: ["meet", "leaky_0", "ce_2"], 11: ["scan_4", "ce_3"], 13: ["sum_1"],
            14: ["leaky_1"], 15: ["diff", "ce_4", "ce_5", "weights"]},
    "pe": {1: ["turn"], 3: ["last_row"], 6: ["column"], 8: ["expand"], 9: ["first_row"], 12: ["column2"],
           14: ["running"], 15: ["factor"]},
    "act": {0: ["first", "small"], 2: ["abs0"], 4: ["abs1"], 6: ["pt0"], 8: ["pt1"], 11: ["expand"], 15: ["exps", "factor"]},
}


class Kernel:

    def __init__(self, nc, a):
        self.nc, self.a, self.sems = nc, a, {}
        self.root = ExitStack()
        self.stack = self.root

    def sem(self, name):
        if name not in self.sems:
            self.sems[name] = self.nc.alloc_semaphore(name=name)
        return self.sems[name]

    def sb(self, name, shape, dt=F32):
        return self.stack.enter_context(self.nc.sbuf_tensor(name, shape, dt))

    def stage(self, run, *args):
        run(self, *args)
        self.nc.clear_and_free_semaphores(list(self.sems.values()))
        self.nc.all_engine_barrier()
        self.sems = {}

    def dram(self, name, shape, dt=F32):
        return self.nc.dram_tensor(name, shape, dt, kind="Internal").ap()

    @contextmanager
    def phase(self):
        outer = self.stack
        with ExitStack() as self.stack:
            yield
        self.stack = outer


def emit(nc, a):
    k = Kernel(nc, a)
    with k.root:
        k.ps = k.root.enter_context(nc.psum_tensor("ps", [P, 8, 512], F32))
        k.acc = k.sb("acc", [P, 3, PADN])
        k.ident = k.sb("ident", [P, P])
        k.iota = k.sb("iota", [P, P])
        k.negpart = k.sb("negpart", [P, 1])
        k.ones = k.sb("ones", [P, 1])
        k.eps = k.sb("eps", [P, 1])
        k.seg = k.dram("seg_start_penalty", [TILES, P])
        k.segr = k.dram("seg_end_penalty", [TILES, P])
        k.reld = k.dram("rel_rows", [TILES, P], BF16)
        k.single = k.dram("single_segment", [1, TILES])
        k.first = k.dram("first_penalty", [1, TILES])
        k.x1 = k.dram("x1", [N, D])
        k.x2 = k.dram("x2", [N, D])
        k.x3 = k.dram("x3", [N, D])
        k.y3 = k.dram("y3", [N, D])
        k.xs = k.dram("xs", [NT * ROWS_OF_TILE, D])
        k.ys = k.dram("ys", [NT * ROWS_OF_TILE, D])
        with k.phase():
            k.srcE = k.sb("srcE", [P, TILES], I32)
            k.relE = k.sb("relE", [P, TILES])
            k.distE = k.sb("distE", [P, TILES])
            k.n0 = k.sb("n0", [1, TILES], I32)
            k.single_row = k.sb("single_row", [1, TILES])
            k.first_row = k.sb("first_row", [1, TILES])
            k.stage(prepare)
            k.stage(table, 0, a["x"], a["L0_gnn_W"], a["att0"])
            k.stage(edges, 0)
        with k.phase():
            k.logits = k.sb("logits", [TB, NB, E])
            k.stage(nodes, 0, a["x"], k.x1)
            ffn0(k)
        with k.phase():
            k.srcE = k.sb("srcE1", [P, TILES], I32)
            k.relE = k.sb("relE1", [P, TILES])
            k.distE = None
            k.n0 = k.sb("n0_1", [1, TILES], I32)
            k.single_row = k.sb("single_row1", [1, TILES])
            k.first_row = k.sb("first_row1", [1, TILES])
            k.stage(reload)
            k.stage(table, 1, k.x2, a["L1_gnn_W"], a["att1"])
            k.stage(edges, 1)
        with k.phase():
            k.ysum = k.sb("ysum", [TB, D])
            k.stage(nodes, 1, k.x2, k.x3)
            with k.phase():
                k.stage(ffn1)


def rows_of(ap, row):
    return ap[bass.ds(row, ROWS), :].rearrange("(b p) d -> p b d", p=TB)


def prepare(k):
    nc, a = k.nc, k.a
    with k.phase():
        dT = k.sb("dT", [G, GT, P], I32)
        prevT = k.sb("prevT", [G, GT, P], I32)
        nextT = k.sb("nextT", [G, GT, P], I32)
        firstT = k.sb("firstT", [G, GT, 1])
        pen = k.sb("pen", [G, GT, P])
        penr = k.sb("penr", [G, GT, P])
        relT = k.sb("relT", [G, GT, P], BF16)
        lone = k.sb("lone", [G, GT])
        dE = k.sb("dE", [P, TILES], I32)
        n0E = k.sb("n0E", [P, TILES], I32)
        n0f = k.sb("n0f", [P, TILES])
        n0raw = k.sb("n0raw", [1, TILES], I32)
        loaded, step, stored = k.sem("prep_loaded"), k.sem("prep_step"), k.sem("prep_stored")
        rows_loaded = k.sem("prep_rows")
        view = lambda ap: ap.rearrange("(g p) e -> p g e", p=G)
        loads = [(dT[:, :, :], view(a["dst_t"])), (prevT[:, :, :], view(a["dst_prev_t"])),
                 (nextT[:, :, :], view(a["dst_next_t"])), (dE[:, :], a["dst_e"]),
                 (n0E[:, :], a["n0"].to_broadcast([P, TILES])), (n0raw[:, :], a["n0"]),
                 (k.srcE[:, :], a["src_e"]), (k.distE[:, :], a["dist_e"]),
                 (k.ident[:, :], a["ident"]), (k.iota[:, :], a["iota"]), (k.negpart[:, :], a["negpart"])]
        with nc.Block() as block:
            @block.sync
            def _(sp):
                for dst, src in loads:
                    sp.dma_start(dst, src).then_inc(loaded, 16)
                sp.wait_ge(step, 11)
                sp.dma_start(view(k.seg), pen[:, :, :]).then_inc(stored, 16)
                sp.dma_start(view(k.segr), penr[:, :, :]).then_inc(stored, 16)
                sp.dma_start(view(k.reld), relT[:, :, :]).then_inc(stored, 16)
                with nc.allow_non_contiguous_dma("832 words of each, once"):
                    sp.dma_start(k.single.rearrange("o (g p) -> p (o g)", p=G), lone[:, :]).then_inc(stored, 16)
                    sp.dma_start(k.first.rearrange("o (g p) -> p (o g)", p=G), pen[:, :, 0]).then_inc(stored, 16)
                sp.wait_ge(stored, 16 * 5)
                sp.dma_start(k.single_row[:, :], k.single).then_inc(rows_loaded, 16)
                sp.dma_start(k.first_row[:, :], k.first).then_inc(rows_loaded, 16)
                sp.wait_ge(rows_loaded, 32)

            @block.vector
            def _(dve):
                done = [0]

                def link(ins):
                    done[0] += 1
                    ins.then_inc(step, 1)
                    dve.wait_ge(step, done[0])

                link(nc.vector.memset(k.ones[:, :], 1.0))
                link(nc.vector.memset(k.eps[:, :], EPS))
                dve.wait_ge(loaded, 16 * len(loads))
                link(nc.vector.tensor_scalar(firstT[:, :, :], dT[:, :, 0:1], 0.0, None, ALU.max))
                link(nc.vector.tensor_tensor(relT[:, :, :], dT[:, :, :], firstT[:, :, :].to_broadcast([G, GT, P]), ALU.subtract))
                link(nc.vector.tensor_tensor(pen[:, :, :], dT[:, :, :], prevT[:, :, :], ALU.not_equal))
                link(nc.vector.tensor_scalar(pen[:, :, :], pen[:, :, :], -BIG, None, ALU.mult))
                link(nc.vector.tensor_tensor(penr[:, :, :], dT[:, :, :], nextT[:, :, :], ALU.not_equal))
                link(nc.vector.tensor_scalar(penr[:, :, :], penr[:, :, :], -BIG, None, ALU.mult))
                link(nc.vector.tensor_reduce(lone[:, :], pen[:, :, :], AX.X, ALU.min))
                link(nc.vector.tensor_scalar(k.n0[:, :], n0raw[:, :], 0.0, None, ALU.max))
                link(nc.vector.tensor_scalar(n0f[:, :], n0E[:, :], 0.0, None, ALU.max))
                link(nc.vector.tensor_tensor(k.relE[:, :], dE[:, :], n0f[:, :], ALU.subtract))


def reload(k):
    nc, a = k.nc, k.a
    with k.phase():
        dE = k.sb("dE1", [P, TILES], I32)
        n0E = k.sb("n0E1", [P, TILES], I32)
        n0f = k.sb("n0f1", [P, TILES])
        n0raw = k.sb("n0raw1", [1, TILES], I32)
        loaded, step = k.sem("reload_loaded"), k.sem("reload_step")
        loads = [(dE[:, :], a["dst_e"]), (n0E[:, :], a["n0"].to_broadcast([P, TILES])),
                 (n0raw[:, :], a["n0"]), (k.srcE[:, :], a["src_e"]),
                 (k.single_row[:, :], k.single), (k.first_row[:, :], k.first)]
        with nc.Block() as block:
            @block.sync
            def _(sp):
                for dst, src in loads:
                    sp.dma_start(dst, src).then_inc(loaded, 16)

            @block.vector
            def _(dve):
                dve.wait_ge(loaded, 16 * len(loads))
                nc.vector.tensor_scalar(k.n0[:, :], n0raw[:, :], 0.0, None, ALU.max)
                nc.vector.tensor_scalar(n0f[:, :], n0E[:, :], 0.0, None, ALU.max).then_inc(step, 1)
                dve.wait_ge(step, 1)
                nc.vector.tensor_tensor(k.relE[:, :], dE[:, :], n0f[:, :], ALU.subtract)


def norm_steps(k, tag, dve, x, stats, mv, out, n, each=None):
    nc = k.nc
    count = x.shape[1]
    for b in range(count):
        last = nc.vector.bn_stats(stats[:, b, :], x[:, b, :])
    last.then_inc(k.sem(tag + "_stats"), 1)
    dve.wait_ge(k.sem(tag + "_stats"), n)
    dve.sem_inc(k.sem(tag + "_pause"), 1)
    for b in range(count):
        last = nc.vector.bn_aggr(mv[:, b, :], stats[:, b, :])
    last.then_inc(k.sem(tag + "_var"), 1)
    dve.wait_ge(k.sem(tag + "_root"), n)
    dve.sem_inc(k.sem(tag + "_pause"), 1)
    nc.vector.reciprocal(mv[:, :, 1:2], mv[:, :, 1:2]).then_inc(k.sem(tag + "_rstd"), 1)
    dve.wait_ge(k.sem(tag + "_rstd"), n)
    for b in range(count):
        last = nc.vector.tensor_scalar(out[:, b, :], x[:, b, :], mv[:, b, 0:1], mv[:, b, 1:2], ALU.subtract, ALU.mult)
        if each is not None:
            last.then_inc(each, 1)
    return last


def root_step(k, tag, act, mv, n):
    act.wait_ge(k.sem(tag + "_var"), n)
    k.nc.scalar.activation(mv[:, :, 1:2], mv[:, :, 1:2], ACT.Sqrt, bias=k.eps[0:TB, :]).then_inc(k.sem(tag + "_root"), 1)


def table(k, layer, x, w, att):
    nc, H = k.nc, HEADS[layer]
    W = D + 2 * H
    t = f"tab{layer}"
    k.rows = k.dram(f"rows{layer}", [N, D + H])
    k.edst = k.dram(f"edst{layer}", [PADN, H])
    S = lambda name: k.sem(f"{t}_{name}")
    with k.phase():
        wsb = k.sb(t + "w", [P, KD, D])
        attsb = k.sb(t + "att", [P, KD, 2 * H])
        wT = k.sb(t + "wT", [P, KD, D])
        wext = k.sb(t + "wext", [P, KD, W])
        zpad = k.sb(t + "zpad", [P, H])
        xb = k.sb(t + "x", [TB, 2, BATCH, D])
        xt = k.sb(t + "xt", [P, 2, KD, TB])
        tb = k.sb(t + "tb", [TB, 2, BATCH, W])
        st = k.sb(t + "st", [TB, 2, BATCH, 6])
        mv = k.sb(t + "mv", [TB, 2, BATCH, 2])
        psT = [k.ps[:, u, 0:KD * TB].rearrange("p (h n) -> p h n", h=KD) for u in range(2)]
        psO = [k.ps[0:TB, 2 + u, 0:W] for u in range(2)]
        psW, psA = k.ps[:, 4, 0:512].rearrange("p (h n) -> p h n", h=KD), k.ps[:, 5, 0:KD * 2 * H].rearrange("p (h n) -> p h n", h=KD)
        with nc.Block() as block:
            @block.sync
            def _(sp):
                sp.dma_start(wsb[:, :, :], w.rearrange("(h p) n -> p h n", p=P)).then_inc(S("w"), 16)
                sp.dma_start(attsb[:, :, :], att.rearrange("(h p) n -> p h n", p=P)).then_inc(S("w"), 16)

                def load(row, u):
                    sp.dma_start(xb[:, u, :, :], rows_of(x, row)).then_inc(S(f"x{u}"), 16)

                def store(row, n, u):
                    sp.wait_ge(S("row"), n * BATCH)
                    sp.dma_start(rows_of(k.rows, row), tb[:, u, :, 0:D + H]).then_inc(S(f"stored{u}"), 16)
                    sp.dma_start(rows_of(k.edst, row), tb[:, u, :, D + H:W]).then_inc(S(f"stored{u}"), 16)

                for u in range(2):
                    load(u * ROWS, u)
                with sp.Fori(0, NBATCH // 2 - 1) as i:
                    for u in range(2):
                        store(i * (2 * ROWS) + u * ROWS, i * 2 + (1 + u), u)
                        load(i * (2 * ROWS) + (2 + u) * ROWS, u)
                for u in range(2):
                    store((NBATCH - 2 + u) * ROWS, NBATCH - 1 + u, u)
                for u in range(2):
                    sp.wait_ge(S(f"stored{u}"), 32 + 32 * (NBATCH // 2))

            @block.vector
            def _(dve):
                nc.vector.memset(zpad[:, :], 0.0).then_inc(S("zpad"), 1)
                dve.wait_ge(S("wTp"), 1)
                nc.vector.tensor_copy(wT[:, :, :], psW).then_inc(S("wT"), 1)
                dve.wait_ge(S("w"), 32)
                nc.vector.tensor_copy(wext[:, :, 0:D], wsb[:, :, :]).then_inc(S("wext"), 1)
                dve.wait_ge(S("attp"), 1)
                nc.vector.tensor_copy(wext[:, :, D:W], psA).then_inc(S("wext"), 1)
                with dve.Fori(0, NBATCH // 2) as i:
                    for u in range(2):
                        dve.wait_ge(S(f"x{u}"), i * 16 + 16)
                        dve.sem_inc(S("pause"), 1)
                        norm_steps(k, t, dve, xb[:, u, :, :], st[:, u, :, :], mv[:, u, :, :], xb[:, u, :, :], i * 2 + (1 + u), S("normed"))

            @block.tensor
            def _(pe):
                pe.wait_ge(S("w"), 32)
                for m in range(KD):
                    for h in range(KD):
                        last = nc.tensor.transpose(psW[:, m, h * P:(h + 1) * P], wsb[:, h, m * P:(m + 1) * P], k.ident[:, :])
                last.then_inc(S("wTp"), 1)
                pe.wait_ge(S("wT"), 1)
                for h in range(KD):
                    for m in range(KD):
                        last = nc.tensor.matmul(psA[:, h, :], wT[:, m, h * P:(h + 1) * P], attsb[:, m, :],
                                                start=(m == 0), stop=(m == KD - 1))
                last.then_inc(S("attp"), 1)
                pe.wait_ge(S("wext"), 2)
                pe.sem_inc(S("row_read"), 2)

                def turn(m, u, b):
                    q = (u * BATCH + b) % 2
                    pe.wait_ge(S("normed"), m)
                    pe.sem_inc(S("pause"), 1)
                    for h in range(KD):
                        last = nc.tensor.transpose(psT[q][:, h, :], xb[:, u, b, h * P:(h + 1) * P], k.ident[0:TB, 0:TB])
                    last.then_inc(S("turned"), 1)

                def project(m, u, b):
                    q = (u * BATCH + b) % 2
                    pe.wait_ge(S("xt"), m)
                    pe.wait_ge(S("row_read"), m)
                    for h in range(KD):
                        last = nc.tensor.matmul(psO[q], xt[:, q, h, :], wext[:, h, :], start=(h == 0), stop=(h == KD - 1))
                    last.then_inc(S("product"), 1)

                with pe.Fori(0, NBATCH // 2) as i:
                    for u in range(2):
                        for b in range(BATCH + 1):
                            m = i * (2 * BATCH) + (u * BATCH + b + 1)
                            if b < BATCH:
                                turn(m, u, b)
                            if b > 0:
                                project(m - 1, u, b - 1)

            @block.gpsimd
            def _(pool):
                nc.gpsimd.memset(k.acc[:, :, :], 0.0).then_inc(S("cleared"), 1)
                pool.wait_ge(S("zpad"), 1)
                pool.dma_start(k.edst[N:PADN, :], zpad[:, :]).then_inc(S("pad"), 16)
                pool.wait_ge(S("pad"), 16)

            @block.scalar
            def _(act):
                for u in range(2):
                    act.sem_inc(S(f"stored{u}"), 32)
                with act.Fori(0, NBATCH // 2) as i:
                    for u in range(2):
                        root_step(k, t, act, mv[:, u, :, :], i * 2 + (1 + u))
                        act.wait_ge(S(f"stored{u}"), i * 32 + 32)
                        for b in range(BATCH + 1):
                            m = i * (2 * BATCH) + (u * BATCH + b + 1)
                            if b < BATCH:
                                q = (u * BATCH + b) % 2
                                act.wait_ge(S("turned"), m)
                                nc.scalar.copy(xt[:, q, :, :], psT[q]).then_inc(S("xt"), 1)
                            if b > 0:
                                act.wait_ge(S("product"), m - 1)
                                nc.scalar.copy(tb[:, u, b - 1, :], psO[(u * BATCH + b - 1) % 2]).then_inc(S("row"), 1)
                                act.wait_ge(S("row"), m - 1)
                                act.sem_inc(S("row_read"), 1)


def edges(k, layer):
    nc, a, H = k.nc, k.a, HEADS[layer]
    t = f"e{layer}"
    R = H * CH
    DH = D // H
    W = D + H
    S = lambda name: k.sem(f"edge{layer}_{name}")
    heads_of = [[h for h in range(H) if h * DH // P == s] for s in range(KD)] + [list(range(H))]
    with k.phase():
        g = k.sb(t + "g", [P, RING, CH, W])
        idx = k.sb(t + "idx", [P, RING, CH], I32)
        relc = k.sb(t + "relc", [P, RING, CH])
        relrow = k.sb(t + "relrow", [P, RING, CH * P], BF16)
        pen = k.sb(t + "pen", [R, RING, P])
        penr = k.sb(t + "penr", [R, RING, P])
        edw = k.sb(t + "edw", [P, RING, CH, H])
        absd = k.sb(t + "absd", [P, CH * P], BF16)
        pt = k.sb(t + "pt", [P, CH * P])
        esrc = k.sb(t + "esrc", [P, R])
        ad = k.sb(t + "ad", [P, R])
        zz = k.sb(t + "zz", [P, 2, R])
        ll = k.sb(t + "ll", [P, 2, R])
        dd = k.sb(t + "dd", [P, R])
        wt = k.sb(t + "wt", [P, RING, R])
        wd = k.sb(t + "wd", [P, RING, R]) if layer == 0 else None
        scan1 = k.sb(t + "scan1", [R, P])
        scan2 = k.sb(t + "scan2", [R, P])
        scan3 = k.sb(t + "scan3", [R, P])
        scan4 = k.sb(t + "scan4", [R, P])
        FLAT = H * (CH + 1)
        cpen = k.sb(t + "cpen", [1, FLAT + 1])
        carry = k.sb(t + "carry", [1, FLAT])
        back = k.sb(t + "back", [1, FLAT])
        brought = k.sb(t + "brought", [1, R])
        later = k.sb(t + "later", [1, R])
        ce = k.sb(t + "ce", [1, 2, H])
        frow = k.sb(t + "frow", [1, H])
        mask = k.sb(t + "mask", [1, H * 3 * P])
        onehot = k.sb(t + "onehot", [P, NSLOT, P])
        msg = k.sb(t + "msg", [P, NSLOT, D])
        ps = k.ps
        psX, psR, psA, psF = ps[0:R, 4, 0:P], ps[:, 5, 0:R], ps[:, 6, 0:R], ps[:, 7, 0:3]
        psCol, psCol2 = ps[0:R, 4, 256:257], ps[0:R, 4, 258:259]
        psFwd, psBack = ps[0:1, 5, P:P + FLAT], ps[0:1, 5, 320:320 + FLAT]
        flat = lambda ap: ap.rearrange("o (h j) -> o h j", h=H)
        hj = lambda ap: ap.rearrange("p (h j) -> p h j", h=H)
        aggr = [ps[:, q, 0:3 * P].rearrange("p (s n) -> p s n", s=3) for q in range(NSLOT)]
        mk = mask[:, :].rearrange("o (h s p) -> o h s p", h=H, s=3)

        with nc.Block() as block:
            @block.gpsimd
            def _(pool):
                def gather(c, u, used=True):
                    if used:
                        pool.wait_ge(S("chunk_done"), c - (RING - 1))
                        pool.sem_inc(S("slot_taken"), 1)
                    nc.gpsimd.tensor_copy(idx[:, u, :], k.srcE[:, bass.ds(c * CH, CH)]).then_inc(S("idx"), 1)
                    pool.wait_ge(S("idx"), c + 1)
                    pool.sem_inc(S("idx_seen"), 1)
                    for j in range(CH):
                        nc.gpsimd.indirect_dma_start(
                            g[:, u, j, :], None, k.rows,
                            bass.IndirectOffsetOnAxis(ap=idx[:, u, j:j + 1].bitcast(U32), axis=0),
                        ).then_inc(S(f"gathered{u}"), 16)

                for c in range(RING):
                    gather(c, c, used=False)
                with pool.Fori(0, CHUNKS // RING - 1) as i:
                    for u in range(RING):
                        gather(i * RING + (RING + u), u)
                gather(CHUNKS - 1, 0)

            def gathered(eng, c, i, u):
                eng.wait_ge(S(f"gathered{u}"), i * (16 * CH) + 16 * CH)

            @block.sync
            def _(sp):
                sp.dma_start(mask[:, :], a[f"mask{layer}"]).then_inc(S("mask"), 16)

                def load(c, i, u, used=True):
                    _, at0 = nc.values_load_multi_w_load_instructions(
                        k.n0[0:1, bass.ds(c * CH, CH)], engines=[ENGINE.SP], min_val=0, max_val=N - 1,
                        skip_runtime_bounds_check_because="destinations are nodes, clamped at zero on the chip")
                    rows = nc.sync.snap(c * CH) if not isinstance(c, int) else c * CH
                    if used:
                        sp.wait_ge(S("weights"), c - (RING - 1))
                        sp.sem_inc(S("loads_free"), 1)
                    sem = S(f"loaded{u}")
                    sp.dma_start(relrow[:, u, :].rearrange("p (o n) -> p o n", o=1),
                                 k.reld[bass.ds(rows, CH), :].rearrange("(o t) e -> o (t e)", o=1).rearrange("(z o) n -> z o n", z=1).to_broadcast([P, 1, CH * P])).then_inc(sem, 16)
                    for h in range(H):
                        sp.dma_start(pen[h * CH:(h + 1) * CH, u, :], k.seg[bass.ds(rows, CH), :]).then_inc(sem, 16)
                        sp.dma_start(penr[h * CH:(h + 1) * CH, u, :], k.segr[bass.ds(rows, CH), :]).then_inc(sem, 16)
                    for j in range(CH):
                        sp.dma_start(edw[:, u, j, :], k.edst[bass.ds(at0[j], P), :]).then_inc(sem, 16)

                for c in range(RING):
                    load(c, 0, c, used=False)
                with sp.Fori(0, CHUNKS // RING - 1) as i:
                    for u in range(RING):
                        load(i * RING + (RING + u), i, u)
                load(CHUNKS - 1, 0, 0)

            LOADS = 16 * (1 + 2 * H + CH)

            def loaded(eng, i, u):
                eng.wait_ge(S(f"loaded{u}"), i * LOADS + LOADS)

            def act_scores(act, c, i, u):
                n = c + 1
                half = CH * P // 2

                def first():
                    gathered(act, c, i, u)
                    act.wait_ge(S("zz0"), n)
                    nc.scalar.copy(hj(esrc[:, :]), g[:, u, :, D:W].rearrange("p j h -> p h j")).then_inc(S("esrc"), 1)

                def small():
                    nc.scalar.copy(relc[:, u, :], k.relE[:, bass.ds(c * CH, CH)]).then_inc(S("relc"), 1)
                    nc.scalar.copy(flat(cpen[:, 0:FLAT])[:, :, 1:CH + 1],
                                   k.single_row[0:1, bass.ds(c * CH, CH)].rearrange("o (z j) -> o z j", z=1).to_broadcast([1, H, CH])).then_inc(S("cpen"), 1)

                def distance(x):
                    loaded(act, i, u)
                    nc.scalar.activation(absd[:, x * half:(x + 1) * half], relrow[:, u, x * half:(x + 1) * half], ACT.Abs,
                                         bias=k.negpart[:, :]).then_inc(S("absd"), 1)

                def onehot_t(x):
                    act.wait_ge(S("absd"), n * 2)
                    act.wait_ge(S("expanded"), n)
                    nc.scalar.activation(pt[:, x * half:(x + 1) * half], absd[:, x * half:(x + 1) * half], ACT.Relu,
                                         bias=k.ones[:, :], scale=-1.0).then_inc(S("pt"), 1)

                def expand():
                    act.wait_ge(S("expanded"), n + 1)
                    act.wait_ge(S("ce"), n * CE - (CE - 1))
                    nc.scalar.copy(hj(ad[:, :]), psA.rearrange("p (j h) -> p h j", h=H)).then_inc(S("ad"), 1)

                def exps():
                    act.wait_ge(S("diff"), n + 1)
                    nc.scalar.activation(wt[:, u, :], dd[:, :], ACT.Exp).then_inc(S("exp"), 1)

                def factor():
                    act.wait_ge(S("ce"), n * CE + 1)
                    nc.scalar.activation(frow[:, :], ce[:, 1, :], ACT.Exp).then_inc(S("frow"), 1)

                return {"first": first, "small": small, "abs0": lambda: distance(0), "abs1": lambda: distance(1),
                        "pt0": lambda: onehot_t(0), "pt1": lambda: onehot_t(1), "expand": expand, "exps": exps, "factor": factor}

            def pe_scores(pe, c, i, u):
                n = c + 1

                def hold(name, value=None):
                    pe.wait_ge(S(name), n if value is None else value)
                    pe.sem_inc(S("pause"), 1)

                def turn():
                    hold("esrc")
                    nc.tensor.transpose(psX, esrc[:, :], k.ident[:, :]).then_inc(S("esrc_t"), 1)

                def last_row():
                    hold("scan1")
                    nc.tensor.transpose(flat(psFwd)[:, :, 1:CH + 1], scan1[:, P - 1:P], k.ident[0:R, 0:R]).then_inc(S("last_ps"), 1)

                def column():
                    hold("brought")
                    nc.tensor.matmul(psCol, brought[:, :], k.ones[0:1, :], start=True, stop=True).then_inc(S("col"), 1)

                def expand():
                    pe.wait_ge(S("pt"), n * 2)
                    for j in range(CH):
                        last = nc.tensor.matmul(psA[:, j * H:(j + 1) * H], pt[:, j * P:(j + 1) * P], edw[:, u, j, :],
                                                start=True, stop=True)
                    last.then_inc(S("expanded"), 1)

                def first_row():
                    hold("scan3")
                    nc.tensor.transpose(flat(psBack)[:, :, 0:CH], scan3[:, 0:1], k.ident[0:R, 0:R]).then_inc(S("first_ps"), 1)

                def column2():
                    hold("later")
                    nc.tensor.matmul(psCol2, later[:, :], k.ones[0:1, :], start=True, stop=True).then_inc(S("col2"), 1)

                def running():
                    hold("scan4")
                    nc.tensor.transpose(psR, scan4[:, :], k.ident[0:R, 0:R]).then_inc(S("max_ps"), 1)

                def factor():
                    pe.wait_ge(S("frow"), n + 1)
                    for s in range(3):
                        for h in heads_of[s]:
                            last = nc.tensor.matmul(psF[:, s:s + 1], mk[:, h, s, :], frow[:, h:h + 1],
                                                    start=(h == heads_of[s][0]), stop=(h == heads_of[s][-1]))
                    last.then_inc(S("fac_ps"), 1)

                return {"turn": turn, "last_row": last_row, "column": column, "expand": expand, "first_row": first_row,
                        "column2": column2, "running": running, "factor": factor}

            CE = 5

            def dve_scores(dve, c, i, u):
                n = c + 1
                scan = nc.vector.tensor_tensor_scan

                def scan_1():
                    loaded(dve, i, u)
                    dve.wait_ge(S("esrc_t"), n)
                    scan(scan1[:, :], pen[:, u, :], psX, -BIG, ALU.add, ALU.max).then_inc(S("scan1"), 1)

                def carries():
                    dve.wait_ge(S("last_ps"), n)
                    dve.wait_ge(S("cpen"), n)
                    dve.wait_ge(S("carried"), n)
                    scan(carry[:, :], cpen[:, 0:FLAT], psFwd, -BIG, ALU.add, ALU.max).then_inc(S("carry"), 1)

                def bring():
                    dve.wait_ge(S("carry"), n)
                    nc.vector.tensor_copy(hj(brought[:, :]), flat(carry[:, :])[:, :, 0:CH]).then_inc(S("brought"), 1)

                def carry_on():
                    nc.vector.tensor_copy(flat(psFwd)[:, :, 0:1], flat(carry[:, :])[:, :, CH:CH + 1]).then_inc(S("carried"), 1)

                def scan_2():
                    dve.wait_ge(S("col"), n)
                    scan(scan2[:, :], pen[:, u, :], psX, psCol, ALU.add, ALU.max).then_inc(S("scan2"), 1)

                def scan_3():
                    dve.wait_ge(S("scan2"), n)
                    scan(scan3[:, ::-1], penr[:, u, ::-1], scan2[:, ::-1], -BIG, ALU.add, ALU.max).then_inc(S("scan3"), 1)

                def backward():
                    dve.wait_ge(S("first_ps"), n)
                    scan(back[:, ::-1], cpen[:, FLAT:0:-1], psBack[:, ::-1], -BIG, ALU.add, ALU.max).then_inc(S("back"), 1)

                def meet():
                    dve.wait_ge(S("back"), n)
                    nc.vector.tensor_copy(hj(later[:, :]), flat(back[:, :])[:, :, 1:CH + 1]).then_inc(S("later"), 1)

                def scan_4():
                    dve.wait_ge(S("col2"), n)
                    scan(scan4[:, ::-1], penr[:, u, ::-1], scan2[:, ::-1], psCol2, ALU.add, ALU.max).then_inc(S("scan4"), 1)

                def sum_0():
                    dve.wait_ge(S("ad"), n)
                    nc.vector.tensor_tensor(zz[:, 0, :], esrc[:, :], ad[:, :], ALU.add).then_inc(S("zz0"), 1)

                def leaky_0():
                    dve.wait_ge(S("zz0"), n + 1)
                    nc.vector.scalar_tensor_tensor(ll[:, 0, :], zz[:, 0, :], SLOPE, zz[:, 0, :], ALU.mult, ALU.max).then_inc(S("ll0"), 1)

                def sum_1():
                    dve.wait_ge(S("max_ps"), n)
                    nc.vector.tensor_tensor(zz[:, 1, :], psR, ad[:, :], ALU.add).then_inc(S("zz1"), 1)

                def leaky_1():
                    dve.wait_ge(S("zz1"), n)
                    nc.vector.scalar_tensor_tensor(ll[:, 1, :], zz[:, 1, :], SLOPE, zz[:, 1, :], ALU.mult, ALU.max).then_inc(S("ll1"), 1)

                def diff():
                    dve.wait_ge(S("ll0"), n)
                    dve.wait_ge(S("ll1"), n)
                    dve.wait_ge(S("exp"), n)
                    nc.vector.tensor_tensor(dd[:, :], ll[:, 0, :], ll[:, 1, :], ALU.subtract).then_inc(S("diff"), 1)

                def weights():
                    dve.wait_ge(S("exp"), n + 1)
                    if layer == 0:
                        dist = k.distE[:, bass.ds(c * CH, CH)].rearrange("p (z j) -> p z j", z=1).to_broadcast([P, H, CH])
                        nc.vector.tensor_tensor(hj(wd[:, u, :]), hj(wt[:, u, :]), dist, ALU.mult).then_inc(S("weights"), 1)
                    else:
                        dve.sem_inc(S("weights"), 1)

                def ce_step(m, ins):
                    ins.then_inc(S("ce"), 1)

                def ce_1():
                    dve.wait_ge(S("brought"), n)
                    dve.wait_ge(S("frow"), n)
                    first = k.first_row[0:1, bass.ds(c * CH, 1)].to_broadcast([1, H])
                    ce_step(1, nc.vector.tensor_tensor(ce[:, 0, :], hj(brought[:, :])[:, :, 0], first, ALU.add))

                def ce_2():
                    dve.wait_ge(S("ce"), n * CE - (CE - 2))
                    ce_step(2, nc.vector.tensor_tensor(ce[:, 1, :], ce[:, 0, :], hj(ad[0:1, :])[:, :, 0], ALU.add))

                def ce_3():
                    dve.wait_ge(S("ce"), n * CE - (CE - 3))
                    ce_step(3, nc.vector.scalar_tensor_tensor(ce[:, 0, :], ce[:, 1, :], SLOPE, ce[:, 1, :], ALU.mult, ALU.max))

                def ce_4():
                    dve.wait_ge(S("ce"), n * CE - (CE - 4))
                    ce_step(4, nc.vector.tensor_tensor(ce[:, 0, :], ce[:, 0, :], hj(ll[0:1, 1, :])[:, :, 0], ALU.subtract))

                def ce_5():
                    dve.wait_ge(S("ce"), n * CE - (CE - 5))
                    ce_step(5, nc.vector.tensor_scalar(ce[:, 1, :], ce[:, 0, :], -200.0, None, ALU.max))

                return dict(scan_1=scan_1, carries=carries, bring=bring, carry_on=carry_on, scan_2=scan_2, scan_3=scan_3,
                            backward=backward, meet=meet, scan_4=scan_4, sum_0=sum_0, leaky_0=leaky_0, sum_1=sum_1,
                            leaky_1=leaky_1, diff=diff, weights=weights, ce_1=ce_1, ce_2=ce_2, ce_3=ce_3, ce_4=ce_4, ce_5=ce_5)

            BY_ACT = ACT_TILES[layer]
            BY_DVE = [j for j in range(CH) if j not in BY_ACT]

            def weight(u, j):
                return hj((wd if layer == 0 else wt)[:, u, :])[:, :, j:j + 1]

            def onehot_of(dve, c, u, j):
                dve.wait_ge(S("summed"), c * CH + (j + 1))
                nc.vector.tensor_scalar(onehot[:, j % NSLOT, :], k.iota[:, :], relc[:, u, j:j + 1], None, ALU.is_equal).then_inc(S("onehot"), 1)

            def message_of(dve, c, u, j):
                nc.vector.tensor_tensor(msg[:, j % NSLOT, :].rearrange("p (h d) -> p h d", h=H), g[:, u, j, 0:D].rearrange("p (h d) -> p h d", h=H),
                                        weight(u, j).to_broadcast([P, H, DH]), ALU.mult).then_inc(S("msg_dve"), 1)

            def dve_tile(dve, c, i, u, j, at0):
                n = c * CH + (j + 1)
                if j == 0:
                    for j2 in range(AHEAD):
                        onehot_of(dve, c, u, j2)
                        if j2 in BY_DVE:
                            message_of(dve, c, u, j2)
                window = k.acc[:, :, bass.ds(at0[j], P)]
                if j == 0:
                    dve.wait_ge(S("fac_ps"), c + 1)
                    first = k.acc[:, :, bass.ds(at0[0], 1)]
                    nc.vector.tensor_tensor(first, first, psF.rearrange("p (s o) -> p s o", o=1), ALU.mult).then_inc(S("rescaled"), 1)
                    dve.wait_ge(S("rescaled"), c + 1)
                dve.wait_ge(S("summed"), n + NSLOT)
                dve.wait_ge(S("added"), n + (NSLOT - 1))
                nc.vector.tensor_tensor(window, window, aggr[j % NSLOT], ALU.add).then_inc(S("added"), 1)
                if j + AHEAD < CH:
                    onehot_of(dve, c, u, j + AHEAD)
                    if j + AHEAD in BY_DVE:
                        message_of(dve, c, u, j + AHEAD)

            def act_tile(act, c, i, u, j):
                if j == BY_ACT[0]:
                    act.wait_ge(S("weights"), c + 1)
                    gathered(act, c, i, u)
                act.wait_ge(S("summed"), c * CH + (j + 1))
                for h in range(H):
                    last = nc.scalar.activation(msg[:, j % NSLOT, h * DH:(h + 1) * DH], g[:, u, j, h * DH:(h + 1) * DH], ACT.Copy,
                                                scale=weight(u, j)[:, h, :])
                last.then_inc(S("msg_act"), 1)

            def pe_tile(pe, c, i, u, j):
                n = c * CH + (j + 1)
                q = j % NSLOT
                pe.wait_ge(S("added"), n)
                pe.wait_ge(S("onehot"), n)
                mine = BY_ACT if j in BY_ACT else BY_DVE
                pe.wait_ge(S("msg_act" if j in BY_ACT else "msg_dve"), c * len(mine) + (mine.index(j) + 1))
                for s in range(KD):
                    nc.tensor.matmul(aggr[q][:, s, :], msg[:, q, s * P:(s + 1) * P], onehot[:, q, :], start=True, stop=True)
                nc.tensor.matmul(aggr[q][0:H, KD, :], hj(wt[:, u, :])[:, :, j], onehot[:, q, :], start=True, stop=True).then_inc(S("summed"), 1)

            SCORE_AT = SCHEDULE

            def scores_after(engine, steps, j):
                for name in SCORE_AT[engine].get(j, []):
                    steps[name]()

            def all_scores(engine, steps):
                for j in range(-1, CH):
                    scores_after(engine, steps, j)

            @block.vector
            def _(dve):
                for q in range(NSLOT):
                    nc.vector.memset(ps[:, q, :], 0.0).then_inc(S("added"), 1)
                nc.vector.memset(cpen[:, :], -BIG).then_inc(S("carry_init"), 1)
                nc.vector.memset(psFwd, -BIG).then_inc(S("carry_init"), 1)
                nc.vector.memset(psBack, -BIG).then_inc(S("carry_init"), 1)
                dve.wait_ge(S("carry_init"), 3)
                for name in ("diff", "zz0", "carried", "ce"):
                    dve.sem_inc(S(name), 1)
                all_scores("dve", dve_scores(dve, 0, 0, 0))

                def turn(c, i, u, following=None):
                    _, at0 = nc.values_load_multi_w_load_instructions(
                        k.n0[0:1, bass.ds(c * CH, CH)], engines=[ENGINE.DVE], min_val=0, max_val=N - 1,
                        skip_runtime_bounds_check_because="destinations are nodes, clamped at zero on the chip")
                    dve.wait_ge(S("relc"), c + 1)
                    dve.wait_ge(S("weights"), c + 1)
                    gathered(dve, c, i, u)
                    steps = dve_scores(dve, *following) if following else {}
                    for j in range(CH):
                        dve_tile(dve, c, i, u, j, at0)
                        if following:
                            scores_after("dve", steps, j)
                    dve.wait_ge(S("added"), c * CH + (CH + NSLOT))
                    dve.sem_inc(S("chunk_done"), 1)

                with dve.Fori(0, CHUNKS // RING) as i:
                    for u in range(RING):
                        c = i * RING + u
                        u1 = (u + 1) % RING
                        turn(c, i, u, (i * RING + (u + 1), i + 1 if u1 == 0 else i, u1))
                turn(CHUNKS - 1, CHUNKS // RING, 0)

            @block.tensor
            def _(pe):
                pe.sem_inc(S("summed"), NSLOT)
                pe.sem_inc(S("expanded"), 1)
                pe.wait_ge(S("mask"), 16)
                pe.wait_ge(S("carry_init"), 3)
                all_scores("pe", pe_scores(pe, 0, 0, 0))

                def turn(c, i, u, following=None):
                    steps = pe_scores(pe, *following) if following else {}
                    for j in range(CH):
                        pe_tile(pe, c, i, u, j)
                        if following:
                            scores_after("pe", steps, j)

                with pe.Fori(0, CHUNKS // RING) as i:
                    for u in range(RING):
                        u1 = (u + 1) % RING
                        turn(i * RING + u, i, u, (i * RING + (u + 1), i + 1 if u1 == 0 else i, u1))
                turn(CHUNKS - 1, CHUNKS // RING, 0)

            @block.scalar
            def _(act):
                act.sem_inc(S("exp"), 1)
                act.sem_inc(S("frow"), 1)
                act.wait_ge(S("carry_init"), 3)
                all_scores("act", act_scores(act, 0, 0, 0))

                def turn(c, i, u, following=None):
                    steps = act_scores(act, *following) if following else {}
                    for j in range(CH):
                        if j in BY_ACT:
                            act_tile(act, c, i, u, j)
                        if following:
                            scores_after("act", steps, j)

                with act.Fori(0, CHUNKS // RING) as i:
                    for u in range(RING):
                        u1 = (u + 1) % RING
                        turn(i * RING + u, i, u, (i * RING + (u + 1), i + 1 if u1 == 0 else i, u1))
                turn(CHUNKS - 1, CHUNKS // RING, 0)


def nodes(k, layer, xin, xout):
    nc, a, H = k.nc, k.a, HEADS[layer]
    t = f"n{layer}"
    S = lambda name: k.sem(f"{t}_{name}")
    with k.phase():
        xb = k.sb(t + "x", [TB, 2, BATCH, D])
        rden = k.sb(t + "rden", [H, 2, ROWS])
        spread = k.sb(t + "spread", [H, KD, P])
        onT = k.sb(t + "onT", [P, 2, KD, TB])
        x1 = k.sb(t + "x1", [TB, 2, BATCH, D])
        y = k.sb(t + "y", [TB, 2, BATCH, D])
        yt = k.sb(t + "yt", [P, 2, KD, ROWS])
        st = k.sb(t + "st", [TB, 2, BATCH, 6])
        mv = k.sb(t + "mv", [TB, 2, BATCH, 2])
        if layer == 0:
            st2 = k.sb(t + "st2", [TB, 2, BATCH, 6])
            mv2 = k.sb(t + "mv2", [TB, 2, BATCH, 2])
            gamma = k.sb(t + "gamma", [P, KD])
            beta = k.sb(t + "beta", [P, KD])
            wr = k.sb(t + "wr", [P, KD, E])
            zero = k.sb(t + "zero", [P, 1, D])
            ZEROS = 8
        else:
            neg = k.sb(t + "neg", [TB, 2, D])
            ex = k.sb(t + "ex", [TB, 2, D])
        ps = k.ps
        psB = [ps[:, q, 0:KD * TB].rearrange("p (h n) -> p h n", h=KD) for q in range(2)]
        psX = [ps[0:TB, 2 + q, 0:D] for q in range(2)]
        psY = [ps[:, 4 + q, 0:KD * TB].rearrange("p (h n) -> p h n", h=KD) for q in range(2)]
        psL = [ps[0:TB, 6 + u, 0:BATCH * E].rearrange("p (b e) -> p b e", b=BATCH) for u in range(2)]
        consts = [(spread[:, :, :], a[f"spread{layer}"])]
        if layer == 0:
            consts += [(gamma[:, :], a["L0_ffn_gamma"].rearrange("o (h p) -> p (o h)", p=P)),
                       (beta[:, :], a["L0_ffn_beta"].rearrange("o (h p) -> p (o h)", p=P)),
                       (wr[:, :, :], a["L0_ffn_Wr"].rearrange("(h p) e -> p h e", p=P))]
        ready = 16 * len(consts)
        place = lambda u, b: (u * BATCH + b) % 2
        block_number = lambda i, u, b: i * (2 * BATCH) + (u * BATCH + b + 1)
        with nc.Block() as block:
            @block.sync
            def _(sp):
                with nc.allow_non_contiguous_dma("256 words of each, once"):
                    for dst, src in consts:
                        sp.dma_start(dst, src).then_inc(S("consts"), 16)

                def load(row, u):
                    sp.dma_start(xb[:, u, :, :], rows_of(xin, row)).then_inc(S(f"x{u}"), 16)

                def store(row, n, u):
                    sp.wait_ge(S("sum"), n * BATCH)
                    sp.dma_start(rows_of(xout, row), x1[:, u, :, :]).then_inc(S(f"xs{u}"), 16)
                    sp.wait_ge(S("y"), n * BATCH)
                    sp.dma_start(rows_of(k.y3, row), y[:, u, :, :]).then_inc(S(f"xs{u}"), 16)

                for u in range(2):
                    load(u * ROWS, u)
                with sp.Fori(0, NBATCH // 2 - 1) as i:
                    for u in range(2):
                        store(i * (2 * ROWS) + u * ROWS, i * 2 + (1 + u), u)
                        load(i * (2 * ROWS) + (2 + u) * ROWS, u)
                for u in range(2):
                    store((NBATCH - 2 + u) * ROWS, NBATCH - 1 + u, u)
                for u in range(2):
                    sp.wait_ge(S(f"xs{u}"), 32 * (1 + NBATCH // 2))

            @block.scalar
            def _(act):
                act.wait_ge(S("consts"), ready)
                with act.Fori(0, NBATCH // 2) as i:
                    for u in range(2):
                        n = i * 2 + (1 + u)
                        if layer == 1:
                            for b in range(BATCH):
                                act.wait_ge(S("neg"), block_number(i, u, b))
                                nc.scalar.activation(ex[:, place(u, b), :], neg[:, place(u, b), :], ACT.Exp).then_inc(S("ex"), 1)
                        root_step(k, t, act, mv[:, u, :, :], n)
                        if layer == 0:
                            root_step(k, t + "b", act, mv2[:, u, :, :], n)
                        if layer == 1:
                            act.wait_ge(S("placed"), n)
                        for b in range(BATCH):
                            act.wait_ge(S("yt_ps"), block_number(i, u, b))
                            for h in range(KD):
                                dst, src = yt[:, u, h, b * TB:(b + 1) * TB], psY[place(u, b)][:, h, :]
                                if layer == 0:
                                    last = nc.scalar.activation(dst, src, ACT.Identity, bias=beta[:, h:h + 1], scale=gamma[:, h:h + 1])
                                else:
                                    last = nc.scalar.copy(dst, src)
                            last.then_inc(S("yt"), 1)
                        if layer == 0:
                            act.wait_ge(S("logit_ps"), n)
                            nc.scalar.copy(k.logits[:, bass.ds((i * 2 + u) * BATCH, BATCH), :], psL[u]).then_inc(S("logit"), 1)

            @block.gpsimd
            def _(pool):
                if layer == 0:
                    nc.gpsimd.memset(zero[:, :, :], 0.0).then_inc(S("zero"), 1)
                    pool.wait_ge(S("zero"), 1)
                    for z in range(ZEROS):
                        pool.dma_start(k.xs[z * (NT * ROWS_OF_TILE // ZEROS):(z + 1) * (NT * ROWS_OF_TILE // ZEROS), :].rearrange("(s p) d -> p s d", p=P),
                                       zero[:, :, :].to_broadcast([P, NT * ROWS_OF_TILE // ZEROS // P, D])).then_inc(S("filled"), 16)
                    pool.wait_ge(S("filled"), 16 * ZEROS)
                    return
                pool.sem_inc(S("placed"), 2)
                nc.gpsimd.memset(k.ysum[:, :], 0.0).then_inc(S("ysum"), 1)
                with pool.Fori(0, NBATCH // 2) as i:
                    for u in range(2):
                        n, row = i * 2 + (1 + u), i * (2 * ROWS) + u * ROWS
                        for b in range(BATCH):
                            pool.wait_ge(S("y"), block_number(i, u, b))
                            pool.wait_ge(S("ysum"), block_number(i, u, b))
                            nc.gpsimd.tensor_tensor(k.ysum[:, :], k.ysum[:, :], y[:, u, b, :], ALU.add).then_inc(S("ysum"), 1)
                        pool.wait_ge(S("yt"), n * BATCH)
                        pool.sem_inc(S("yt_seen"), 1)
                        nc.gpsimd.tensor_copy(k.acc[:, 0:KD, bass.ds(row, ROWS)], yt[:, u, :, :]).then_inc(S("placed"), 1)

            @block.tensor
            def _(pe):
                pe.wait_ge(S("consts"), ready)

                def divide(i, u, b):
                    for h in range(KD):
                        last = nc.tensor.matmul(psB[place(u, b)][:, h, :], spread[:, h, :], rden[:, u, b * TB:(b + 1) * TB], start=True, stop=True)
                    last.then_inc(S("spread"), 1)

                def message(i, u, b):
                    pe.wait_ge(S("onT"), block_number(i, u, b))
                    pe.sem_inc(S("pause"), 1)
                    for h in range(KD):
                        last = nc.tensor.transpose(psX[place(u, b)][:, h * P:(h + 1) * P], onT[:, place(u, b), h, :], k.ident[:, :])
                    last.then_inc(S("msg"), 1)

                with pe.Fori(0, NBATCH // 2) as i:
                    for u in range(2):
                        pe.wait_ge(S("rden"), i * 2 + (1 + u))
                        divide(i, u, 0)
                        divide(i, u, 1)
                        for b in range(BATCH):
                            message(i, u, b)
                            if b + 2 < BATCH:
                                divide(i, u, b + 2)
                        for b in range(BATCH):
                            pe.wait_ge(S("y"), block_number(i, u, b))
                            if b >= 2:
                                pe.wait_ge(S("yt"), block_number(i, u, b - 2))
                            pe.sem_inc(S("pause"), 1)
                            for h in range(KD):
                                last = nc.tensor.transpose(psY[place(u, b)][:, h, :], y[:, u, b, h * P:(h + 1) * P], k.ident[0:TB, 0:TB])
                            last.then_inc(S("yt_ps"), 1)
                        pe.wait_ge(S("yt"), (i * 2 + (1 + u)) * BATCH)
                        if layer == 0:
                            for b in range(BATCH):
                                for h in range(KD):
                                    last = nc.tensor.matmul(psL[u][:, b, :], yt[:, u, h, b * TB:(b + 1) * TB], wr[:, h, :], start=(h == 0), stop=(h == KD - 1))
                            last.then_inc(S("logit_ps"), 1)

            @block.vector
            def _(dve):
                dve.wait_ge(S("consts"), ready)
                for u in range(2):
                    dve.sem_inc(S(f"xs{u}"), 32)

                def divide(i, u, b):
                    row = i * (2 * ROWS) + (u * BATCH + b) * TB
                    dve.wait_ge(S("spread"), block_number(i, u, b))
                    nc.vector.tensor_tensor(onT[:, place(u, b), :, :], k.acc[:, 0:KD, bass.ds(row, TB)], psB[place(u, b)], ALU.mult).then_inc(S("onT"), 1)

                def add(i, u, b):
                    q, m = place(u, b), block_number(i, u, b)
                    dve.wait_ge(S("msg"), m)
                    if layer == 0:
                        nc.vector.tensor_tensor(x1[:, u, b, :], xb[:, u, b, :], psX[q], ALU.add).then_inc(S("sum"), 1)
                    else:
                        nc.vector.tensor_scalar(neg[:, q, :], psX[q], 0.0, None, ALU.min).then_inc(S("neg"), 1)
                        nc.vector.scalar_tensor_tensor(x1[:, u, b, :], psX[q], 0.0, xb[:, u, b, :], ALU.max, ALU.add).then_inc(S("pos"), 1)

                def add_exp(i, u, b):
                    q, m = place(u, b), block_number(i, u, b)
                    dve.wait_ge(S("pos"), m)
                    dve.wait_ge(S("ex"), m)
                    nc.vector.scalar_tensor_tensor(x1[:, u, b, :], ex[:, q, :], -1.0, x1[:, u, b, :], ALU.add, ALU.add).then_inc(S("sum"), 1)

                with dve.Fori(0, NBATCH // 2) as i:
                    for u in range(2):
                        n, row = i * 2 + (1 + u), i * (2 * ROWS) + u * ROWS
                        nc.vector.reciprocal(rden[:, u, :], k.acc[0:H, KD, bass.ds(row, ROWS)]).then_inc(S("rden"), 1)
                        divide(i, u, 0)
                        divide(i, u, 1)
                        dve.wait_ge(S(f"x{u}"), i * 16 + 16)
                        dve.wait_ge(S(f"xs{u}"), i * 32 + 32)
                        for b in range(BATCH):
                            add(i, u, b)
                            if b + 2 < BATCH:
                                divide(i, u, b + 2)
                            if layer == 1 and b > 0:
                                add_exp(i, u, b - 1)
                        if layer == 1:
                            add_exp(i, u, BATCH - 1)
                        dve.wait_ge(S("sum"), n * BATCH)
                        if layer == 0:
                            norm_steps(k, t, dve, x1[:, u, :, :], st[:, u, :, :], mv[:, u, :, :], y[:, u, :, :], n).then_inc(S("y1"), 1)
                            dve.wait_ge(S("y1"), n)
                            norm_steps(k, t + "b", dve, y[:, u, :, :], st2[:, u, :, :], mv2[:, u, :, :], y[:, u, :, :], n, S("y"))
                        else:
                            dve.wait_ge(S("placed"), n)
                            norm_steps(k, t, dve, x1[:, u, :, :], st[:, u, :, :], mv[:, u, :, :], y[:, u, :, :], n, S("y"))


def ffn0(k):
    with k.phase():
        k.slots = k.sb("f0slots", [TB, NB, 2], I32)
        k.share = k.sb("f0share", [TB, NB, 2])
        k.expert = k.sb("f0expert", [1, NT], I32)
        with k.phase():
            k.w1 = k.sb("f0w1", [P, E, KD, HID])
            k.w2 = k.sb("f0w2", [P, E, KH, D])
            with k.phase():
                k.stage(route)
            with k.phase():
                k.stage(scatter)
            with k.phase():
                k.stage(experts)
        with k.phase():
            k.stage(combine)


def route(k):
    nc, a = k.nc, k.a
    S = lambda name: k.sem(f"rt_{name}")
    iota8 = k.sb("rt_iota8", [TB, E])
    br = k.sb("rt_br", [TB, 1, E])
    before = k.sb("rt_before", [TB, TB])
    all_ones = k.sb("rt_ones", [TB, TB])
    top = k.sb("rt_top", [TB, NB, E])
    topi = k.sb("rt_topi", [TB, NB, E], U32)
    idxf = k.sb("rt_idxf", [TB, NB, 2])
    gap = k.sb("rt_gap", [TB, NB, 1])
    e2 = k.sb("rt_e2", [TB, NB, 1])
    den = k.sb("rt_den", [TB, NB, 1])
    hit = k.sb("rt_hit", [TB, 2, NB, E])
    both = k.sb("rt_both", [TB, NB, E])
    go_on = k.sb("rt_go_on", [TB, E, NB])
    upto = k.sb("rt_upto", [TB, E, NB])
    slot = k.sb("rt_slot", [TB, E, NB])
    start = k.sb("rt_start", [TB, MOST])
    begun = k.sb("rt_begun", [TB, E, MOST])
    tiles = k.sb("rt_tiles", [TB, E])
    tiles_upto = k.sb("rt_tiles_upto", [TB, E])
    origin = k.sb("rt_origin", [TB, E, 1])
    past = k.sb("rt_past", [1, NT, E - 1])
    expertf = k.sb("rt_expertf", [1, NT])
    picked = k.sb("rt_picked", [TB, NB, E])
    slotf = k.sb("rt_slotf", [TB, NB, 2])
    psBefore = k.ps[0:TB, 0, 0:E * NB].rearrange("p (e b) -> p e b", e=E)
    psAll = k.ps[0:TB, 1, 0:E * NB].rearrange("p (e b) -> p e b", e=E)
    with nc.Block() as block:
        @block.sync
        def _(sp):
            sp.dma_start(iota8[:, :], a["iota"][0:TB, 0:E]).then_inc(S("small"), 16)
            sp.dma_start(br[:, 0, :], a["L0_ffn_br"].to_broadcast([TB, E])).then_inc(S("small"), 16)
            sp.dma_start(before[:, :], a["before"]).then_inc(S("small"), 16)
            for e in range(E):
                sp.dma_start(k.w1[:, e, :, :], a["L0_ffn_W1"][e].rearrange("(h p) n -> p h n", p=P)).then_inc(S("w"), 16)
                sp.dma_start(k.w2[:, e, :, :], a["L0_ffn_W2"][e].rearrange("(c p) n -> p c n", p=P)).then_inc(S("w"), 16)
            sp.wait_ge(S("w"), 32 * E)

        @block.tensor
        def _(pe):
            pe.wait_ge(S("small"), 48)
            pe.wait_ge(S("both"), 1)
            columns = both[:, :, :].rearrange("p b e -> p e b")
            nc.tensor.matmul(psBefore, before[:, :], columns, start=True, stop=True).then_inc(S("counted"), 1)
            nc.tensor.matmul(psAll, all_ones[:, :], columns, start=True, stop=True).then_inc(S("counted"), 1)

        @block.scalar
        def _(act):
            act.wait_ge(S("gap"), 1)
            nc.scalar.activation(e2[:, :, :], gap[:, :, :], ACT.Exp).then_inc(S("e2"), 1)

        @block.vector
        def _(dve):
            chain = [0]

            def link(ins):
                chain[0] += 1
                ins.then_inc(S("step"), 1)
                dve.wait_ge(S("step"), chain[0])

            nc.vector.memset(all_ones[:, :], 1.0)
            link(nc.vector.memset(go_on[:, :, :], 1.0))
            dve.wait_ge(S("small"), 48)
            link(nc.vector.memset(go_on[:, :, 0:1], 0.0))
            link(nc.vector.tensor_tensor(k.logits[:, :, :], k.logits[:, :, :], br[:, :, :].to_broadcast([TB, NB, E]), ALU.add))
            for b in range(NB):
                last = nc.vector.max(top[:, b, :], k.logits[:, b, :])
            link(last)
            for b in range(NB):
                last = nc.vector.max_index(topi[:, b, :], top[:, b, :], k.logits[:, b, :])
            link(last)
            nc.vector.tensor_tensor(gap[:, :, :], top[:, :, 1:2], top[:, :, 0:1], ALU.subtract).then_inc(S("gap"), 1)
            link(nc.vector.tensor_copy(idxf[:, :, :], topi[:, :, 0:2]))
            each = iota8[:, :].rearrange("p (z e) -> p z e", z=1).to_broadcast([TB, NB, E])
            for j in range(2):
                link(nc.vector.tensor_tensor(hit[:, j, :, :], each, idxf[:, :, j:j + 1].to_broadcast([TB, NB, E]), ALU.is_equal))
            nc.vector.tensor_tensor(both[:, :, :], hit[:, 0, :, :], hit[:, 1, :, :], ALU.add).then_inc(S("both"), 1)
            dve.wait_ge(S("e2"), 1)
            link(nc.vector.tensor_scalar(den[:, :, :], e2[:, :, :], 1.0, None, ALU.add))
            link(nc.vector.reciprocal(k.share[:, :, 0:1], den[:, :, :]))
            link(nc.vector.tensor_tensor(k.share[:, :, 1:2], k.share[:, :, 0:1], e2[:, :, :], ALU.mult))
            dve.wait_ge(S("counted"), 2)
            link(nc.vector.tensor_tensor_scan(upto[:, :, :].rearrange("p e b -> p (e b)"), go_on[:, :, :].rearrange("p e b -> p (e b)"),
                                              k.ps[0:TB, 1, 0:E * NB], 0.0, ALU.mult, ALU.add))
            link(nc.vector.tensor_scalar(start[:, :], k.iota[0:TB, 0:MOST], float(ROWS_OF_TILE), None, ALU.mult))
            link(nc.vector.tensor_tensor(begun[:, :, :], start[:, :].rearrange("p (z j) -> p z j", z=1).to_broadcast([TB, E, MOST]),
                                         upto[:, :, NB - 1:NB].to_broadcast([TB, E, MOST]), ALU.is_lt))
            link(nc.vector.tensor_reduce(tiles[:, :], begun[:, :, :], AX.X, ALU.add))
            link(nc.vector.tensor_tensor_scan(tiles_upto[:, :], go_on[:, 0, 1:1 + E], tiles[:, :], 0.0, ALU.mult, ALU.add))
            link(nc.vector.tensor_tensor(origin[:, :, 0], tiles_upto[:, :], tiles[:, :], ALU.subtract))
            link(nc.vector.tensor_scalar(origin[:, :, 0], origin[:, :, 0], float(ROWS_OF_TILE), None, ALU.mult))
            link(nc.vector.tensor_tensor(slot[:, :, :], upto[:, :, :], psAll, ALU.subtract))
            link(nc.vector.tensor_tensor(slot[:, :, :], slot[:, :, :], psBefore, ALU.add))
            link(nc.vector.tensor_tensor(slot[:, :, :], slot[:, :, :], origin[:, :, :].to_broadcast([TB, E, NB]), ALU.add))
            for j in range(2):
                link(nc.vector.tensor_tensor(picked[:, :, :], hit[:, j, :, :], slot[:, :, :].rearrange("p e b -> p b e"), ALU.mult))
                link(nc.vector.tensor_reduce(slotf[:, :, j], picked[:, :, :], AX.X, ALU.add))
            link(nc.vector.tensor_copy(k.slots[:, :, :], slotf[:, :, :]))
            link(nc.vector.tensor_tensor(past[:, :, :], tiles_upto[0:1, 0:E - 1].rearrange("o (z e) -> o z e", z=1).to_broadcast([1, NT, E - 1]),
                                         k.iota[0:1, 0:NT].rearrange("o (t z) -> o t z", z=1).to_broadcast([1, NT, E - 1]), ALU.is_le))
            link(nc.vector.tensor_reduce(expertf[:, :], past[:, :, :], AX.X, ALU.add))
            link(nc.vector.tensor_copy(k.expert[:, :], expertf[:, :]))


def scatter(k):
    nc = k.nc
    S = lambda name: k.sem(f"sc_{name}")
    yb = k.sb("sc_y", [TB, 2, BATCH, D])
    idx = k.sb("sc_idx", [TB, 2, BATCH, 2], I32)
    with nc.Block() as block:
        @block.sync
        def _(sp):
            def load(row, u):
                sp.dma_start(yb[:, u, :, :], rows_of(k.y3, row)).then_inc(S(f"y{u}"), 16)

            for u in range(2):
                load(u * ROWS, u)
            with sp.Fori(0, NBATCH // 2 - 1) as i:
                for u in range(2):
                    sp.wait_ge(S(f"sent{u}"), (i + 1) * (16 * BATCH * 2))
                    load(i * (2 * ROWS) + (2 + u) * ROWS, u)

        @block.gpsimd
        def _(pool):
            with pool.Fori(0, NBATCH // 2) as i:
                for u in range(2):
                    pool.wait_ge(S(f"y{u}"), i * 16 + 16)
                    pool.sem_inc(S("pause"), 1)
                    nc.gpsimd.tensor_copy(idx[:, u, :, :], k.slots[:, bass.ds((i * 2 + u) * BATCH, BATCH), :]).then_inc(S("idx"), 1)
                    pool.wait_ge(S("idx"), i * 2 + (1 + u))
                    pool.sem_inc(S("pause"), 1)
                    for b in range(BATCH):
                        for j in range(2):
                            nc.gpsimd.indirect_dma_start(
                                k.xs, bass.IndirectOffsetOnAxis(ap=idx[:, u, b, j:j + 1].bitcast(U32), axis=0),
                                yb[:, u, b, :], None).then_inc(S(f"sent{u}"), 16)
            for u in range(2):
                pool.wait_ge(S(f"sent{u}"), 16 * BATCH * 2 * (NBATCH // 2))


def experts(k):
    nc, a = k.nc, k.a
    S = lambda name: k.sem(f"ex_{name}")
    SUB = ROWS_OF_TILE // P
    b1 = k.sb("ex_b1", [P, E, KH])
    b2 = k.sb("ex_b2", [P, E, D])
    gamma = k.sb("ex_gamma", [P, KD])
    beta = k.sb("ex_beta", [P, KD])
    xs = k.sb("ex_xs", [P, 2, SUB, D])
    w1s = k.sb("ex_w1s", [P, 2, KD, HID])
    b1s = k.sb("ex_b1s", [P, 2, KH])
    xT = k.sb("ex_xT", [P, 2, KD, ROWS_OF_TILE])
    hT = k.sb("ex_hT", [P, 2, KH, ROWS_OF_TILE])
    out = k.sb("ex_out", [P, 2, SUB, D])
    ps = k.ps
    psX = [ps[:, q, 0:KD * ROWS_OF_TILE].rearrange("p (h n) -> p h n", h=KD) for q in range(2)]
    psH = [[ps[:, 2 + 2 * q + c // 2, (c % 2) * ROWS_OF_TILE:(c % 2 + 1) * ROWS_OF_TILE] for c in range(KH)] for q in range(2)]
    psY = [ps[:, 6 + q, 0:SUB * D].rearrange("p (s d) -> p s d", s=SUB) for q in range(2)]
    tile_rows = lambda ap, t: ap[bass.ds(t * ROWS_OF_TILE, ROWS_OF_TILE), :].rearrange("(s p) d -> p s d", p=P)

    def expert_of(engine, t, count):
        _, which = nc.values_load_multi_w_load_instructions(
            k.expert[0:1, bass.ds(t, count)], engines=[engine], min_val=0, max_val=E - 1,
            skip_runtime_bounds_check_because="a count of seven comparisons")
        return which

    with nc.Block() as block:
        @block.sync
        def _(sp):
            sp.dma_start(b1[:, :, :], a["L0_ffn_b1"].rearrange("e p c -> p e c")).then_inc(S("b1"), 16)
            with nc.allow_non_contiguous_dma("256 words of each, once"):
                sp.dma_start(gamma[:, :], a["L0_ffn_gamma"].rearrange("o (h p) -> p (o h)", p=P)).then_inc(S("norm"), 16)
                sp.dma_start(beta[:, :], a["L0_ffn_beta"].rearrange("o (h p) -> p (o h)", p=P)).then_inc(S("norm"), 16)

            def load(t, q):
                sp.dma_start(xs[:, q, :, :], tile_rows(k.xs, t)).then_inc(S(f"xs{q}"), 16)

            def store(t, q):
                sp.wait_ge(S("evicted"), t + 3)
                sp.dma_start(tile_rows(k.ys, t), out[:, q, :, :]).then_inc(S(f"stored{q}"), 16)

            def step(t, q):
                sp.wait_ge(S("turned"), t + 1)
                load(t + 2, q)
                store(t - 1, 1 - q)

            load(0, 0)
            load(1, 1)
            for e in range(E):
                sp.dma_start(b2[:, e, :], a["L0_ffn_b2"][e:e + 1, :].to_broadcast([P, D])).then_inc(S("b2"), 16)
            sp.wait_ge(S("turned"), 1)
            load(2, 0)
            with sp.Fori(0, NT // 2 - 2) as i:
                step(i * 2 + 1, 1)
                step(i * 2 + 2, 0)
            step(NT - 3, 1)
            for t in range(NT - 3, NT):
                store(t, t % 2)
            for q in range(2):
                sp.wait_ge(S(f"stored{q}"), 16 + 16 * (NT // 2))

        @block.gpsimd
        def _(pool):
            pool.wait_ge(S("b1"), 16)
            with pool.Fori(0, NT // 2) as i:
                which = expert_of(ENGINE.Pool, i * 2, 2)
                for q in range(2):
                    t = i * 2 + q
                    pool.wait_ge(S("gelu"), t + 1)
                    pool.wait_ge(S("up"), t * 2 + 2)
                    pool.sem_inc(S("pause"), 1)
                    nc.gpsimd.tensor_copy(b1s[:, q, :], b1[:, bass.ds(which[q], 1), :].rearrange("p o c -> p (o c)"))
                    nc.gpsimd.tensor_copy(w1s[:, q, :, :], k.w1[:, bass.ds(which[q], 1), :, :].rearrange("p o h n -> p (o h) n")).then_inc(S("w1s"), 1)

        @block.tensor
        def _(pe):
            pe.sem_inc(S("up"), 4)
            pe.sem_inc(S("down"), 2)

            def turn(i, q):
                pe.wait_ge(S(f"xs{q}"), i * 16 + 16)
                pe.sem_inc(S("pause"), 1)
                for s in range(SUB):
                    for h in range(KD):
                        last = nc.tensor.transpose(psX[q][:, h, s * P:(s + 1) * P], xs[:, q, s, h * P:(h + 1) * P], k.ident[:, :])
                last.then_inc(S("turned"), 1)

            def up(t, q):
                pe.wait_ge(S("xT"), t + 1)
                pe.wait_ge(S("w1s"), t + 1)
                for c in range(KH):
                    for h in range(KD):
                        last = nc.tensor.matmul(psH[q][c], w1s[:, q, h, c * P:(c + 1) * P], xT[:, q, h, :], start=(h == 0), stop=(h == KD - 1))
                    if c % 2:
                        last.then_inc(S("up"), 1)

            def down(t, q, e):
                pe.wait_ge(S("gelu"), t + 3)
                pe.wait_ge(S("evicted"), t + 1)
                for s in range(SUB):
                    for c in range(KH):
                        last = nc.tensor.matmul(psY[q][:, s, :], hT[:, q, c, s * P:(s + 1) * P],
                                                k.w2[:, bass.ds(e, 1), c, :].rearrange("p o n -> p (o n)"), start=(c == 0), stop=(c == KH - 1))
                last.then_inc(S("down"), 1)

            turn(0, 0)
            turn(0, 1)
            up(0, 0)
            with pe.Fori(0, NT // 2 - 1) as i:
                which = expert_of(ENGINE.PE, i * 2, 2)
                for q in range(2):
                    turn(i + 1, q)
                    up(i * 2 + (1 + q), 1 - q)
                    down(i * 2 + q, q, which[q])
            which = expert_of(ENGINE.PE, NT - 2, 2)
            up(NT - 1, 1)
            down(NT - 2, 0, which[0])
            down(NT - 1, 1, which[1])

        @block.scalar
        def _(act):
            act.sem_inc(S("gelu"), 2)
            with act.Fori(0, NT // 2) as i:
                for q in range(2):
                    t = i * 2 + q
                    act.wait_ge(S("down"), t + 1)
                    act.wait_ge(S("w1s"), t + 1)
                    for c in range(KH):
                        if c % 2 == 0:
                            act.wait_ge(S("up"), t * 2 + (5 + c // 2))
                        last = nc.scalar.activation(hT[:, q, c, :], psH[q][c], ACT.Gelu, bias=b1s[:, q, c:c + 1])
                    last.then_inc(S("gelu"), 1)

        @block.vector
        def _(dve):
            dve.sem_inc(S("evicted"), 2)
            for q in range(2):
                dve.sem_inc(S(f"stored{q}"), 16)
            dve.wait_ge(S("norm"), 32)

            def scale(t, q):
                dve.wait_ge(S("turned"), t + 1)
                dve.wait_ge(S("up"), t * 2 + 2)
                dve.sem_inc(S("pause"), 1)
                for h in range(KD):
                    last = nc.vector.tensor_scalar(xT[:, q, h, :], psX[q][:, h, :], gamma[:, h:h + 1], beta[:, h:h + 1], ALU.mult, ALU.add)
                last.then_inc(S("xT"), 1)

            def evict(t, i, q, e):
                dve.wait_ge(S("down"), t + 3)
                dve.wait_ge(S(f"stored{q}"), i * 16 + 16)
                dve.sem_inc(S("pause"), 1)
                nc.vector.tensor_tensor(out[:, q, :, :], psY[q], b2[:, bass.ds(e, 1), :].to_broadcast([P, SUB, D]), ALU.add).then_inc(S("evicted"), 1)

            scale(0, 0)
            scale(1, 1)
            dve.wait_ge(S("b2"), 16 * E)
            with dve.Fori(0, NT // 2 - 1) as i:
                which = expert_of(ENGINE.DVE, i * 2, 2)
                for q in range(2):
                    scale(i * 2 + (2 + q), q)
                    evict(i * 2 + q, i, q, which[q])
            which = expert_of(ENGINE.DVE, NT - 2, 2)
            for q in range(2):
                evict(NT - 2 + q, NT // 2 - 1, q, which[q])


def combine(k):
    nc = k.nc
    S = lambda name: k.sem(f"co_{name}")
    xb = k.sb("co_x", [TB, 2, BATCH, D])
    g = k.sb("co_g", [TB, 2, BATCH, 2, D])
    idx = k.sb("co_idx", [TB, 2, BATCH, 2], I32)
    share = k.sb("co_share", [TB, 2, BATCH, 2])
    with nc.Block() as block:
        @block.sync
        def _(sp):
            def load(row, u):
                sp.dma_start(xb[:, u, :, :], rows_of(k.x1, row)).then_inc(S(f"x{u}"), 16)

            def store(row, n, u):
                sp.wait_ge(S("sum"), n + 2)
                sp.dma_start(rows_of(k.x2, row), xb[:, u, :, :]).then_inc(S(f"stored{u}"), 16)

            for u in range(2):
                load(u * ROWS, u)
            with sp.Fori(0, NBATCH // 2 - 1) as i:
                for u in range(2):
                    store(i * (2 * ROWS) + u * ROWS, i * 2 + (1 + u), u)
                    sp.wait_ge(S(f"stored{u}"), i * 16 + 16)
                    load(i * (2 * ROWS) + (2 + u) * ROWS, u)
            for u in range(2):
                store((NBATCH - 2 + u) * ROWS, NBATCH - 1 + u, u)
            for u in range(2):
                sp.wait_ge(S(f"stored{u}"), 16 * (NBATCH // 2))

        @block.gpsimd
        def _(pool):
            with pool.Fori(0, NBATCH // 2) as i:
                for u in range(2):
                    pool.wait_ge(S("sum"), i * 2 + (1 + u))
                    pool.sem_inc(S("pause"), 1)
                    nc.gpsimd.tensor_copy(share[:, u, :, :], k.share[:, bass.ds((i * 2 + u) * BATCH, BATCH), :])
                    nc.gpsimd.tensor_copy(idx[:, u, :, :], k.slots[:, bass.ds((i * 2 + u) * BATCH, BATCH), :]).then_inc(S("idx"), 1)
                    pool.wait_ge(S("idx"), i * 2 + (1 + u))
                    pool.sem_inc(S("pause"), 1)
                    for b in range(BATCH):
                        for j in range(2):
                            nc.gpsimd.indirect_dma_start(
                                g[:, u, b, j, :], None, k.ys,
                                bass.IndirectOffsetOnAxis(ap=idx[:, u, b, j:j + 1].bitcast(U32), axis=0)).then_inc(S(f"g{u}"), 16)

        @block.vector
        def _(dve):
            dve.sem_inc(S("sum"), 2)
            with dve.Fori(0, NBATCH // 2) as i:
                for u in range(2):
                    dve.wait_ge(S(f"x{u}"), i * 16 + 16)
                    dve.wait_ge(S("idx"), i * 2 + (1 + u))
                    dve.wait_ge(S(f"g{u}"), (i + 1) * (16 * BATCH * 2))
                    dve.sem_inc(S("pause"), 1)
                    for j in range(2):
                        for b in range(BATCH):
                            last = nc.vector.scalar_tensor_tensor(xb[:, u, b, :], g[:, u, b, j, :], share[:, u, b, j:j + 1], xb[:, u, b, :], ALU.mult, ALU.add)
                        if j == 0:
                            last.then_inc(S("half"), 1)
                            dve.wait_ge(S("half"), i * 2 + (1 + u))
                            dve.sem_inc(S("pause"), 1)
                    last.then_inc(S("sum"), 1)


def ffn1(k):
    nc, a = k.nc, k.a
    S = lambda name: k.sem(f"f1_{name}")
    K = 2
    w1 = k.sb("f1w1", [P, K, KD, HID])
    w2 = k.sb("f1w2", [P, K, KH, D])
    w2s = k.sb("f1w2s", [P, K, KH, D])
    b1 = k.sb("f1b1", [P, K, KH])
    b2 = k.sb("f1b2", [1, K, D])
    b2m = k.sb("f1b2m", [1, K, D])
    bias = k.sb("f1bias", [TB, 1, D])
    gamma = k.sb("f1gamma", [TB, 1, D])
    beta = k.sb("f1beta", [TB, 1, D])
    wr = k.sb("f1wr", [P, KD, E])
    br = k.sb("f1br", [1, E])
    ones = k.sb("f1ones", [1, P])
    mean = k.sb("f1mean", [P, KD])
    row = k.sb("f1row", [1, 8, E])
    best = k.sb("f1best", [1, 8])
    besti = k.sb("f1besti", [1, 8], U32)
    pair = k.sb("f1pair", [1, 4])
    pcol = k.sb("f1pcol", [P, K])
    xg = k.sb("f1xg", [TB, 2, 2, D])
    yg = k.sb("f1yg", [TB, 2, 2, D])
    res = k.sb("f1res", [TB, 2, 2, D])
    z = k.sb("f1z", [TB, 2, 2, D])
    st = k.sb("f1st", [TB, 2, 2, 6])
    mv = k.sb("f1mv", [TB, 2, 2, 2])
    hT = k.sb("f1hT", [P, 2, K, KH, GTOK])
    ps = k.ps
    psH = [[ps[:, 2 * q + c // 2, (c % 2) * 256:(c % 2) * 256 + GTOK] for c in range(KH)] for q in range(2)]
    psY = [ps[0:TB, 4 + q, 0:2 * D].rearrange("p (t d) -> p t d", t=2) for q in range(2)]
    with nc.Block() as block:
        @block.sync
        def _(sp):
            for dst, src in [(gamma[:, 0, :], a["L1_ffn_gamma"].to_broadcast([TB, D])), (beta[:, 0, :], a["L1_ffn_beta"].to_broadcast([TB, D])),
                             (wr[:, :, :], a["L1_ffn_Wr"].rearrange("(h p) e -> p h e", p=P)), (br[:, :], a["L1_ffn_br"])]:
                sp.dma_start(dst, src).then_inc(S("small"), 16)
            sp.wait_ge(S("besti"), 1)
            _, which = nc.values_load_multi_w_load_instructions(
                besti[0:1, 0:K].bitcast(I32), engines=[ENGINE.SP], min_val=0, max_val=E - 1,
                skip_runtime_bounds_check_because="a place in a row of eight")
            for j in range(K):
                sp.dma_start(w1[:, j, :, :], a["L1_ffn_W1"][bass.ds(which[j], 1), :, :].rearrange("o (h p) n -> p (o h) n", p=P)).then_inc(S("w"), 16)
                sp.dma_start(w2[:, j, :, :], a["L1_ffn_W2"][bass.ds(which[j], 1), :, :].rearrange("o (c p) n -> p (o c) n", p=P)).then_inc(S("w"), 16)
                sp.dma_start(b1[:, j, :], a["L1_ffn_b1"][bass.ds(which[j], 1), :, :].rearrange("o p c -> p (o c)")).then_inc(S("w"), 16)
                sp.dma_start(b2[:, j, :], a["L1_ffn_b2"][bass.ds(which[j], 1), :]).then_inc(S("w"), 16)

        @block.tensor
        def _(pe):
            for h in range(KD):
                last = nc.tensor.matmul(ps[:, 0, h:h + 1], k.ysum[:, h * P:(h + 1) * P], k.ones[0:TB, :], start=True, stop=True)
            last.then_inc(S("mean_ps"), 1)
            pe.wait_ge(S("small"), 64)
            pe.wait_ge(S("mean"), 1)
            for h in range(KD):
                last = nc.tensor.matmul(ps[0:1, 1, 0:E], mean[:, h:h + 1], wr[:, h, :], start=(h == 0), stop=(h == KD - 1))
            last.then_inc(S("logit_ps"), 1)
            pe.wait_ge(S("pair"), 1)
            nc.tensor.matmul(ps[:, 2, 0:K], ones[:, :], pair[:, 0:K], start=True, stop=True).then_inc(S("pcol_ps"), 1)
            pe.wait_ge(S("b2m"), 1)
            for j in range(K):
                last = nc.tensor.matmul(ps[0:TB, 3, 0:D], ones[:, 0:TB], b2m[:, j, :], start=(j == 0), stop=(j == K - 1))
            last.then_inc(S("bias_ps"), 1)

        @block.scalar
        def _(act):
            act.wait_ge(S("mean_ps"), 1)
            nc.scalar.mul(mean[:, :], ps[:, 0, 0:KD], 1.0 / N).then_inc(S("mean"), 1)
            for n in range(2):
                act.wait_ge(S("shifted"), n + 1)
                nc.scalar.activation(row[:, 2, :], row[:, 1, :], ACT.Exp).then_inc(S("ex"), 1)
            act.wait_ge(S("gap"), 1)
            nc.scalar.activation(pair[:, 3:4], pair[:, 2:3], ACT.Exp).then_inc(S("ex"), 1)

        @block.vector
        def _(dve):
            done = [0]

            def link(ins):
                done[0] += 1
                ins.then_inc(S("chain"), 1)
                dve.wait_ge(S("chain"), done[0])

            link(nc.vector.memset(ones[:, :], 1.0))
            dve.wait_ge(S("logit_ps"), 1)
            link(nc.vector.tensor_tensor(row[:, 0, :], ps[0:1, 1, 0:E], br[:, :], ALU.add))

            def softmax(n):
                link(nc.vector.tensor_reduce(row[:, 4, 0:1], row[:, 0, :], AX.X, ALU.max))
                nc.vector.tensor_scalar(row[:, 1, :], row[:, 0, :], row[:, 4, 0:1], None, ALU.subtract).then_inc(S("shifted"), 1)
                dve.wait_ge(S("ex"), n)
                link(nc.vector.tensor_reduce(row[:, 4, 1:2], row[:, 2, :], AX.X, ALU.add))
                link(nc.vector.reciprocal(row[:, 4, 2:3], row[:, 4, 1:2]))
                link(nc.vector.tensor_scalar(row[:, 3, :], row[:, 2, :], row[:, 4, 2:3], None, ALU.mult))

            softmax(1)
            link(nc.vector.tensor_scalar(row[:, 5, :], row[:, 3, :], float(N), CAPACITY, ALU.mult, ALU.max))
            link(nc.vector.reciprocal(row[:, 5, :], row[:, 5, :]))
            link(nc.vector.tensor_scalar(row[:, 5, :], row[:, 5, :], CAPACITY, None, ALU.mult))
            link(nc.vector.tensor_tensor(row[:, 0, :], row[:, 3, :], row[:, 5, :], ALU.mult))
            softmax(2)
            link(nc.vector.max(best[:, :], row[:, 3, :]))
            nc.vector.max_index(besti[:, :], best[:, :], row[:, 3, :]).then_inc(S("besti"), 1)
            nc.vector.tensor_tensor(pair[:, 2:3], best[:, 1:2], best[:, 0:1], ALU.subtract).then_inc(S("gap"), 1)
            dve.wait_ge(S("ex"), 3)
            link(nc.vector.tensor_scalar(row[:, 6, 0:1], pair[:, 3:4], 1.0, None, ALU.add))
            link(nc.vector.reciprocal(pair[:, 0:1], row[:, 6, 0:1]))
            nc.vector.tensor_tensor(pair[:, 1:2], pair[:, 0:1], pair[:, 3:4], ALU.mult).then_inc(S("pair"), 1)
            dve.wait_ge(S("pcol_ps"), 1)
            link(nc.vector.tensor_copy(pcol[:, :], ps[:, 2, 0:K]))
            dve.wait_ge(S("w"), 16 * 4 * K)
            for j in range(K):
                link(nc.vector.tensor_scalar(w2s[:, j, :, :], w2[:, j, :, :], pcol[:, j:j + 1], None, ALU.mult))
            link(nc.vector.tensor_scalar(b2m[:, 0, :], b2[:, 0, :], pcol[0:1, 0:1], None, ALU.mult))
            nc.vector.tensor_scalar(b2m[:, 1, :], b2[:, 1, :], pcol[0:1, 1:2], None, ALU.mult).then_inc(S("b2m"), 1)
            dve.wait_ge(S("bias_ps"), 1)
            nc.vector.tensor_copy(bias[:, 0, :], ps[0:TB, 3, 0:D])

    with nc.Block() as block:
        @block.sync
        def _(sp):
            group = lambda ap, g: ap[bass.ds(g * GTOK, GTOK), :].rearrange("(t p) d -> p t d", p=TB)

            def load(g, q):
                sp.dma_start(yg[:, q, :, :], group(k.y3, g)).then_inc(S(f"in{q}"), 16)
                sp.dma_start(xg[:, q, :, :], group(k.x3, g)).then_inc(S(f"in{q}"), 16)

            def store(g, q):
                sp.wait_ge(S("out"), g + 1)
                sp.dma_start(group(a["out"], g), res[:, q, :, :]).then_inc(S(f"stored{q}"), 16)

            for q in range(2):
                load(q, q)
            with sp.Fori(0, NG // 2 - 1) as i:
                for q in range(2):
                    store(i * 2 + q, q)
                    load(i * 2 + (2 + q), q)
            store(NG - 3, 0)
            load(NG - 1, 0)
            store(NG - 2, 1)
            store(NG - 1, 0)
            for q in range(2):
                sp.wait_ge(S(f"stored{q}"), 16 * (1 + NG // 2 + (NG - q) % 2))

        @block.tensor
        def _(pe):
            pe.sem_inc(S("down"), 2)

            def up(g):
                for j in range(K):
                    pe.wait_ge(S("gelu"), g * K + (j + 1))
                    for c in range(KH):
                        for h in range(KD):
                            last = nc.tensor.matmul(psH[j][c], w1[:, j, h, c * P:(c + 1) * P], k.acc[:, h, bass.ds(g * GTOK, GTOK)],
                                                    start=(h == 0), stop=(h == KD - 1))
                    last.then_inc(S("up"), 1)

            def down(g, q):
                pe.wait_ge(S("gelu"), g * K + (K + 2))
                pe.wait_ge(S("read"), g + 1)
                for tt in range(2):
                    for j in range(K):
                        for c in range(KH):
                            last = nc.tensor.matmul(psY[q][:, tt, :], hT[:, q, j, c, tt * TB:(tt + 1) * TB], w2s[:, j, c, :],
                                                    start=(j == 0 and c == 0), stop=(j == K - 1 and c == KH - 1))
                last.then_inc(S("down"), 1)

            up(0)
            with pe.Fori(0, NG // 2) as i:
                for q in range(2):
                    up(i * 2 + (1 + q))
                    down(i * 2 + q, q)
            down(NG - 1, 0)

        @block.scalar
        def _(act):
            act.sem_inc(S("gelu"), 2)

            def gelu(g, q):
                act.wait_ge(S("down"), g + 1)
                for j in range(K):
                    act.wait_ge(S("up"), g * K + (j + 1))
                    for c in range(KH):
                        last = nc.scalar.activation(hT[:, q, j, c, :], psH[j][c], ACT.Gelu, bias=b1[:, j, c:c + 1])
                    last.then_inc(S("gelu"), 1)

            gelu(0, 0)
            with act.Fori(0, NG // 2) as i:
                for q in range(2):
                    gelu(i * 2 + (1 + q), 1 - q)
                    root_step(k, "f1", act, mv[:, q, :, :], i * 2 + (1 + q))
            root_step(k, "f1", act, mv[:, 0, :, :], NG)

        @block.vector
        def _(dve):
            dve.sem_inc(S("read"), 2)
            for q in range(2):
                dve.sem_inc(S(f"stored{q}"), 16)
            both = lambda row: row[:, :, :].to_broadcast([TB, 2, D])

            def finish(g, i, q):
                n = g + 1
                dve.wait_ge(S(f"in{q}"), i * 32 + 32)
                nc.vector.tensor_tensor(yg[:, q, :, :], yg[:, q, :, :], both(bias), ALU.add).then_inc(S("biased"), 1)
                nc.vector.tensor_tensor(xg[:, q, :, :], xg[:, q, :, :], both(beta), ALU.add).then_inc(S("shifted_x"), 1)
                dve.wait_ge(S("biased"), n)
                dve.wait_ge(S("down"), n + 2)
                nc.vector.tensor_tensor(yg[:, q, :, :], psY[q], yg[:, q, :, :], ALU.add).then_inc(S("read"), 1)
                dve.wait_ge(S("read"), n + 2)
                norm_steps(k, "f1", dve, yg[:, q, :, :], st[:, q, :, :], mv[:, q, :, :], z[:, q, :, :], n).then_inc(S("normed"), 1)
                dve.wait_ge(S("normed"), n)
                nc.vector.tensor_tensor(z[:, q, :, :], z[:, q, :, :], both(gamma), ALU.mult).then_inc(S("scaled"), 1)
                dve.wait_ge(S("scaled"), n)
                dve.wait_ge(S("shifted_x"), n)
                dve.wait_ge(S(f"stored{q}"), i * 16 + 16)
                nc.vector.tensor_tensor(res[:, q, :, :], z[:, q, :, :], xg[:, q, :, :], ALU.add).then_inc(S("out"), 1)

            with dve.Fori(0, NG // 2) as i:
                for q in range(2):
                    finish(i * 2 + q, i, q)
            finish(NG - 1, NG // 2, 0)


_PLAIN = ["x", "L0_gnn_W", "L1_gnn_W", "L0_ffn_Wr", "L0_ffn_W1", "L0_ffn_W2", "L0_ffn_b2",
          "L1_ffn_Wr", "L1_ffn_W1", "L1_ffn_W2", "L1_ffn_b2"]
_ROWS = ["L0_ffn_gamma", "L0_ffn_beta", "L0_ffn_br", "L1_ffn_gamma", "L1_ffn_beta", "L1_ffn_br"]


def laid_out(inputs):
    import numpy as np

    out = {n: np.ascontiguousarray(inputs[n]) for n in _PLAIN}
    out.update({n: np.ascontiguousarray(inputs[n]).reshape(1, -1) for n in _ROWS})
    for n in ("L0_ffn_b1", "L1_ffn_b1"):
        out[n] = np.ascontiguousarray(np.asarray(inputs[n]).reshape(E, KH, P).transpose(0, 2, 1))
    pad = TILES * P - NE
    src, dst = np.asarray(inputs["src"]), np.asarray(inputs["dst"])
    dist = np.asarray(inputs["edge_attr3_1x1"]).reshape(-1)
    nodest = np.full(pad, -1, dst.dtype)
    dstp = np.concatenate([dst, nodest])
    edge_major = lambda v: np.ascontiguousarray(v.reshape(TILES, P).T)
    out["src_e"] = edge_major(np.concatenate([src, np.zeros(pad, src.dtype)]))
    out["dst_e"] = edge_major(dstp)
    out["dist_e"] = edge_major(np.concatenate([dist, np.zeros(pad, dist.dtype)]))
    out["dst_t"] = dstp.reshape(TILES, P)
    out["dst_prev_t"] = np.concatenate([np.full(1, -2, dst.dtype), dstp[:-1]]).reshape(TILES, P)
    out["dst_next_t"] = np.concatenate([dstp[1:], np.full(1, -2, dst.dtype)]).reshape(TILES, P)
    out["n0"] = np.ascontiguousarray(dstp[::P]).reshape(1, TILES)
    for layer, (left, right) in enumerate([("L0_gnn_w_att_src", "L0_gnn_w_att_dst"), ("L1_gnn_attn_l", "L1_gnn_attn_r")]):
        H = HEADS[layer]
        DH = D // H
        att = np.zeros((D, 2 * H), np.float32)
        for side, name in enumerate((left, right)):
            v = np.asarray(inputs[name]).reshape(H, DH)
            for h in range(H):
                att[h * DH:(h + 1) * DH, side * H + h] = v[h]
        out[f"att{layer}"] = att
        f = np.arange(D)
        spread = np.zeros((H, KD, P), np.float32)
        spread[f // DH, f // P, f % P] = 1
        out[f"spread{layer}"] = spread
        mask = np.zeros((H, 3, P), np.float32)
        mask[:, 0:KD, :] = spread
        mask[np.arange(H), KD, np.arange(H)] = 1
        out[f"mask{layer}"] = mask.reshape(1, -1)
    out["ident"] = np.eye(P, dtype=np.float32)
    out["before"] = np.triu(np.ones((TB, TB), np.float32), 1)
    out["iota"] = np.tile(np.arange(P, dtype=np.float32), (P, 1))
    out["negpart"] = -np.arange(P, dtype=np.float32).reshape(P, 1)
    return out


def kernel(**inputs):
    from concourse import bacc
    from concourse.bass_utils import run_bass_kernel_spmd as run

    nc = bacc.Bacc("TRN2", target_bir_lowering=False, num_devices=1)
    arrays = laid_out(inputs)
    aps = {n: nc.dram_tensor("in_" + n, v.shape, mybir.dt.from_np(v.dtype), kind="ExternalInput").ap() for n, v in arrays.items()}
    aps["out"] = nc.dram_tensor("out_0", (N, D), F32, kind="ExternalOutput").ap()
    emit(nc, aps)
    r = run(nc, [{"in_" + n: v for n, v in arrays.items()}], core_ids=[0])
    return r.results[0]["out_0"]
```

```python
import concourse.bass as bass
from concourse import mybir
from contextlib import ExitStack, contextmanager

F32 = mybir.dt.float32
BF16 = mybir.dt.bfloat16
F32R = mybir.dt.float32r
I32 = mybir.dt.int32
U32 = mybir.dt.uint32
ALU = mybir.AluOpType
ACT = mybir.ActivationFunctionType
AX = mybir.AxisListType
ENGINE = mybir.EngineType

N = 6250
D = 256
NE = 106250
P = 128
KD = D // P
TILES = 832
CH = 16
CHUNKS = TILES // CH
RING = 4
TB = 125
NB = N // TB
BATCH = 5
ROWS = BATCH * TB
NBATCH = NB // BATCH
PADN = N + P
NSLOT = 4
AHEAD = 3
G = 104
GT = TILES // G
GTOK = 2 * TB
NG = N // GTOK
E = 8
HID = 512
KH = HID // P
BIG = 1.0e30
EPS = 1e-5
SLOPE = 0.2
CAPACITY = 977.0
ROWS_OF_TILE = 256
NT = (2 * N + E * (ROWS_OF_TILE - 1)) // ROWS_OF_TILE
MOST = -(-N // ROWS_OF_TILE)
REGION = (MOST + 1) * ROWS_OF_TILE
PASSES = ((0, 0), (0, 1), (1, 0))
HEADS = (4, 8)
ACT_TILES = ([0, 2, 3, 4, 5, 6, 7, 8, 9, 10, 11, 12, 15], [1, 2, 4, 5, 7, 9, 10, 11, 12, 15])
SCHEDULE = ({
    "dve": {-8: ["one_hot"], -4: ["scan_1"], -2: ["carries"], -1: ["bring", "carry_on"], 0: ["scan_2"],
            1: ["ce_1"], 2: ["scan_3"], 3: ["sum_0", "backward"], 4: ["leaky_0"], 5: ["meet", "ce_2"],
            7: ["scan_4", "ce_3"], 9: ["sum_1"], 10: ["leaky_1"], 11: ["diff", "ce_4"],
            12: ["ce_5", "weights"]},
    "pe": {-6: ["expand0"], -5: ["expand1"], -4: ["expand2"], -3: ["turn", "expand3"], -2: ["last_row"],
            1: ["column"], 4: ["first_row"], 7: ["column2"], 9: ["running"], 14: ["factor"]},
    "act": {-4: ["first", "small"], 1: ["expand"], 12: ["exps"], 14: ["factor"]},
}, {
    "dve": {-8: ["one_hot"], -4: ["scan_1"], -2: ["carries"], -1: ["bring", "carry_on"],
            1: ["scan_2", "ce_1"], 2: ["scan_3"], 3: ["sum_0"], 4: ["backward", "leaky_0"],
            5: ["meet", "ce_2"], 7: ["scan_4", "ce_3"], 9: ["sum_1", "leaky_1", "diff", "ce_4", "ce_5"],
            11: ["weights"]},
    "pe": {-6: ["expand0", "expand1"], -4: ["expand2"], -3: ["turn", "expand3"], -1: ["last_row"],
            1: ["column"], 4: ["first_row"], 7: ["column2"], 9: ["running"], 15: ["factor"]},
    "act": {-4: ["first", "small"], 1: ["expand"], 14: ["exps", "factor"]},
})


class Kernel:

    def __init__(self, nc, a):
        self.nc, self.a, self.sems = nc, a, {}
        self.root = ExitStack()
        self.stack = self.root

    def sem(self, name):
        if name not in self.sems:
            self.sems[name] = self.nc.alloc_semaphore(name=name)
        return self.sems[name]

    def sb(self, name, shape, dt=F32):
        return self.stack.enter_context(self.nc.sbuf_tensor(name, shape, dt))

    def stage(self, run, *args):
        run(self, *args)
        self.nc.clear_and_free_semaphores(list(self.sems.values()))
        self.nc.all_engine_barrier()
        self.sems = {}

    def dram(self, name, shape, dt=F32):
        return self.nc.dram_tensor(name, shape, dt, kind="Internal").ap()

    @contextmanager
    def phase(self):
        outer = self.stack
        with ExitStack() as self.stack:
            yield
        self.stack = outer


def emit(nc, a):
    k = Kernel(nc, a)
    with k.root:
        k.ps = k.root.enter_context(nc.psum_tensor("ps", [P, 8, 512], F32))
        k.acc = k.sb("acc", [P, 3, PADN])
        k.ident = k.sb("ident", [P, P])
        k.iota = k.sb("iota", [P, P])
        k.iota_b = k.sb("iota_b", [P, P], BF16)
        k.part = k.sb("part", [P, 1])
        k.ones = k.sb("ones", [P, 1])
        k.eps = k.sb("eps", [P, 1])
        k.seg = k.dram("seg_start_penalty", [TILES, P])
        k.segr = k.dram("seg_end_penalty", [TILES, P])
        k.reld = k.dram("rel_rows", [TILES, P], BF16)
        k.single = k.dram("single_segment", [1, TILES])
        k.first = k.dram("first_penalty", [1, TILES])
        k.x1 = k.dram("x1", [N, D])
        k.x2 = k.dram("x2", [N, D])
        k.x3 = k.dram("x3", [N, D])
        k.y3 = k.dram("y3", [N, D])
        k.xs = k.dram("xs", [E * REGION, D])
        k.ys = k.dram("ys", [NT * ROWS_OF_TILE, D])
        with k.phase():
            k.srcE = k.sb("srcE", [P, TILES], I32)
            k.relE = k.sb("relE", [P, TILES])
            k.distE = k.sb("distE", [P, TILES])
            k.n0 = k.sb("n0", [1, TILES], I32)
            k.single_row = k.sb("single_row", [1, TILES])
            k.first_row = k.sb("first_row", [1, TILES])
            k.stage(prepare)
            k.stage(table, 0, a["x"], a["L0_gnn_W"], a["att0"])
            k.stage(edges, 0)
        with k.phase():
            k.slots = k.sb("slots", [TB, NB, 2], I32)
            k.share = k.sb("share", [TB, NB, 2])
            with k.phase():
                k.w1 = k.sb("f0w1", [P, E, KD, HID])
                k.w2 = k.sb("f0w2", [P, E, KH, D])
                k.best = k.sb("best", [TB, NB, 2])
                k.chosen = k.sb("chosen", [TB, NB, 2])
                k.sent = k.sb("sent", [TB, NB, 2])
                k.run = k.sb("run", [TB, 1, E])
                k.iota8 = k.sb("iota8", [TB, E])
                k.zero = k.sb("zero", [P, 1, D])
                k.stage(nodes, 0, a["x"], k.x1)
                ffn0(k)
            k.srcE = k.sb("srcE1", [P, TILES], I32)
            k.relE = k.sb("relE1", [P, TILES])
            k.distE = None
            k.n0 = k.sb("n0_1", [1, TILES], I32)
            k.single_row = k.sb("single_row1", [1, TILES])
            k.first_row = k.sb("first_row1", [1, TILES])
            k.stage(reload)
            k.stage(table, 1, k.x1, a["L1_gnn_W"], a["att1"])
            k.stage(edges, 1)
        with k.phase():
            k.ysum = k.sb("ysum", [TB, D])
            k.stage(nodes, 1, k.x2, k.x3)
            with k.phase():
                k.stage(ffn1)


def rows_of(ap, row):
    return ap[bass.ds(row, ROWS), :].rearrange("(b p) d -> p b d", p=TB)


def prepare(k):
    nc, a = k.nc, k.a
    with k.phase():
        dT = k.sb("dT", [G, GT, P], I32)
        prevT = k.sb("prevT", [G, GT, P], I32)
        nextT = k.sb("nextT", [G, GT, P], I32)
        firstT = k.sb("firstT", [G, GT, 1])
        pen = k.sb("pen", [G, GT, P])
        penr = k.sb("penr", [G, GT, P])
        relT = k.sb("relT", [G, GT, P], BF16)
        lone = k.sb("lone", [G, GT])
        dE = k.sb("dE", [P, TILES], I32)
        n0E = k.sb("n0E", [P, TILES], I32)
        n0f = k.sb("n0f", [P, TILES])
        n0raw = k.sb("n0raw", [1, TILES], I32)
        loaded, step, stored = k.sem("prep_loaded"), k.sem("prep_step"), k.sem("prep_stored")
        rows_loaded = k.sem("prep_rows")
        view = lambda ap: ap.rearrange("(g p) e -> p g e", p=G)
        loads = [(dT[:, :, :], view(a["dst_t"])), (prevT[:, :, :], view(a["dst_prev_t"])),
                 (nextT[:, :, :], view(a["dst_next_t"])), (dE[:, :], a["dst_e"]),
                 (n0E[:, :], a["n0"].to_broadcast([P, TILES])), (n0raw[:, :], a["n0"]),
                 (k.srcE[:, :], a["src_e"]), (k.distE[:, :], a["dist_e"]),
                 (k.ident[:, :], a["ident"]), (k.iota[:, :], a["iota"]), (k.part[:, :], a["part"])]
        with nc.Block() as block:
            @block.sync
            def _(sp):
                for dst, src in loads:
                    sp.dma_start(dst, src).then_inc(loaded, 16)
                sp.wait_ge(step, 12)
                sp.dma_start(view(k.seg), pen[:, :, :]).then_inc(stored, 16)
                sp.dma_start(view(k.segr), penr[:, :, :]).then_inc(stored, 16)
                sp.dma_start(view(k.reld), relT[:, :, :]).then_inc(stored, 16)
                with nc.allow_non_contiguous_dma("832 words of each, once"):
                    sp.dma_start(k.single.rearrange("o (g p) -> p (o g)", p=G), lone[:, :]).then_inc(stored, 16)
                    sp.dma_start(k.first.rearrange("o (g p) -> p (o g)", p=G), pen[:, :, 0]).then_inc(stored, 16)
                sp.wait_ge(stored, 16 * 5)
                sp.dma_start(k.single_row[:, :], k.single).then_inc(rows_loaded, 16)
                sp.dma_start(k.first_row[:, :], k.first).then_inc(rows_loaded, 16)
                sp.wait_ge(rows_loaded, 32)

            @block.vector
            def _(dve):
                done = [0]

                def link(ins):
                    done[0] += 1
                    ins.then_inc(step, 1)
                    dve.wait_ge(step, done[0])

                link(nc.vector.memset(k.ones[:, :], 1.0))
                link(nc.vector.memset(k.eps[:, :], EPS))
                dve.wait_ge(loaded, 16 * len(loads))
                link(nc.vector.tensor_copy(k.iota_b[:, :], k.iota[:, :]))
                link(nc.vector.tensor_scalar(firstT[:, :, :], dT[:, :, 0:1], 0.0, None, ALU.max))
                link(nc.vector.tensor_tensor(relT[:, :, :], dT[:, :, :], firstT[:, :, :].to_broadcast([G, GT, P]), ALU.subtract))
                link(nc.vector.tensor_tensor(pen[:, :, :], dT[:, :, :], prevT[:, :, :], ALU.not_equal))
                link(nc.vector.tensor_scalar(pen[:, :, :], pen[:, :, :], -BIG, None, ALU.mult))
                link(nc.vector.tensor_tensor(penr[:, :, :], dT[:, :, :], nextT[:, :, :], ALU.not_equal))
                link(nc.vector.tensor_scalar(penr[:, :, :], penr[:, :, :], -BIG, None, ALU.mult))
                link(nc.vector.tensor_reduce(lone[:, :], pen[:, :, :], AX.X, ALU.min))
                link(nc.vector.tensor_scalar(k.n0[:, :], n0raw[:, :], 0.0, None, ALU.max))
                link(nc.vector.tensor_scalar(n0f[:, :], n0E[:, :], 0.0, None, ALU.max))
                link(nc.vector.tensor_tensor(k.relE[:, :], dE[:, :], n0f[:, :], ALU.subtract))


def reload(k):
    nc, a = k.nc, k.a
    with k.phase():
        dE = k.sb("dE1", [P, TILES], I32)
        n0E = k.sb("n0E1", [P, TILES], I32)
        n0f = k.sb("n0f1", [P, TILES])
        n0raw = k.sb("n0raw1", [1, TILES], I32)
        loaded, step = k.sem("reload_loaded"), k.sem("reload_step")
        loads = [(dE[:, :], a["dst_e"]), (n0E[:, :], a["n0"].to_broadcast([P, TILES])),
                 (n0raw[:, :], a["n0"]), (k.srcE[:, :], a["src_e"]),
                 (k.single_row[:, :], k.single), (k.first_row[:, :], k.first)]
        with nc.Block() as block:
            @block.sync
            def _(sp):
                for dst, src in loads:
                    sp.dma_start(dst, src).then_inc(loaded, 16)

            @block.vector
            def _(dve):
                dve.wait_ge(loaded, 16 * len(loads))
                nc.vector.tensor_scalar(k.n0[:, :], n0raw[:, :], 0.0, None, ALU.max)
                nc.vector.tensor_scalar(n0f[:, :], n0E[:, :], 0.0, None, ALU.max).then_inc(step, 1)
                dve.wait_ge(step, 1)
                nc.vector.tensor_tensor(k.relE[:, :], dE[:, :], n0f[:, :], ALU.subtract)


def norm_stats(k, dve, tag, x, stats, mv, out, n):
    for b in range(x.shape[1]):
        last = k.nc.vector.bn_stats(stats[:, b, :], x[:, b, :])
    last.then_inc(k.sem(tag + "_stats"), 1)


def norm_var(k, dve, tag, x, stats, mv, out, n):
    dve.wait_ge(k.sem(tag + "_stats"), n)
    dve.sem_inc(k.sem(tag + "_pause"), 1)
    for b in range(x.shape[1]):
        last = k.nc.vector.bn_aggr(mv[:, b, :], stats[:, b, :])
    last.then_inc(k.sem(tag + "_var"), 1)


def norm_root(k, dve, tag, x, stats, mv, out, n):
    dve.wait_ge(k.sem(tag + "_root"), n)
    dve.sem_inc(k.sem(tag + "_pause"), 1)
    k.nc.vector.reciprocal(mv[:, :, 1:2], mv[:, :, 1:2]).then_inc(k.sem(tag + "_rstd"), 1)


def norm_rows(k, dve, tag, x, stats, mv, out, n, each=None, between=None):
    dve.wait_ge(k.sem(tag + "_rstd"), n)
    for b in range(x.shape[1]):
        last = k.nc.vector.tensor_scalar(out[:, b, :], x[:, b, :], mv[:, b, 0:1], mv[:, b, 1:2], ALU.subtract, ALU.mult)
        if each is not None:
            last.then_inc(each, 1)
        if between is not None:
            between()
    return last


def norm_steps(k, tag, dve, x, stats, mv, out, n, each=None):
    norm_stats(k, dve, tag, x, stats, mv, out, n)
    norm_var(k, dve, tag, x, stats, mv, out, n)
    norm_root(k, dve, tag, x, stats, mv, out, n)
    return norm_rows(k, dve, tag, x, stats, mv, out, n, each)


def root_step(k, tag, act, mv, n):
    act.wait_ge(k.sem(tag + "_var"), n)
    k.nc.scalar.activation(mv[:, :, 1:2], mv[:, :, 1:2], ACT.Sqrt, bias=k.eps[0:TB, :]).then_inc(k.sem(tag + "_root"), 1)


def table(k, layer, x, w, att):
    nc, H = k.nc, HEADS[layer]
    W = D + 2 * H
    t = f"tab{layer}"
    k.rows = k.dram(f"rows{layer}", [N, D + H])
    k.edst = k.dram(f"edst{layer}", [PADN, 3 * H], BF16)
    S = lambda name: k.sem(f"{t}_{name}")
    with k.phase():
        wsb = k.sb(t + "w", [P, KD, D])
        attsb = k.sb(t + "att", [P, KD, 2 * H])
        wT = k.sb(t + "wT", [P, KD, D])
        wext = k.sb(t + "wext", [P, KD, W])
        zpad = k.sb(t + "zpad", [P, 3 * H], BF16)
        parts = k.sb(t + "parts", [TB, 2, BATCH, 3, H], BF16)
        rest = k.sb(t + "rest", [TB, 2, BATCH, 2, H])
        xb = k.sb(t + "x", [TB, 2, BATCH, D])
        xn = k.sb(t + "xn", [TB, 2, BATCH, D]) if layer == 1 else xb
        if layer == 1:
            g = k.sb(t + "g", [TB, 2, BATCH, 2, D])
            idx = k.sb(t + "idx", [TB, 2, BATCH, 2], I32)
            share = k.sb(t + "share", [TB, 2, BATCH, 2])
        xt = k.sb(t + "xt", [P, 2, KD, TB])
        tb = k.sb(t + "tb", [TB, 2, BATCH, W])
        st = k.sb(t + "st", [TB, 2, BATCH, 6])
        mv = k.sb(t + "mv", [TB, 2, BATCH, 2])
        psT = [k.ps[:, u, 0:KD * TB].rearrange("p (h n) -> p h n", h=KD) for u in range(2)]
        psO = [k.ps[0:TB, 2 + u, 0:W] for u in range(2)]
        psW, psA = k.ps[:, 4, 0:512].rearrange("p (h n) -> p h n", h=KD), k.ps[:, 5, 0:KD * 2 * H].rearrange("p (h n) -> p h n", h=KD)
        with nc.Block() as block:
            @block.sync
            def _(sp):
                sp.dma_start(wsb[:, :, :], w.rearrange("(h p) n -> p h n", p=P)).then_inc(S("w"), 16)
                sp.dma_start(attsb[:, :, :], att.rearrange("(h p) n -> p h n", p=P)).then_inc(S("w"), 16)

                def load(row, u):
                    sp.dma_start(xb[:, u, :, :], rows_of(x, row)).then_inc(S(f"x{u}"), 16)

                def store(row, n, u):
                    if layer == 1:
                        sp.wait_ge(S("sum"), n + 2)
                        sp.dma_start(rows_of(k.x2, row), xb[:, u, :, :]).then_inc(S(f"kept{u}"), 16)
                    sp.wait_ge(S("row"), n * BATCH)
                    sp.dma_start(rows_of(k.rows, row), tb[:, u, :, 0:D + H]).then_inc(S(f"stored{u}"), 16)
                    sp.wait_ge(S("parts"), n)
                    sp.dma_start(rows_of(k.edst, row), parts[:, u, :, :, :].rearrange("p b k h -> p b (k h)")).then_inc(S(f"stored{u}"), 16)

                for u in range(2):
                    load(u * ROWS, u)
                with sp.Fori(0, NBATCH // 2 - 1) as i:
                    for u in range(2):
                        store(i * (2 * ROWS) + u * ROWS, i * 2 + (1 + u), u)
                        if layer == 1:
                            sp.wait_ge(S(f"kept{u}"), i * 16 + 16)
                        load(i * (2 * ROWS) + (2 + u) * ROWS, u)
                for u in range(2):
                    store((NBATCH - 2 + u) * ROWS, NBATCH - 1 + u, u)
                for u in range(2):
                    sp.wait_ge(S(f"stored{u}"), 32 + 32 * (NBATCH // 2))
                    if layer == 1:
                        sp.wait_ge(S(f"kept{u}"), 16 * (NBATCH // 2))

            @block.vector
            def _(dve):
                nc.vector.memset(zpad[:, :], 0.0).then_inc(S("zpad"), 1)
                dve.wait_ge(S("wTp"), 1)
                nc.vector.tensor_copy(wT[:, :, :], psW).then_inc(S("wT"), 1)
                dve.wait_ge(S("w"), 32)
                nc.vector.tensor_copy(wext[:, :, 0:D], wsb[:, :, :]).then_inc(S("wext"), 1)
                dve.wait_ge(S("attp"), 1)
                nc.vector.tensor_copy(wext[:, :, D:W], psA).then_inc(S("wext"), 1)
                if layer == 1:
                    dve.sem_inc(S("sum"), 2)

                def add_experts(i, u):
                    dve.wait_ge(S("idx"), i * 2 + (1 + u))
                    dve.wait_ge(S(f"g{u}"), (i + 1) * (16 * BATCH * 2))
                    dve.sem_inc(S("pause"), 1)
                    for j in range(2):
                        for b in range(BATCH):
                            last = nc.vector.scalar_tensor_tensor(xb[:, u, b, :], g[:, u, b, j, :], share[:, u, b, j:j + 1], xb[:, u, b, :], ALU.mult, ALU.add)
                        name = ("half", "sum")[j]
                        last.then_inc(S(name), 1)
                        dve.wait_ge(S(name), i * 2 + (1 + u + 2 * j))
                        dve.sem_inc(S("pause"), 1)

                with dve.Fori(0, NBATCH // 2) as i:
                    for u in range(2):
                        dve.wait_ge(S(f"x{u}"), i * 16 + 16)
                        dve.sem_inc(S("pause"), 1)
                        if layer == 1:
                            add_experts(i, u)
                        norm_steps(k, t, dve, xb[:, u, :, :], st[:, u, :, :], mv[:, u, :, :], xn[:, u, :, :], i * 2 + (1 + u), S("normed"))

            @block.tensor
            def _(pe):
                pe.wait_ge(S("w"), 32)
                for m in range(KD):
                    for h in range(KD):
                        last = nc.tensor.transpose(psW[:, m, h * P:(h + 1) * P], wsb[:, h, m * P:(m + 1) * P], k.ident[:, :])
                last.then_inc(S("wTp"), 1)
                pe.wait_ge(S("wT"), 1)
                for h in range(KD):
                    for m in range(KD):
                        last = nc.tensor.matmul(psA[:, h, :], wT[:, m, h * P:(h + 1) * P], attsb[:, m, :],
                                                start=(m == 0), stop=(m == KD - 1))
                last.then_inc(S("attp"), 1)
                pe.wait_ge(S("wext"), 2)
                pe.sem_inc(S("row_read"), 2)

                def turn(m, u, b):
                    q = (u * BATCH + b) % 2
                    pe.wait_ge(S("normed"), m)
                    pe.sem_inc(S("pause"), 1)
                    for h in range(KD):
                        last = nc.tensor.transpose(psT[q][:, h, :], xn[:, u, b, h * P:(h + 1) * P], k.ident[0:TB, 0:TB])
                    last.then_inc(S("turned"), 1)

                def project(m, u, b):
                    q = (u * BATCH + b) % 2
                    pe.wait_ge(S("xt"), m)
                    pe.wait_ge(S("row_read"), m)
                    for h in range(KD):
                        last = nc.tensor.matmul(psO[q], xt[:, q, h, :], wext[:, h, :], start=(h == 0), stop=(h == KD - 1))
                    last.then_inc(S("product"), 1)

                with pe.Fori(0, NBATCH // 2) as i:
                    for u in range(2):
                        for b in range(BATCH + 1):
                            m = i * (2 * BATCH) + (u * BATCH + b + 1)
                            if b < BATCH:
                                turn(m, u, b)
                            if b > 0:
                                project(m - 1, u, b - 1)

            @block.gpsimd
            def _(pool):
                def gather(i, u):
                    pool.wait_ge(S("sum"), i * 2 + (1 + u))
                    pool.sem_inc(S("pause"), 1)
                    nc.gpsimd.tensor_copy(share[:, u, :, :], k.share[:, bass.ds((i * 2 + u) * BATCH, BATCH), :])
                    nc.gpsimd.tensor_copy(idx[:, u, :, :], k.slots[:, bass.ds((i * 2 + u) * BATCH, BATCH), :]).then_inc(S("idx"), 1)
                    pool.wait_ge(S("idx"), i * 2 + (1 + u))
                    pool.sem_inc(S("pause"), 1)
                    for b in range(BATCH):
                        for j in range(2):
                            nc.gpsimd.indirect_dma_start(
                                g[:, u, b, j, :], None, k.ys,
                                bass.IndirectOffsetOnAxis(ap=idx[:, u, b, j:j + 1].bitcast(U32), axis=0)).then_inc(S(f"g{u}"), 16)

                if layer == 0:
                    nc.gpsimd.memset(k.acc[:, :, :], 0.0).then_inc(S("cleared"), 1)
                else:
                    gather(0, 0)
                    gather(0, 1)
                pool.wait_ge(S("zpad"), 1)
                pool.dma_start(k.edst[N:PADN, :], zpad[:, :]).then_inc(S("pad"), 16)
                pool.wait_ge(S("pad"), 16)
                def split(i, u):
                    n = i * 2 + (1 + u)
                    value = tb[:, u, :, D + H:W]
                    pool.wait_ge(S("row"), n * BATCH)
                    pool.wait_ge(S(f"stored{u}"), i * 32 + 32)
                    pool.sem_inc(S("pause"), 1)
                    for part in range(3):
                        nc.gpsimd.tensor_copy(parts[:, u, :, part, :], value).then_inc(S("parts" if part == 2 else f"part{part}"), 1)
                        if part < 2:
                            pool.wait_ge(S(f"part{part}"), n)
                            pool.sem_inc(S("pause"), 1)
                            nc.gpsimd.tensor_tensor(rest[:, u, :, part, :], value, parts[:, u, :, part, :], ALU.subtract).then_inc(S(f"rest{part}"), 1)
                            pool.wait_ge(S(f"rest{part}"), n)
                            pool.sem_inc(S("pause"), 1)
                            value = rest[:, u, :, part, :]

                with pool.Fori(0, NBATCH // 2 - layer) as i:
                    for u in range(2):
                        if layer == 1:
                            gather(i + 1, u)
                        split(i, u)
                if layer == 1:
                    for u in range(2):
                        split(NBATCH // 2 - 1, u)

            @block.scalar
            def _(act):
                for u in range(2):
                    act.sem_inc(S(f"stored{u}"), 32)
                with act.Fori(0, NBATCH // 2) as i:
                    for u in range(2):
                        root_step(k, t, act, mv[:, u, :, :], i * 2 + (1 + u))
                        act.wait_ge(S(f"stored{u}"), i * 32 + 32)
                        for b in range(BATCH + 1):
                            m = i * (2 * BATCH) + (u * BATCH + b + 1)
                            if b < BATCH:
                                q = (u * BATCH + b) % 2
                                act.wait_ge(S("turned"), m)
                                nc.scalar.copy(xt[:, q, :, :], psT[q]).then_inc(S("xt"), 1)
                            if b > 0:
                                act.wait_ge(S("product"), m - 1)
                                nc.scalar.copy(tb[:, u, b - 1, :], psO[(u * BATCH + b - 1) % 2]).then_inc(S("row"), 1)
                                act.wait_ge(S("row"), m - 1)
                                act.sem_inc(S("row_read"), 1)


def edges(k, layer):
    nc, a, H = k.nc, k.a, HEADS[layer]
    t = f"e{layer}"
    R = H * CH
    DH = D // H
    W = D + H
    S = lambda name: k.sem(f"edge{layer}_{name}")
    with k.phase():
        g = k.sb(t + "g", [P, RING, CH, W])
        idx = k.sb(t + "idx", [P, RING, CH], I32)
        relc = k.sb(t + "relc", [P, RING, CH])
        relrow = k.sb(t + "relrow", [P, RING, CH * P], BF16)
        pen = k.sb(t + "pen", [R, RING, P])
        penr = k.sb(t + "penr", [R, RING, P])
        edw = k.sb(t + "edw", [P, RING, CH, 3 * H], BF16)
        pt = k.sb(t + "pt", [P, CH * P], BF16)
        esrc = k.sb(t + "esrc", [P, R])
        ad = k.sb(t + "ad", [P, R])
        zz = k.sb(t + "zz", [P, 2, R])
        ll = k.sb(t + "ll", [P, 2, R])
        dd = k.sb(t + "dd", [P, R])
        wt = k.sb(t + "wt", [P, RING, R])
        wd = k.sb(t + "wd", [P, RING, R]) if layer == 0 else None
        scan1 = k.sb(t + "scan1", [R, P])
        scan2 = k.sb(t + "scan2", [R, P])
        scan3 = k.sb(t + "scan3", [R, P])
        scan4 = k.sb(t + "scan4", [R, P])
        FLAT = H * (CH + 1)
        cpen = k.sb(t + "cpen", [1, FLAT + 1])
        carry = k.sb(t + "carry", [1, FLAT])
        back = k.sb(t + "back", [1, FLAT])
        brought = k.sb(t + "brought", [1, R])
        later = k.sb(t + "later", [1, R])
        ce = k.sb(t + "ce", [1, 2, H])
        frow = k.sb(t + "frow", [1, 3 * P])
        onehot = k.sb(t + "onehot", [P, NSLOT, P])
        msg = k.sb(t + "msg", [P, NSLOT, D])
        ps = k.ps
        psX, psR, psA, psF = ps[0:R, 4, 0:P], ps[:, 5, 0:R], ps[:, 6, 0:R], ps[:, 7, 0:3]
        psCol, psCol2 = ps[0:R, 4, 256:257], ps[0:R, 4, 258:259]
        psFwd, psBack = ps[0:1, 5, P:P + FLAT], ps[0:1, 5, 320:320 + FLAT]
        flat = lambda ap: ap.rearrange("o (h j) -> o h j", h=H)
        hj = lambda ap: ap.rearrange("p (h j) -> p h j", h=H)
        aggr = [ps[:, q, 0:3 * P].rearrange("p (s n) -> p s n", s=3) for q in range(NSLOT)]

        with nc.Block() as block:
            @block.gpsimd
            def _(pool):
                def gather(c, u, used=True):
                    if used:
                        pool.wait_ge(S("chunk_done"), c - (RING - 1))
                        pool.sem_inc(S("slot_taken"), 1)
                    nc.gpsimd.tensor_copy(idx[:, u, :], k.srcE[:, bass.ds(c * CH, CH)]).then_inc(S("idx"), 1)
                    pool.wait_ge(S("idx"), c + 1)
                    pool.sem_inc(S("idx_seen"), 1)
                    for j in range(CH):
                        nc.gpsimd.indirect_dma_start(
                            g[:, u, j, :], None, k.rows,
                            bass.IndirectOffsetOnAxis(ap=idx[:, u, j:j + 1].bitcast(U32), axis=0),
                        ).then_inc(S(f"gathered{u}"), 16)

                for c in range(RING):
                    gather(c, c, used=False)
                with pool.Fori(0, CHUNKS // RING - 1) as i:
                    for u in range(RING):
                        gather(i * RING + (RING + u), u)

            def gathered(eng, c, i, u):
                eng.wait_ge(S(f"gathered{u}"), i * (16 * CH) + 16 * CH)

            @block.sync
            def _(sp):
                def load(c, i, u, used=True):
                    _, at0 = nc.values_load_multi_w_load_instructions(
                        k.n0[0:1, bass.ds(c * CH, CH)], engines=[ENGINE.SP], min_val=0, max_val=N - 1,
                        skip_runtime_bounds_check_because="destinations are nodes, clamped at zero on the chip")
                    rows = nc.sync.snap(c * CH) if not isinstance(c, int) else c * CH
                    if used:
                        sp.wait_ge(S("weights"), c - (RING - 1))
                        sp.sem_inc(S("loads_free"), 1)
                    sem = S(f"loaded{u}")
                    sp.dma_start(relrow[:, u, :].rearrange("p (o n) -> p o n", o=1),
                                 k.reld[bass.ds(rows, CH), :].rearrange("(o t) e -> o (t e)", o=1).rearrange("(z o) n -> z o n", z=1).to_broadcast([P, 1, CH * P])).then_inc(sem, 16)
                    for h in range(H):
                        sp.dma_start(pen[h * CH:(h + 1) * CH, u, :], k.seg[bass.ds(rows, CH), :]).then_inc(sem, 16)
                        sp.dma_start(penr[h * CH:(h + 1) * CH, u, :], k.segr[bass.ds(rows, CH), :]).then_inc(sem, 16)
                    for j in range(CH):
                        sp.dma_start(edw[:, u, j, :], k.edst[bass.ds(at0[j], P), :]).then_inc(sem, 16)

                for c in range(RING):
                    load(c, 0, c, used=False)
                with sp.Fori(0, CHUNKS // RING - 1) as i:
                    for u in range(RING):
                        load(i * RING + (RING + u), i, u)

            LOADS = 16 * (1 + 2 * H + CH)

            def loaded(eng, i, u):
                eng.wait_ge(S(f"loaded{u}"), i * LOADS + LOADS)

            def act_scores(act, c, i, u):
                n = c + 1

                def first():
                    gathered(act, c, i, u)
                    act.wait_ge(S("zz0"), n)
                    nc.scalar.copy(hj(esrc[:, :]), g[:, u, :, D:W].rearrange("p j h -> p h j")).then_inc(S("esrc"), 1)

                def small():
                    nc.scalar.copy(relc[:, u, :], k.relE[:, bass.ds(c * CH, CH)]).then_inc(S("relc"), 1)
                    nc.scalar.copy(flat(cpen[:, 0:FLAT])[:, :, 1:CH + 1],
                                   k.single_row[0:1, bass.ds(c * CH, CH)].rearrange("o (z j) -> o z j", z=1).to_broadcast([1, H, CH])).then_inc(S("cpen"), 1)

                def expand():
                    act.wait_ge(S("expanded"), n * 4 + 4)
                    act.wait_ge(S("ce"), n * CE - (CE - 1))
                    nc.scalar.copy(hj(ad[:, :]), psA.rearrange("p (j h) -> p h j", h=H)).then_inc(S("ad"), 1)

                def exps():
                    act.wait_ge(S("diff"), n + 1)
                    nc.scalar.activation(wt[:, u, :], dd[:, :], ACT.Exp).then_inc(S("exp"), 1)

                def factor():
                    act.wait_ge(S("ce"), n * CE + 1)
                    ours = ce[:, 1, :].rearrange("o (h z) -> o h z", z=1).to_broadcast([1, H, DH])
                    nc.scalar.activation(frow[:, 0:D].rearrange("o (h d) -> o h d", h=H), ours, ACT.Exp)
                    nc.scalar.activation(frow[:, D:D + H], ce[:, 1, :], ACT.Exp).then_inc(S("frow"), 1)

                return {"first": first, "small": small, "expand": expand, "exps": exps, "factor": factor}

            def pe_scores(pe, c, i, u):
                n = c + 1

                def hold(name, value=None):
                    pe.wait_ge(S(name), n if value is None else value)
                    pe.sem_inc(S("pause"), 1)

                def turn():
                    hold("esrc")
                    nc.tensor.transpose(psX, esrc[:, :], k.ident[:, :]).then_inc(S("esrc_t"), 1)

                def last_row():
                    hold("scan1")
                    nc.tensor.transpose(flat(psFwd)[:, :, 1:CH + 1], scan1[:, P - 1:P], k.ident[0:R, 0:R]).then_inc(S("last_ps"), 1)

                def column():
                    hold("brought")
                    nc.tensor.matmul(psCol, brought[:, :], k.ones[0:1, :], start=True, stop=True).then_inc(S("col"), 1)

                def expand(x):
                    pe.wait_ge(S("pt"), n)
                    for j in range(x * CH // 4, (x + 1) * CH // 4):
                        for part in range(3):
                            last = nc.tensor.matmul(psA[:, j * H:(j + 1) * H], pt[:, j * P:(j + 1) * P], edw[:, u, j, part * H:(part + 1) * H],
                                                    start=(part == 0), stop=(part == 2))
                    last.then_inc(S("expanded"), 1)

                def first_row():
                    hold("scan3")
                    nc.tensor.transpose(flat(psBack)[:, :, 0:CH], scan3[:, 0:1], k.ident[0:R, 0:R]).then_inc(S("first_ps"), 1)

                def column2():
                    hold("later")
                    nc.tensor.matmul(psCol2, later[:, :], k.ones[0:1, :], start=True, stop=True).then_inc(S("col2"), 1)

                def running():
                    hold("scan4")
                    nc.tensor.transpose(psR, scan4[:, :], k.ident[0:R, 0:R]).then_inc(S("max_ps"), 1)

                def factor():
                    pe.wait_ge(S("frow"), n + 1)
                    for s in range(3):
                        last = nc.tensor.matmul(psF[:, s:s + 1], frow[:, s * P:(s + 1) * P], k.ones[0:1, :], start=True, stop=True)
                    last.then_inc(S("fac_ps"), 1)

                return {"turn": turn, "last_row": last_row, "column": column, "expand0": lambda: expand(0), "expand1": lambda: expand(1),
                        "expand2": lambda: expand(2), "expand3": lambda: expand(3), "first_row": first_row,
                        "column2": column2, "running": running, "factor": factor}

            CE = 5

            def dve_scores(dve, c, i, u):
                n = c + 1
                scan = nc.vector.tensor_tensor_scan

                def one_hot():
                    loaded(dve, i, u)
                    dve.wait_ge(S("expanded"), n * 4)
                    dve.sem_inc(S("pause"), 1)
                    nc.vector.tensor_scalar(pt[:, :], relrow[:, u, :], k.part[:, :], None, ALU.is_equal).then_inc(S("pt"), 1)

                def scan_1():
                    loaded(dve, i, u)
                    dve.wait_ge(S("esrc_t"), n)
                    scan(scan1[:, :], pen[:, u, :], psX, -BIG, ALU.add, ALU.max).then_inc(S("scan1"), 1)

                def carries():
                    dve.wait_ge(S("last_ps"), n)
                    dve.wait_ge(S("cpen"), n)
                    dve.wait_ge(S("carried"), n)
                    scan(carry[:, :], cpen[:, 0:FLAT], psFwd, -BIG, ALU.add, ALU.max).then_inc(S("carry"), 1)

                def bring():
                    dve.wait_ge(S("carry"), n)
                    nc.vector.tensor_copy(hj(brought[:, :]), flat(carry[:, :])[:, :, 0:CH]).then_inc(S("brought"), 1)

                def carry_on():
                    nc.vector.tensor_copy(flat(psFwd)[:, :, 0:1], flat(carry[:, :])[:, :, CH:CH + 1]).then_inc(S("carried"), 1)

                def scan_2():
                    dve.wait_ge(S("col"), n)
                    scan(scan2[:, :], pen[:, u, :], psX, psCol, ALU.add, ALU.max).then_inc(S("scan2"), 1)

                def scan_3():
                    dve.wait_ge(S("scan2"), n)
                    scan(scan3[:, ::-1], penr[:, u, ::-1], scan2[:, ::-1], -BIG, ALU.add, ALU.max).then_inc(S("scan3"), 1)

                def backward():
                    dve.wait_ge(S("first_ps"), n)
                    scan(back[:, ::-1], cpen[:, FLAT:0:-1], psBack[:, ::-1], -BIG, ALU.add, ALU.max).then_inc(S("back"), 1)

                def meet():
                    dve.wait_ge(S("back"), n)
                    nc.vector.tensor_copy(hj(later[:, :]), flat(back[:, :])[:, :, 1:CH + 1]).then_inc(S("later"), 1)

                def scan_4():
                    dve.wait_ge(S("col2"), n)
                    scan(scan4[:, ::-1], penr[:, u, ::-1], scan2[:, ::-1], psCol2, ALU.add, ALU.max).then_inc(S("scan4"), 1)

                def sum_0():
                    dve.wait_ge(S("ad"), n)
                    nc.vector.tensor_tensor(zz[:, 0, :], esrc[:, :], ad[:, :], ALU.add).then_inc(S("zz0"), 1)

                def leaky_0():
                    dve.wait_ge(S("zz0"), n + 1)
                    nc.vector.scalar_tensor_tensor(ll[:, 0, :], zz[:, 0, :], SLOPE, zz[:, 0, :], ALU.mult, ALU.max).then_inc(S("ll0"), 1)

                def sum_1():
                    dve.wait_ge(S("max_ps"), n)
                    nc.vector.tensor_tensor(zz[:, 1, :], psR, ad[:, :], ALU.add).then_inc(S("zz1"), 1)

                def leaky_1():
                    dve.wait_ge(S("zz1"), n)
                    nc.vector.scalar_tensor_tensor(ll[:, 1, :], zz[:, 1, :], SLOPE, zz[:, 1, :], ALU.mult, ALU.max).then_inc(S("ll1"), 1)

                def diff():
                    dve.wait_ge(S("ll0"), n)
                    dve.wait_ge(S("ll1"), n)
                    dve.wait_ge(S("exp"), n)
                    nc.vector.tensor_tensor(dd[:, :], ll[:, 0, :], ll[:, 1, :], ALU.subtract).then_inc(S("diff"), 1)

                def weights():
                    dve.wait_ge(S("exp"), n + 1)
                    if layer == 0:
                        dist = k.distE[:, bass.ds(c * CH, CH)].rearrange("p (z j) -> p z j", z=1).to_broadcast([P, H, CH])
                        nc.vector.tensor_tensor(hj(wd[:, u, :]), hj(wt[:, u, :]), dist, ALU.mult).then_inc(S("weights"), 1)
                    else:
                        dve.sem_inc(S("weights"), 1)

                def ce_step(m, ins):
                    ins.then_inc(S("ce"), 1)

                def ce_1():
                    dve.wait_ge(S("brought"), n)
                    dve.wait_ge(S("frow"), n)
                    first = k.first_row[0:1, bass.ds(c * CH, 1)].to_broadcast([1, H])
                    ce_step(1, nc.vector.tensor_tensor(ce[:, 0, :], hj(brought[:, :])[:, :, 0], first, ALU.add))

                def ce_2():
                    dve.wait_ge(S("ce"), n * CE - (CE - 2))
                    ce_step(2, nc.vector.tensor_tensor(ce[:, 1, :], ce[:, 0, :], hj(ad[0:1, :])[:, :, 0], ALU.add))

                def ce_3():
                    dve.wait_ge(S("ce"), n * CE - (CE - 3))
                    ce_step(3, nc.vector.scalar_tensor_tensor(ce[:, 0, :], ce[:, 1, :], SLOPE, ce[:, 1, :], ALU.mult, ALU.max))

                def ce_4():
                    dve.wait_ge(S("ce"), n * CE - (CE - 4))
                    ce_step(4, nc.vector.tensor_tensor(ce[:, 0, :], ce[:, 0, :], hj(ll[0:1, 1, :])[:, :, 0], ALU.subtract))

                def ce_5():
                    dve.wait_ge(S("ce"), n * CE - (CE - 5))
                    ce_step(5, nc.vector.tensor_scalar(ce[:, 1, :], ce[:, 0, :], -200.0, None, ALU.max))

                return dict(one_hot=one_hot, scan_1=scan_1, carries=carries, bring=bring, carry_on=carry_on, scan_2=scan_2, scan_3=scan_3,
                            backward=backward, meet=meet, scan_4=scan_4, sum_0=sum_0, leaky_0=leaky_0, sum_1=sum_1,
                            leaky_1=leaky_1, diff=diff, weights=weights, ce_1=ce_1, ce_2=ce_2, ce_3=ce_3, ce_4=ce_4, ce_5=ce_5)

            BY_ACT = ACT_TILES[layer]
            BY_DVE = [j for j in range(CH) if j not in BY_ACT]

            def weight(u, j):
                return hj((wd if layer == 0 else wt)[:, u, :])[:, :, j:j + 1]

            def onehot_of(dve, c, u, j):
                dve.wait_ge(S("summed"), c * CH + (j + 1))
                nc.vector.tensor_scalar(onehot[:, j % NSLOT, :], k.iota_b[:, :], relc[:, u, j:j + 1], None, ALU.is_equal).then_inc(S("onehot"), 1)

            def message_of(dve, c, u, j):
                nc.vector.tensor_tensor(msg[:, j % NSLOT, :].rearrange("p (h d) -> p h d", h=H), g[:, u, j, 0:D].rearrange("p (h d) -> p h d", h=H),
                                        weight(u, j).to_broadcast([P, H, DH]), ALU.mult).then_inc(S("msg_dve"), 1)

            def operands(dve, c, i, u, j):
                if j == 0:
                    dve.wait_ge(S("relc"), c + 1)
                onehot_of(dve, c, u, j)
                if j in BY_DVE:
                    if j == BY_DVE[0]:
                        dve.wait_ge(S("weights"), c + 1)
                        gathered(dve, c, i, u)
                    message_of(dve, c, u, j)

            def dve_tile(dve, c, i, u, j, at0, after):
                n = c * CH + (j + 1)
                window = k.acc[:, :, bass.ds(at0[j], P)]
                if j == 0:
                    dve.wait_ge(S("fac_ps"), c + 1)
                    dve.wait_ge(S("added"), n + (NSLOT - 1))
                    first = k.acc[:, :, bass.ds(at0[0], 1)]
                    nc.vector.tensor_tensor(first, first, psF.rearrange("p (s o) -> p s o", o=1), ALU.mult).then_inc(S("rescaled"), 1)
                    dve.wait_ge(S("rescaled"), c + 1)
                dve.wait_ge(S("summed"), n + NSLOT)
                dve.wait_ge(S("added"), n + (NSLOT - 1))
                nc.vector.tensor_tensor(window, window, aggr[j % NSLOT], ALU.add).then_inc(S("added"), 1)
                if j + AHEAD < CH:
                    operands(dve, c, i, u, j + AHEAD)
                elif after:
                    operands(dve, *after, j + AHEAD - CH)

            def act_tile(act, c, i, u, j):
                if j == BY_ACT[0]:
                    act.wait_ge(S("weights"), c + 1)
                    gathered(act, c, i, u)
                act.wait_ge(S("summed"), c * CH + (j + 1))
                for h in range(H):
                    last = nc.scalar.activation(msg[:, j % NSLOT, h * DH:(h + 1) * DH], g[:, u, j, h * DH:(h + 1) * DH], ACT.Copy,
                                                scale=weight(u, j)[:, h, :])
                last.then_inc(S("msg_act"), 1)

            def pe_tile(pe, c, i, u, j):
                n = c * CH + (j + 1)
                q = j % NSLOT
                pe.wait_ge(S("added"), n)
                pe.wait_ge(S("onehot"), n)
                mine = BY_ACT if j in BY_ACT else BY_DVE
                pe.wait_ge(S("msg_act" if j in BY_ACT else "msg_dve"), c * len(mine) + (mine.index(j) + 1))
                for s in range(KD):
                    nc.tensor.matmul(aggr[q][:, s, :], msg[:, q, s * P:(s + 1) * P], onehot[:, q, :], start=True, stop=True)
                nc.tensor.matmul(aggr[q][0:H, KD, :], hj(wt[:, u, :])[:, :, j], onehot[:, q, :], start=True, stop=True).then_inc(S("summed"), 1)

            SCORE_AT = SCHEDULE[layer]

            def scores_after(engine, scores, following, second, j):
                table = SCORE_AT[engine]
                if following and j in table:
                    for name in table[j]:
                        scores(*following)[name]()
                if second and j - CH in table:
                    for name in table[j - CH]:
                        scores(*second)[name]()

            def scores_before(engine, scores):
                for j in range(-CH, CH):
                    scores_after(engine, scores, (0, 0, 0), None, j)
                for j in range(CH):
                    scores_after(engine, scores, None, (1, 0, 1), j)

            def all_turns(eng, turn):
                def place(i, u):
                    return i * RING + u, (i + 1 if u >= RING else i) if not isinstance(i, int) else i + u // RING, u % RING

                with eng.Fori(0, CHUNKS // RING - 1) as i:
                    for u in range(RING):
                        turn(place(i, u), place(i, u + 1), place(i, u + 2))
                i = CHUNKS // RING - 1
                for u in range(RING):
                    turn(place(i, u), place(i, u + 1) if u + 1 < RING else None, place(i, u + 2) if u + 2 < RING else None)

            @block.vector
            def _(dve):
                for q in range(NSLOT):
                    nc.vector.memset(ps[:, q, :], 0.0).then_inc(S("added"), 1)
                nc.vector.memset(cpen[:, :], -BIG).then_inc(S("carry_init"), 1)
                nc.vector.memset(psFwd, -BIG).then_inc(S("carry_init"), 1)
                nc.vector.memset(psBack, -BIG).then_inc(S("carry_init"), 1)
                nc.vector.memset(frow[:, :], 1.0).then_inc(S("carry_init"), 1)
                dve.wait_ge(S("carry_init"), 4)
                for name in ("diff", "zz0", "carried", "ce"):
                    dve.sem_inc(S(name), 1)
                scores_before("dve", lambda *x: dve_scores(dve, *x))

                for j in range(AHEAD):
                    operands(dve, 0, 0, 0, j)

                def turn(this, following, second):
                    c, i, u = this
                    _, at0 = nc.values_load_multi_w_load_instructions(
                        k.n0[0:1, bass.ds(c * CH, CH)], engines=[ENGINE.DVE], min_val=0, max_val=N - 1,
                        skip_runtime_bounds_check_because="destinations are nodes, clamped at zero on the chip")
                    for j in range(CH):
                        dve_tile(dve, c, i, u, j, at0, following)
                        scores_after("dve", lambda *x: dve_scores(dve, *x), following, second, j)
                    dve.wait_ge(S("added"), c * CH + (CH + NSLOT))
                    dve.sem_inc(S("chunk_done"), 1)

                all_turns(dve, turn)

            @block.tensor
            def _(pe):
                pe.sem_inc(S("summed"), NSLOT)
                pe.sem_inc(S("expanded"), 4)
                pe.wait_ge(S("carry_init"), 4)
                scores_before("pe", lambda *x: pe_scores(pe, *x))

                def turn(this, following, second):
                    for j in range(CH):
                        pe_tile(pe, *this, j)
                        scores_after("pe", lambda *x: pe_scores(pe, *x), following, second, j)

                all_turns(pe, turn)

            @block.scalar
            def _(act):
                act.sem_inc(S("exp"), 1)
                act.sem_inc(S("frow"), 1)
                act.wait_ge(S("carry_init"), 4)
                scores_before("act", lambda *x: act_scores(act, *x))

                def turn(this, following, second):
                    for j in range(CH):
                        if j in BY_ACT:
                            act_tile(act, *this, j)
                        scores_after("act", lambda *x: act_scores(act, *x), following, second, j)

                all_turns(act, turn)


def nodes(k, layer, xin, xout):
    nc, a, H = k.nc, k.a, HEADS[layer]
    t = f"n{layer}"
    S = lambda name: k.sem(f"{t}_{name}")
    with k.phase():
        xb = k.sb(t + "x", [TB, 2, BATCH, D])
        rden = k.sb(t + "rden", [H, 2, ROWS])
        spread = k.sb(t + "spread", [H, KD, P])
        onT = k.sb(t + "onT", [P, 2, KD, TB])
        x1 = k.sb(t + "x1", [TB, 2, BATCH, D])
        y = k.sb(t + "y", [TB, 2, BATCH, D])
        yt = k.sb(t + "yt", [P, 2, KD, ROWS])
        st = k.sb(t + "st", [TB, 2, BATCH, 6])
        mv = k.sb(t + "mv", [TB, 2, BATCH, 2])
        if layer == 0:
            st2 = k.sb(t + "st2", [TB, 2, BATCH, 6])
            mv2 = k.sb(t + "mv2", [TB, 2, BATCH, 2])
            gamma = k.sb(t + "gamma", [P, KD])
            beta = k.sb(t + "beta", [P, KD])
            wr = k.sb(t + "wr", [P, KD, E])
            y1 = k.sb(t + "y1", [TB, BATCH, D])
            br = k.sb(t + "br", [TB, 1, E])
            before = k.sb(t + "before", [TB, TB])
            all_ones = k.sb(t + "ones", [TB, TB])
            logits = k.sb(t + "logits", [TB, 2, BATCH, E])
            top = k.sb(t + "top", [TB, BATCH, E])
            topi = k.sb(t + "topi", [TB, BATCH, E], U32)
            idxf = k.sb(t + "idxf", [TB, BATCH, 2])
            hit = k.sb(t + "hit", [TB, 2, BATCH, E])
            both = k.sb(t + "both", [TB, BATCH + 1, E])
            slot = k.sb(t + "slot", [TB, BATCH, E])
            picked = k.sb(t + "picked", [TB, 2, BATCH, E])
            slotf = k.sb(t + "slotf", [TB, BATCH, 2])
            rows = k.sb(t + "rows", [TB, 2, BATCH, 2], I32)
        else:
            neg = k.sb(t + "neg", [TB, 2, D])
            ex = k.sb(t + "ex", [TB, 2, D])
        ps = k.ps
        psB = [ps[:, q, 0:KD * TB].rearrange("p (h n) -> p h n", h=KD) for q in range(2)]
        psX = [ps[0:TB, 2 + q, 0:D] for q in range(2)]
        psY = [ps[:, 4 + q, 0:KD * TB].rearrange("p (h n) -> p h n", h=KD) for q in range(2)]
        psL = [ps[0:TB, 6 + u, 0:BATCH * E].rearrange("p (b e) -> p b e", b=BATCH) for u in range(2)]
        psC = [ps[0:TB, 6 + u, 128:128 + (BATCH + 1) * E].rearrange("p (b e) -> p b e", e=E) for u in range(2)]
        consts = [(spread[:, :, :], a[f"spread{layer}"])]
        if layer == 0:
            consts += [(gamma[:, :], a["L0_ffn_gamma"].rearrange("o (h p) -> p (o h)", p=P)),
                       (beta[:, :], a["L0_ffn_beta"].rearrange("o (h p) -> p (o h)", p=P)),
                       (wr[:, :, :], a["L0_ffn_Wr"].rearrange("(h p) e -> p h e", p=P)),
                       (br[:, 0, :], a["L0_ffn_br"].to_broadcast([TB, E])), (before[:, :], a["before"]),
                       (k.iota8[:, :], a["iota"][0:TB, 0:E])]
        ready = 16 * len(consts)
        place = lambda u, b: (u * BATCH + b) % 2
        SENT = 16 * BATCH * 2
        block_number = lambda i, u, b: i * (2 * BATCH) + (u * BATCH + b + 1)
        with nc.Block() as block:
            @block.sync
            def _(sp):
                with nc.allow_non_contiguous_dma("256 words of each, once"):
                    for dst, src in consts:
                        sp.dma_start(dst, src).then_inc(S("consts"), 16)

                def load(row, u):
                    sp.dma_start(xb[:, u, :, :], rows_of(xin, row)).then_inc(S(f"x{u}"), 16)

                def keep(row, n, u):
                    sp.wait_ge(S("sum"), n * BATCH)
                    sp.dma_start(rows_of(xout, row), x1[:, u, :, :]).then_inc(S(f"xs{u}"), 16)

                def store(row, n, u):
                    if layer == 0:
                        return
                    sp.wait_ge(S("y"), n * BATCH)
                    sp.dma_start(rows_of(k.y3, row), y[:, u, :, :]).then_inc(S(f"ys{u}"), 16)

                for u in range(2):
                    load(u * ROWS, u)
                if layer == 0:
                    for e in range(E):
                        sp.dma_start(k.w1[:, e, :, :], a["L0_ffn_W1"][e].rearrange("(h p) n -> p h n", p=P)).then_inc(S("w"), 16)
                        sp.dma_start(k.w2[:, e, :, :], a["L0_ffn_W2"][e].rearrange("(c p) n -> p c n", p=P)).then_inc(S("w"), 16)
                with sp.Fori(0, NBATCH // 2 - 1) as i:
                    for u in range(2):
                        row = i * (2 * ROWS) + u * ROWS
                        keep(row, i * 2 + (1 + u), u)
                        load(row + 2 * ROWS, u)
                        store(row, i * 2 + (1 + u), u)
                for u in range(2):
                    keep((NBATCH - 2 + u) * ROWS, NBATCH - 1 + u, u)
                    store((NBATCH - 2 + u) * ROWS, NBATCH - 1 + u, u)
                for u in range(2):
                    sp.wait_ge(S(f"xs{u}"), 16 * (1 + NBATCH // 2))
                    if layer == 1:
                        sp.wait_ge(S(f"ys{u}"), 16 * (1 + NBATCH // 2))
                if layer == 0:
                    sp.wait_ge(S("w"), 32 * E)

            def turns(eng, turn, first):
                first(0, 0)
                turn(0, 0, (0, 1), None)
                with eng.Fori(0, NBATCH // 2 - 1) as i:
                    turn(i, 1, (i + 1, 0), (i, 0))
                    turn(i + 1, 0, (i + 1, 1), (i, 1))
                turn(NBATCH // 2 - 1, 1, None, (NBATCH // 2 - 1, 0))

            LAST = (NBATCH // 2 - 1, 1)

            @block.scalar
            def _(act):
                act.wait_ge(S("consts"), ready)

                def exps(i, u):
                    if layer == 1:
                        for b in range(BATCH):
                            act.wait_ge(S("neg"), block_number(i, u, b))
                            nc.scalar.activation(ex[:, place(u, b), :], neg[:, place(u, b), :], ACT.Exp).then_inc(S("ex"), 1)

                def turn(i, u, following, previous):
                    n = i * 2 + (1 + u)
                    root_step(k, t, act, mv[:, u, :, :], n)
                    if following:
                        exps(*following)
                    if layer == 0:
                        root_step(k, t + "b", act, mv2[:, u, :, :], n)
                    if layer == 1:
                        act.wait_ge(S("placed"), n)
                    for b in range(BATCH):
                        act.wait_ge(S("yt_ps"), block_number(i, u, b))
                        for h in range(KD):
                            dst, src = yt[:, u, h, b * TB:(b + 1) * TB], psY[place(u, b)][:, h, :]
                            if layer == 0:
                                last = nc.scalar.activation(dst, src, ACT.Identity, bias=beta[:, h:h + 1], scale=gamma[:, h:h + 1])
                            else:
                                last = nc.scalar.copy(dst, src)
                        last.then_inc(S("yt"), 1)
                    if layer == 0:
                        act.wait_ge(S("logit_ps"), n)
                        nc.scalar.copy(logits[:, u, :, :], psL[u]).then_inc(S("logit"), 1)

                turns(act, turn, exps)

            @block.gpsimd
            def _(pool):
                if layer == 0:
                    nc.gpsimd.memset(k.zero[:, :, :], 0.0)
                    with pool.Fori(0, NBATCH // 2) as i:
                        for u in range(2):
                            pool.wait_ge(S("rows"), i * 2 + (1 + u))
                            pool.sem_inc(S("pause"), 1)
                            for b in range(BATCH):
                                for j in range(2):
                                    nc.gpsimd.indirect_dma_start(
                                        k.xs, bass.IndirectOffsetOnAxis(ap=rows[:, u, b, j:j + 1].bitcast(U32), axis=0),
                                        y[:, u, b, :], None).then_inc(S("sent"), 16)
                            pool.wait_ge(S("sent"), (i * 2 + (1 + u)) * SENT)
                            pool.sem_inc(S("y_sent"), 1)
                    return
                pool.sem_inc(S("placed"), 2)
                nc.gpsimd.memset(k.ysum[:, :], 0.0).then_inc(S("ysum"), 1)
                with pool.Fori(0, NBATCH // 2) as i:
                    for u in range(2):
                        n, row = i * 2 + (1 + u), i * (2 * ROWS) + u * ROWS
                        for b in range(BATCH):
                            pool.wait_ge(S("y"), block_number(i, u, b))
                            pool.wait_ge(S("ysum"), block_number(i, u, b))
                            nc.gpsimd.tensor_tensor(k.ysum[:, :], k.ysum[:, :], y[:, u, b, :], ALU.add).then_inc(S("ysum"), 1)
                        pool.wait_ge(S("yt"), n * BATCH)
                        pool.sem_inc(S("yt_seen"), 1)
                        nc.gpsimd.tensor_copy(k.acc[:, 0:KD, bass.ds(row, ROWS)], yt[:, u, :, :]).then_inc(S("placed"), 1)

            @block.tensor
            def _(pe):
                pe.wait_ge(S("consts"), ready)

                def divide(i, u, b):
                    for h in range(KD):
                        last = nc.tensor.matmul(psB[place(u, b)][:, h, :], spread[:, h, :], rden[:, u, b * TB:(b + 1) * TB], start=True, stop=True)
                    last.then_inc(S("spread"), 1)

                def message(i, u, b):
                    pe.wait_ge(S("onT"), block_number(i, u, b))
                    pe.sem_inc(S("pause"), 1)
                    for h in range(KD):
                        last = nc.tensor.transpose(psX[place(u, b)][:, h * P:(h + 1) * P], onT[:, place(u, b), h, :], k.ident[:, :])
                    last.then_inc(S("msg"), 1)

                def messages(i, u):
                    pe.wait_ge(S("rden"), i * 2 + (1 + u))
                    divide(i, u, 0)
                    divide(i, u, 1)
                    for b in range(BATCH):
                        message(i, u, b)
                        if b + 2 < BATCH:
                            divide(i, u, b + 2)

                def turn(i, u, following, previous):
                    if following:
                        messages(*following)
                    if layer == 0 and previous:
                        count(*previous)
                    for b in range(BATCH):
                        pe.wait_ge(S("y"), block_number(i, u, b))
                        if b >= 2:
                            pe.wait_ge(S("yt"), block_number(i, u, b - 2))
                        pe.sem_inc(S("pause"), 1)
                        for h in range(KD):
                            last = nc.tensor.transpose(psY[place(u, b)][:, h, :], y[:, u, b, h * P:(h + 1) * P], k.ident[0:TB, 0:TB])
                        last.then_inc(S("yt_ps"), 1)
                    pe.wait_ge(S("yt"), (i * 2 + (1 + u)) * BATCH)
                    if layer == 0:
                        for b in range(BATCH):
                            for h in range(KD):
                                last = nc.tensor.matmul(psL[u][:, b, :], yt[:, u, h, b * TB:(b + 1) * TB], wr[:, h, :], start=(h == 0), stop=(h == KD - 1))
                        last.then_inc(S("logit_ps"), 1)

                def count(i, u):
                    pe.wait_ge(S("both"), i * 2 + (1 + u))
                    nc.tensor.matmul(psC[u], before[:, :], both[:, :, :], start=True, stop=False)
                    for b in range(BATCH):
                        later = both[:, b:b + 1, :].to_broadcast([TB, BATCH - b, E])
                        last = nc.tensor.matmul(psC[u][:, b + 1:, :], all_ones[:, :], later, start=False, stop=(b == BATCH - 1))
                    last.then_inc(S("counted"), 1)

                turns(pe, turn, messages)
                if layer == 0:
                    count(*LAST)

            @block.vector
            def _(dve):
                dve.wait_ge(S("consts"), ready)
                for u in range(2):
                    dve.sem_inc(S(f"xs{u}"), 16)
                    dve.sem_inc(S(f"ys{u}"), 16)
                if layer == 0:
                    dve.sem_inc(S("y_sent"), 2)
                    nc.vector.memset(all_ones[:, :], 1.0)
                    nc.vector.memset(both[:, :, :], 0.0)
                    nc.vector.tensor_scalar(k.run[:, 0, :], k.iota8[:, :], float(REGION), None, ALU.mult).then_inc(S("run"), 1)
                    dve.wait_ge(S("run"), 1)

                def divide(i, u, b):
                    row = i * (2 * ROWS) + (u * BATCH + b) * TB
                    dve.wait_ge(S("spread"), block_number(i, u, b))
                    nc.vector.tensor_tensor(onT[:, place(u, b), :, :], k.acc[:, 0:KD, bass.ds(row, TB)], psB[place(u, b)], ALU.mult).then_inc(S("onT"), 1)

                def add(i, u, b):
                    q, m = place(u, b), block_number(i, u, b)
                    dve.wait_ge(S("msg"), m)
                    if layer == 0:
                        nc.vector.tensor_tensor(x1[:, u, b, :], xb[:, u, b, :], psX[q], ALU.add).then_inc(S("sum"), 1)
                    else:
                        nc.vector.tensor_scalar(neg[:, q, :], psX[q], 0.0, None, ALU.min).then_inc(S("neg"), 1)
                        nc.vector.scalar_tensor_tensor(x1[:, u, b, :], psX[q], 0.0, xb[:, u, b, :], ALU.max, ALU.add).then_inc(S("pos"), 1)

                def add_exp(i, u, b):
                    q, m = place(u, b), block_number(i, u, b)
                    dve.wait_ge(S("pos"), m)
                    dve.wait_ge(S("ex"), m)
                    nc.vector.scalar_tensor_tensor(x1[:, u, b, :], ex[:, q, :], -1.0, x1[:, u, b, :], ALU.add, ALU.add).then_inc(S("sum"), 1)

                def invert(i, u):
                    row = i * (2 * ROWS) + u * ROWS
                    nc.vector.reciprocal(rden[:, u, :], k.acc[0:H, KD, bass.ds(row, ROWS)]).then_inc(S("rden"), 1)

                def first_add(i, u):
                    dve.wait_ge(S(f"x{u}"), i * 16 + 16)
                    dve.wait_ge(S(f"xs{u}"), i * 16 + 16)
                    add(i, u, 0)

                def message_steps(i, u):
                    steps = [[lambda: invert(i, u)], [lambda: divide(i, u, 0), lambda: divide(i, u, 1)]]
                    for b in range(BATCH):
                        group = [lambda b=b: add(i, u, b) if b else first_add(i, u)]
                        if b + 2 < BATCH:
                            group.append(lambda b=b: divide(i, u, b + 2))
                        if layer == 1 and b:
                            group.append(lambda b=b: add_exp(i, u, b - 1))
                        steps.append(group)
                    if layer == 1:
                        steps.append([lambda: add_exp(i, u, BATCH - 1)])
                    return steps

                def messages(i, u):
                    for group in message_steps(i, u):
                        for step in group:
                            step()

                def turn(i, u, following, previous):
                    n = i * 2 + (1 + u)
                    dve.wait_ge(S("sum"), n * BATCH)
                    between = message_steps(*following) if following else []
                    routing = route_steps(*previous) if layer == 0 and previous else []

                    def route(count):
                        for step in routing[:count]:
                            step()
                        del routing[:count]

                    def other(count=1):
                        for group in between[:count]:
                            for step in group:
                                step()
                        del between[:count]

                    first = (t, x1[:, u, :, :], st[:, u, :, :], mv[:, u, :, :], y1[:, :, :] if layer == 0 else y[:, u, :, :])
                    norm_stats(k, dve, *first, n)
                    other()
                    norm_var(k, dve, *first, n)
                    other(1 + layer)
                    norm_root(k, dve, *first, n)
                    other()
                    if layer == 1:
                        dve.wait_ge(S(f"ys{u}"), i * 16 + 16)
                        dve.wait_ge(S("placed"), n)
                        norm_rows(k, dve, *first, n, S("y"), other)
                    else:
                        norm_rows(k, dve, *first, n, S("y1"))
                        route(1)
                        other()
                        route(1)
                        dve.wait_ge(S("y1"), n * BATCH)
                        second = (t + "b", y1[:, :, :], st2[:, u, :, :], mv2[:, u, :, :], y[:, u, :, :])
                        norm_stats(k, dve, *second, n)
                        route(1)
                        other()
                        route(1)
                        norm_var(k, dve, *second, n)
                        route(1)
                        other()
                        route(1)
                        other()
                        norm_root(k, dve, *second, n)
                        dve.wait_ge(S("y_sent"), n)
                        norm_rows(k, dve, *second, n, S("y"), lambda: route(1))
                        route(len(routing))
                    other(len(between))

                def route_steps(i, u):
                    n = i * 2 + (1 + u)
                    mine = lambda ap: ap[:, bass.ds((i * 2 + u) * BATCH, BATCH), :]
                    each = k.iota8[:, :].rearrange("p (z e) -> p z e", z=1).to_broadcast([TB, BATCH, E])

                    def bias():
                        dve.wait_ge(S("logit"), n)
                        nc.vector.tensor_tensor(logits[:, u, :, :], logits[:, u, :, :], br[:, :, :].to_broadcast([TB, BATCH, E]), ALU.add).then_inc(S("biased"), 1)

                    def largest():
                        dve.wait_ge(S("biased"), n)
                        dve.sem_inc(S("pause"), 1)
                        for b in range(BATCH):
                            last = nc.vector.max(top[:, b, :], logits[:, u, b, :])
                        last.then_inc(S("top"), 1)

                    def where():
                        dve.wait_ge(S("top"), n)
                        dve.sem_inc(S("pause"), 1)
                        for b in range(BATCH):
                            last = nc.vector.max_index(topi[:, b, :], top[:, b, :], logits[:, u, b, :])
                        last.then_inc(S("topi"), 1)
                        nc.vector.tensor_copy(mine(k.best), top[:, :, 0:2])

                    def to_float():
                        dve.wait_ge(S("topi"), n)
                        nc.vector.tensor_copy(idxf[:, :, :], topi[:, :, 0:2]).then_inc(S("idxf"), 1)
                        nc.vector.tensor_copy(mine(k.chosen), topi[:, :, 0:2])

                    def hits():
                        dve.wait_ge(S("idxf"), n)
                        dve.sem_inc(S("pause"), 1)
                        for j in range(2):
                            last = nc.vector.tensor_tensor(hit[:, j, :, :], each, idxf[:, :, j:j + 1].to_broadcast([TB, BATCH, E]), ALU.is_equal)
                        last.then_inc(S("hits"), 1)

                    def together():
                        dve.wait_ge(S("hits"), n)
                        nc.vector.tensor_tensor(both[:, 0:BATCH, :], hit[:, 0, :, :], hit[:, 1, :, :], ALU.add).then_inc(S("both"), 1)

                    def slots():
                        dve.wait_ge(S("counted"), n)
                        nc.vector.tensor_tensor(slot[:, :, :], psC[u][:, 0:BATCH, :], k.run[:, :, :].to_broadcast([TB, BATCH, E]), ALU.add).then_inc(S("slot"), 1)

                    def pick():
                        dve.wait_ge(S("slot"), n)
                        dve.sem_inc(S("pause"), 1)
                        for j in range(2):
                            last = nc.vector.tensor_tensor(picked[:, j, :, :], hit[:, j, :, :], slot[:, :, :], ALU.mult)
                        last.then_inc(S("picked"), 1)
                        nc.vector.tensor_tensor(k.run[:, :, :], psC[u][:, BATCH:BATCH + 1, :], k.run[:, :, :], ALU.add).then_inc(S("run"), 1)

                    def reduce():
                        dve.wait_ge(S("picked"), n)
                        dve.sem_inc(S("pause"), 1)
                        for j in range(2):
                            last = nc.vector.tensor_reduce(slotf[:, :, j], picked[:, j, :, :], AX.X, ALU.add)
                        last.then_inc(S("slotf"), 1)

                    def publish():
                        dve.wait_ge(S("slotf"), n)
                        dve.wait_ge(S("run"), n + 1)
                        dve.sem_inc(S("pause"), 1)
                        nc.vector.tensor_copy(rows[:, u, :, :], slotf[:, :, :]).then_inc(S("rows"), 1)
                        nc.vector.tensor_copy(mine(k.sent), slotf[:, :, :])

                    return [bias, largest, where, to_float, hits, together, slots, pick, reduce, publish]

                turns(dve, turn, messages)
                if layer == 0:
                    for step in route_steps(*LAST):
                        step()


def ffn0(k):
    with k.phase():
        k.expert = k.sb("f0expert", [1, NT], I32)
        k.tile_row = k.sb("f0tile_row", [1, NT], I32)
        with k.phase():
            k.stage(route)
        with k.phase():
            k.stage(experts)


def route(k):
    nc, a = k.nc, k.a
    S = lambda name: k.sem(f"rt_{name}")
    ones8 = k.sb("rt_ones8", [TB, E])
    gap = k.sb("rt_gap", [TB, NB, 1])
    e2 = k.sb("rt_e2", [TB, NB, 1])
    den = k.sb("rt_den", [TB, NB, 1])
    hit = k.sb("rt_hit", [TB, NB, E])
    end = k.sb("rt_end", [1, E], I32)
    region = k.sb("rt_region", [TB, E])
    count = k.sb("rt_count", [TB, E, 1])
    start = k.sb("rt_start", [TB, MOST])
    begun = k.sb("rt_begun", [TB, E, MOST])
    tiles = k.sb("rt_tiles", [TB, E])
    tiles_upto = k.sb("rt_tiles_upto", [TB, E])
    tiles_before = k.sb("rt_tiles_before", [TB, 1, E])
    last_tile = k.sb("rt_last_tile", [TB, 1, E])
    shift = k.sb("rt_shift", [TB, 1, E])
    moved = k.sb("rt_moved", [TB, NB, 2])
    past = k.sb("rt_past", [1, NT, E - 1])
    expertf = k.sb("rt_expertf", [1, NT, 1])
    own = k.sb("rt_own", [1, NT, E])
    part = k.sb("rt_part", [1, NT, E])
    local = k.sb("rt_local", [1, NT, 1])
    limit = k.sb("rt_limit", [1, NT, 1])
    with nc.Block() as block:
        @block.sync
        def _(sp):
            sp.wait_ge(S("end"), 1)
            _, ends = nc.values_load_multi_w_load_instructions(
                end[0:1, 0:E], engines=[ENGINE.SP], min_val=0, max_val=E * REGION - ROWS_OF_TILE,
                skip_runtime_bounds_check_because="a region has a tile more than its expert can fill")
            for e in range(E):
                sp.dma_start(k.xs[bass.ds(ends[e], ROWS_OF_TILE), :].rearrange("(s p) d -> p s d", p=P),
                             k.zero[:, :, :].to_broadcast([P, ROWS_OF_TILE // P, D])).then_inc(S("zeros"), 16)
            sp.wait_ge(S("zeros"), 16 * E)

        @block.gpsimd
        def _(pool):
            nc.gpsimd.memset(k.acc[:, :, :], 0.0).then_inc(S("cleared"), 1)
            pool.wait_ge(S("cleared"), 1)

        @block.scalar
        def _(act):
            act.wait_ge(S("gap"), 1)
            nc.scalar.activation(e2[:, :, :], gap[:, :, :], ACT.Exp).then_inc(S("e2"), 1)

        @block.vector
        def _(dve):
            chain = [0]

            def link(ins):
                chain[0] += 1
                ins.then_inc(S("step"), 1)
                dve.wait_ge(S("step"), chain[0])

            nc.vector.tensor_copy(end[:, :], k.run[0:1, 0, :]).then_inc(S("end"), 1)
            nc.vector.memset(ones8[:, :], 1.0)
            nc.vector.tensor_tensor(gap[:, :, :], k.best[:, :, 1:2], k.best[:, :, 0:1], ALU.subtract).then_inc(S("gap"), 1)
            nc.vector.tensor_scalar(start[:, :], k.iota[0:TB, 0:MOST], float(ROWS_OF_TILE), None, ALU.mult)
            link(nc.vector.tensor_scalar(region[:, :], k.iota8[:, :], float(REGION), None, ALU.mult))
            link(nc.vector.tensor_tensor(count[:, :, 0], k.run[:, 0, :], region[:, :], ALU.subtract))
            link(nc.vector.tensor_tensor(begun[:, :, :], start[:, :].rearrange("p (z j) -> p z j", z=1).to_broadcast([TB, E, MOST]),
                                         count[:, :, :].to_broadcast([TB, E, MOST]), ALU.is_lt))
            link(nc.vector.tensor_reduce(tiles[:, :], begun[:, :, :], AX.X, ALU.add))
            link(nc.vector.tensor_tensor_scan(tiles_upto[:, :], ones8[:, :], tiles[:, :], 0.0, ALU.mult, ALU.add))
            link(nc.vector.tensor_tensor(tiles_before[:, 0, :], tiles_upto[:, :], tiles[:, :], ALU.subtract))
            link(nc.vector.tensor_scalar(last_tile[:, 0, :], tiles[:, :], -1.0, 0.0, ALU.add, ALU.max))
            link(nc.vector.scalar_tensor_tensor(shift[:, 0, :], tiles_before[:, 0, :], float(ROWS_OF_TILE), region[:, :], ALU.mult, ALU.subtract))
            link(nc.vector.tensor_tensor(past[:, :, :], tiles_upto[0:1, 0:E - 1].rearrange("o (z e) -> o z e", z=1).to_broadcast([1, NT, E - 1]),
                                         k.iota[0:1, 0:NT].rearrange("o (t z) -> o t z", z=1).to_broadcast([1, NT, E - 1]), ALU.is_le))
            link(nc.vector.tensor_reduce(expertf[:, :, 0], past[:, :, :], AX.X, ALU.add))
            link(nc.vector.tensor_copy(k.expert[:, :], expertf[:, :, 0]))
            each = k.iota8[0:1, :].rearrange("o (z e) -> o z e", z=1).to_broadcast([1, NT, E])
            link(nc.vector.tensor_tensor(own[:, :, :], each, expertf[:, :, :].to_broadcast([1, NT, E]), ALU.is_equal))
            for value, into in ((tiles_before, local), (last_tile, limit)):
                link(nc.vector.tensor_tensor(part[:, :, :], own[:, :, :], value[0:1, :, :].to_broadcast([1, NT, E]), ALU.mult))
                link(nc.vector.tensor_reduce(into[:, :, 0], part[:, :, :], AX.X, ALU.add))
            link(nc.vector.tensor_tensor(local[:, :, 0], k.iota[0:1, 0:NT], local[:, :, 0], ALU.subtract))
            link(nc.vector.tensor_tensor(local[:, :, 0], local[:, :, 0], limit[:, :, 0], ALU.min))
            link(nc.vector.tensor_scalar(local[:, :, 0], local[:, :, 0], float(ROWS_OF_TILE), None, ALU.mult))
            link(nc.vector.scalar_tensor_tensor(local[:, :, 0], expertf[:, :, 0], float(REGION), local[:, :, 0], ALU.mult, ALU.add))
            link(nc.vector.tensor_copy(k.tile_row[:, :], local[:, :, 0]))
            dve.wait_ge(S("e2"), 1)
            link(nc.vector.tensor_scalar(den[:, :, :], e2[:, :, :], 1.0, None, ALU.add))
            link(nc.vector.reciprocal(k.share[:, :, 0:1], den[:, :, :]))
            link(nc.vector.tensor_tensor(k.share[:, :, 1:2], k.share[:, :, 0:1], e2[:, :, :], ALU.mult))
            every = k.iota8[:, :].rearrange("p (z e) -> p z e", z=1).to_broadcast([TB, NB, E])
            for j in range(2):
                link(nc.vector.tensor_tensor(hit[:, :, :], every, k.chosen[:, :, j:j + 1].to_broadcast([TB, NB, E]), ALU.is_equal))
                link(nc.vector.tensor_tensor(hit[:, :, :], hit[:, :, :], shift[:, :, :].to_broadcast([TB, NB, E]), ALU.mult))
                link(nc.vector.tensor_reduce(moved[:, :, j], hit[:, :, :], AX.X, ALU.add))
            link(nc.vector.tensor_tensor(moved[:, :, :], moved[:, :, :], k.sent[:, :, :], ALU.add))
            link(nc.vector.tensor_copy(k.slots[:, :, :], moved[:, :, :]))


def experts(k):
    nc, a = k.nc, k.a
    S = lambda name: k.sem(f"ex_{name}")
    SUB = ROWS_OF_TILE // P
    b1 = k.sb("ex_b1", [P, E, KH])
    b2 = k.sb("ex_b2", [P, E, D])
    gamma = k.sb("ex_gamma", [P, KD])
    beta = k.sb("ex_beta", [P, KD])
    xs = k.sb("ex_xs", [P, 2, SUB, D])
    w1p = k.sb("ex_w1p", [P, 2, 2, KD, HID], F32R)
    b1s = k.sb("ex_b1s", [P, 2, KH])
    xT = k.sb("ex_xT", [P, 2, KD, ROWS_OF_TILE])
    hT = k.sb("ex_hT", [P, 2, KH, ROWS_OF_TILE])
    xp = k.sb("ex_xp", [P, 2, 2, KD, ROWS_OF_TILE], F32R)
    out = k.sb("ex_out", [P, 2, SUB, D])
    ps = k.ps
    psX = [ps[:, q, 0:KD * ROWS_OF_TILE].rearrange("p (h n) -> p h n", h=KD) for q in range(2)]
    psH = [[ps[:, 2 + 2 * q + c // 2, (c % 2) * ROWS_OF_TILE:(c % 2 + 1) * ROWS_OF_TILE] for c in range(KH)] for q in range(2)]
    psY = [ps[:, 6 + q, 0:SUB * D].rearrange("p (s d) -> p s d", s=SUB) for q in range(2)]
    tile_rows = lambda ap, t: ap[bass.ds(t * ROWS_OF_TILE, ROWS_OF_TILE), :].rearrange("(s p) d -> p s d", p=P)

    def expert_of(engine, t, count):
        _, which = nc.values_load_multi_w_load_instructions(
            k.expert[0:1, bass.ds(t, count)], engines=[engine], min_val=0, max_val=E - 1,
            skip_runtime_bounds_check_because="a count of seven comparisons")
        return which

    with nc.Block() as block:
        @block.sync
        def _(sp):
            sp.dma_start(b1[:, :, :], a["L0_ffn_b1"].rearrange("e p c -> p e c")).then_inc(S("b1"), 16)
            with nc.allow_non_contiguous_dma("256 words of each, once"):
                sp.dma_start(gamma[:, :], a["L0_ffn_gamma"].rearrange("o (h p) -> p (o h)", p=P)).then_inc(S("norm"), 16)
                sp.dma_start(beta[:, :], a["L0_ffn_beta"].rearrange("o (h p) -> p (o h)", p=P)).then_inc(S("norm"), 16)

            def rows_from(t, count):
                _, at = nc.values_load_multi_w_load_instructions(
                    k.tile_row[0:1, bass.ds(t, count)], engines=[ENGINE.SP], min_val=0, max_val=E * REGION - ROWS_OF_TILE,
                    skip_runtime_bounds_check_because="a tile of an expert's region")
                return at

            def load(row, q):
                sp.dma_start(xs[:, q, :, :], k.xs[bass.ds(row, ROWS_OF_TILE), :].rearrange("(s p) d -> p s d", p=P)).then_inc(S(f"xs{q}"), 16)

            def store(t, q):
                sp.wait_ge(S("evicted"), t + 3)
                sp.dma_start(tile_rows(k.ys, t), out[:, q, :, :]).then_inc(S(f"stored{q}"), 16)

            def step(t, q, row):
                sp.wait_ge(S("turned"), t + 1)
                load(row, q)
                store(t - 1, 1 - q)

            at = rows_from(0, 3)
            load(at[0], 0)
            load(at[1], 1)
            for e in range(E):
                sp.dma_start(b2[:, e, :], a["L0_ffn_b2"][e:e + 1, :].to_broadcast([P, D])).then_inc(S("b2"), 16)
            sp.wait_ge(S("turned"), 1)
            load(at[2], 0)
            with sp.Fori(0, NT // 2 - 2) as i:
                at = rows_from(i * 2 + 3, 2)
                step(i * 2 + 1, 1, at[0])
                step(i * 2 + 2, 0, at[1])
            at = rows_from(NT - 1, 1)
            step(NT - 3, 1, at[0])
            for t in range(NT - 3, NT):
                store(t, t % 2)
            for q in range(2):
                sp.wait_ge(S(f"stored{q}"), 16 + 16 * (NT // 2))

        @block.gpsimd
        def _(pool):
            pool.wait_ge(S("b1"), 16)
            with pool.Fori(0, NT // 2) as i:
                which = expert_of(ENGINE.Pool, i * 2, 2)
                for q in range(2):
                    t = i * 2 + q
                    pool.wait_ge(S("gelu"), t + 1)
                    pool.sem_inc(S("pause"), 1)
                    nc.gpsimd.tensor_copy(b1s[:, q, :], b1[:, bass.ds(which[q], 1), :].rearrange("p o c -> p (o c)")).then_inc(S("b1s"), 1)
                    pool.wait_ge(S("w1_high"), t + 1)
                    pool.sem_inc(S("pause"), 1)
                    mine = k.w1[:, bass.ds(which[q], 1), :, :].rearrange("p o h n -> p (o h) n")
                    nc.gpsimd.tensor_tensor(w1p[:, q, 1, :, :], mine, w1p[:, q, 0, :, :], ALU.subtract).then_inc(S("w1p"), 1)

        @block.tensor
        def _(pe):
            pe.sem_inc(S("up"), 4)
            pe.sem_inc(S("down"), 2)

            def turn(i, q):
                pe.wait_ge(S(f"xs{q}"), i * 16 + 16)
                pe.sem_inc(S("pause"), 1)
                for s in range(SUB):
                    for h in range(KD):
                        last = nc.tensor.transpose(psX[q][:, h, s * P:(s + 1) * P], xs[:, q, s, h * P:(h + 1) * P], k.ident[:, :])
                last.then_inc(S("turned"), 1)

            def up(t, q):
                pe.wait_ge(S("xp"), t + 1)
                pe.wait_ge(S("w1p"), t + 1)
                for c in range(KH):
                    for h in range(KD):
                        for m, (v, w) in enumerate(PASSES):
                            last = nc.tensor.matmul(psH[q][c], w1p[:, q, v, h, c * P:(c + 1) * P], xp[:, q, w, h, :],
                                                    start=(h == 0 and m == 0), stop=(h == KD - 1 and m == 2))
                    if c % 2:
                        last.then_inc(S("up"), 1)

            def down(t, q, e):
                pe.wait_ge(S("gelu"), t + 3)
                pe.wait_ge(S("evicted"), t + 1)
                for s in range(SUB):
                    for c in range(KH):
                        last = nc.tensor.matmul(psY[q][:, s, :], hT[:, q, c, s * P:(s + 1) * P],
                                                k.w2[:, bass.ds(e, 1), c, :].rearrange("p o n -> p (o n)"), start=(c == 0), stop=(c == KH - 1))
                last.then_inc(S("down"), 1)

            turn(0, 0)
            turn(0, 1)
            up(0, 0)
            with pe.Fori(0, NT // 2 - 1) as i:
                which = expert_of(ENGINE.PE, i * 2, 2)
                for q in range(2):
                    turn(i + 1, q)
                    up(i * 2 + (1 + q), 1 - q)
                    down(i * 2 + q, q, which[q])
            which = expert_of(ENGINE.PE, NT - 2, 2)
            up(NT - 1, 1)
            down(NT - 2, 0, which[0])
            down(NT - 1, 1, which[1])

        @block.scalar
        def _(act):
            act.sem_inc(S("gelu"), 2)

            def high(q, e):
                nc.scalar.copy(w1p[:, q, 0, :, :], k.w1[:, bass.ds(e, 1), :, :].rearrange("p o h n -> p (o h) n")).then_inc(S("w1_high"), 1)

            def gelu(t, q):
                act.wait_ge(S("down"), t + 1)
                act.wait_ge(S("b1s"), t + 1)
                for c in range(KH):
                    if c % 2 == 0:
                        act.wait_ge(S("up"), t * 2 + (5 + c // 2))
                    last = nc.scalar.activation(hT[:, q, c, :], psH[q][c], ACT.Gelu, bias=b1s[:, q, c:c + 1])
                last.then_inc(S("gelu"), 1)

            which = expert_of(ENGINE.Activation, 0, 2)
            for q in range(2):
                high(q, which[q])
            with act.Fori(0, NT // 2 - 1) as i:
                which = expert_of(ENGINE.Activation, i * 2 + 2, 2)
                for q in range(2):
                    gelu(i * 2 + q, q)
                    high(q, which[q])
            for q in range(2):
                gelu(NT - 2 + q, q)

        @block.vector
        def _(dve):
            dve.sem_inc(S("evicted"), 2)
            for q in range(2):
                dve.sem_inc(S(f"stored{q}"), 16)
            dve.wait_ge(S("norm"), 32)

            def scale(t, q):
                dve.wait_ge(S("turned"), t + 1)
                dve.wait_ge(S("up"), t * 2 + 2)
                dve.sem_inc(S("pause"), 1)
                for h in range(KD):
                    last = nc.vector.tensor_scalar(xT[:, q, h, :], psX[q][:, h, :], gamma[:, h:h + 1], beta[:, h:h + 1], ALU.mult, ALU.add)
                last.then_inc(S("xT"), 1)
                dve.wait_ge(S("xT"), t + 1)
                dve.sem_inc(S("pause"), 1)
                nc.vector.tensor_copy(xp[:, q, 0, :, :], xT[:, q, :, :]).then_inc(S("x_high"), 1)
                dve.wait_ge(S("x_high"), t + 1)
                dve.sem_inc(S("pause"), 1)
                nc.vector.tensor_tensor(xp[:, q, 1, :, :], xT[:, q, :, :], xp[:, q, 0, :, :], ALU.subtract).then_inc(S("xp"), 1)

            def evict(t, i, q, e):
                dve.wait_ge(S("down"), t + 3)
                dve.wait_ge(S(f"stored{q}"), i * 16 + 16)
                dve.sem_inc(S("pause"), 1)
                nc.vector.tensor_tensor(out[:, q, :, :], psY[q], b2[:, bass.ds(e, 1), :].to_broadcast([P, SUB, D]), ALU.add).then_inc(S("evicted"), 1)

            scale(0, 0)
            scale(1, 1)
            dve.wait_ge(S("b2"), 16 * E)
            with dve.Fori(0, NT // 2 - 1) as i:
                which = expert_of(ENGINE.DVE, i * 2, 2)
                for q in range(2):
                    scale(i * 2 + (2 + q), q)
                    evict(i * 2 + q, i, q, which[q])
            which = expert_of(ENGINE.DVE, NT - 2, 2)
            for q in range(2):
                evict(NT - 2 + q, NT // 2 - 1, q, which[q])


def ffn1(k):
    nc, a = k.nc, k.a
    S = lambda name: k.sem(f"f1_{name}")
    K = 2
    w1 = k.sb("f1w1", [P, K, KD, HID])
    w2 = k.sb("f1w2", [P, K, KH, D])
    w2s = w2
    b1 = k.sb("f1b1", [P, K, KH])
    b2 = k.sb("f1b2", [1, K, D])
    b2m = k.sb("f1b2m", [1, K, D])
    bias = k.sb("f1bias", [TB, 1, D])
    gamma = k.sb("f1gamma", [TB, 1, D])
    beta = k.sb("f1beta", [TB, 1, D])
    wr = k.sb("f1wr", [P, KD, E])
    br = k.sb("f1br", [1, E])
    ones = k.sb("f1ones", [1, P])
    mean = k.sb("f1mean", [P, KD])
    row = k.sb("f1row", [1, 8, E])
    best = k.sb("f1best", [1, 8])
    besti = k.sb("f1besti", [1, 8], U32)
    pair = k.sb("f1pair", [1, 4])
    pcol = k.sb("f1pcol", [P, K])
    xg = k.sb("f1xg", [TB, 2, 2, D])
    yg = k.sb("f1yg", [TB, 2, 2, D])
    res = k.sb("f1res", [TB, 2, 2, D])
    z = k.sb("f1z", [TB, 2, 2, D])
    st = k.sb("f1st", [TB, 2, 2, 6])
    mv = k.sb("f1mv", [TB, 2, 2, 2])
    hT = k.sb("f1hT", [P, 2, K, KH, GTOK])
    w1p = k.sb("f1w1p", [P, 2, K, KD, HID], F32R)
    w2p = k.sb("f1w2p", [P, 2, K, KH, D], F32R)
    xp = k.sb("f1xp", [P, 2, 2, KD, GTOK], F32R)
    hp = k.sb("f1hp", [P, 2, 2, K, KH, GTOK], F32R)
    ps = k.ps
    psH = [[ps[:, 2 * q + c // 2, (c % 2) * 256:(c % 2) * 256 + GTOK] for c in range(KH)] for q in range(2)]
    psY = [ps[0:TB, 4 + q, 0:2 * D].rearrange("p (t d) -> p t d", t=2) for q in range(2)]
    with nc.Block() as block:
        @block.sync
        def _(sp):
            for dst, src in [(gamma[:, 0, :], a["L1_ffn_gamma"].to_broadcast([TB, D])), (beta[:, 0, :], a["L1_ffn_beta"].to_broadcast([TB, D])),
                             (wr[:, :, :], a["L1_ffn_Wr"].rearrange("(h p) e -> p h e", p=P)), (br[:, :], a["L1_ffn_br"])]:
                sp.dma_start(dst, src).then_inc(S("small"), 16)
            sp.wait_ge(S("besti"), 1)
            _, which = nc.values_load_multi_w_load_instructions(
                besti[0:1, 0:K].bitcast(I32), engines=[ENGINE.SP], min_val=0, max_val=E - 1,
                skip_runtime_bounds_check_because="a place in a row of eight")
            for j in range(K):
                sp.dma_start(w1[:, j, :, :], a["L1_ffn_W1"][bass.ds(which[j], 1), :, :].rearrange("o (h p) n -> p (o h) n", p=P)).then_inc(S("w"), 16)
                sp.dma_start(w2[:, j, :, :], a["L1_ffn_W2"][bass.ds(which[j], 1), :, :].rearrange("o (c p) n -> p (o c) n", p=P)).then_inc(S("w"), 16)
                sp.dma_start(b1[:, j, :], a["L1_ffn_b1"][bass.ds(which[j], 1), :, :].rearrange("o p c -> p (o c)")).then_inc(S("w"), 16)
                sp.dma_start(b2[:, j, :], a["L1_ffn_b2"][bass.ds(which[j], 1), :]).then_inc(S("w"), 16)

        @block.tensor
        def _(pe):
            for h in range(KD):
                last = nc.tensor.matmul(ps[:, 0, h:h + 1], k.ysum[:, h * P:(h + 1) * P], k.ones[0:TB, :], start=True, stop=True)
            last.then_inc(S("mean_ps"), 1)
            pe.wait_ge(S("small"), 64)
            pe.wait_ge(S("mean"), 1)
            for h in range(KD):
                last = nc.tensor.matmul(ps[0:1, 1, 0:E], mean[:, h:h + 1], wr[:, h, :], start=(h == 0), stop=(h == KD - 1))
            last.then_inc(S("logit_ps"), 1)
            pe.wait_ge(S("pair"), 1)
            nc.tensor.matmul(ps[:, 2, 0:K], ones[:, :], pair[:, 0:K], start=True, stop=True).then_inc(S("pcol_ps"), 1)
            pe.wait_ge(S("b2m"), 1)
            for j in range(K):
                last = nc.tensor.matmul(ps[0:TB, 3, 0:D], ones[:, 0:TB], b2m[:, j, :], start=(j == 0), stop=(j == K - 1))
            last.then_inc(S("bias_ps"), 1)

        @block.gpsimd
        def _(pool):
            pool.wait_ge(S("w"), 16 * 4 * K)
            nc.gpsimd.tensor_copy(w1p[:, 0, :, :, :], w1[:, :, :, :]).then_inc(S("w1p"), 1)
            pool.wait_ge(S("w1p"), 1)
            nc.gpsimd.tensor_tensor(w1p[:, 1, :, :, :], w1[:, :, :, :], w1p[:, 0, :, :, :], ALU.subtract).then_inc(S("w1p"), 1)
            pool.wait_ge(S("w1p"), 2)

        @block.scalar
        def _(act):
            act.wait_ge(S("mean_ps"), 1)
            nc.scalar.mul(mean[:, :], ps[:, 0, 0:KD], 1.0 / N).then_inc(S("mean"), 1)
            for n in range(2):
                act.wait_ge(S("shifted"), n + 1)
                nc.scalar.activation(row[:, 2, :], row[:, 1, :], ACT.Exp).then_inc(S("ex"), 1)
            act.wait_ge(S("gap"), 1)
            nc.scalar.activation(pair[:, 3:4], pair[:, 2:3], ACT.Exp).then_inc(S("ex"), 1)

        @block.vector
        def _(dve):
            done = [0]

            def link(ins):
                done[0] += 1
                ins.then_inc(S("chain"), 1)
                dve.wait_ge(S("chain"), done[0])

            link(nc.vector.memset(ones[:, :], 1.0))
            dve.wait_ge(S("logit_ps"), 1)
            link(nc.vector.tensor_tensor(row[:, 0, :], ps[0:1, 1, 0:E], br[:, :], ALU.add))

            def softmax(n):
                link(nc.vector.tensor_reduce(row[:, 4, 0:1], row[:, 0, :], AX.X, ALU.max))
                nc.vector.tensor_scalar(row[:, 1, :], row[:, 0, :], row[:, 4, 0:1], None, ALU.subtract).then_inc(S("shifted"), 1)
                dve.wait_ge(S("ex"), n)
                link(nc.vector.tensor_reduce(row[:, 4, 1:2], row[:, 2, :], AX.X, ALU.add))
                link(nc.vector.reciprocal(row[:, 4, 2:3], row[:, 4, 1:2]))
                link(nc.vector.tensor_scalar(row[:, 3, :], row[:, 2, :], row[:, 4, 2:3], None, ALU.mult))

            softmax(1)
            link(nc.vector.tensor_scalar(row[:, 5, :], row[:, 3, :], float(N), CAPACITY, ALU.mult, ALU.max))
            link(nc.vector.reciprocal(row[:, 5, :], row[:, 5, :]))
            link(nc.vector.tensor_scalar(row[:, 5, :], row[:, 5, :], CAPACITY, None, ALU.mult))
            link(nc.vector.tensor_tensor(row[:, 0, :], row[:, 3, :], row[:, 5, :], ALU.mult))
            softmax(2)
            link(nc.vector.max(best[:, :], row[:, 3, :]))
            nc.vector.max_index(besti[:, :], best[:, :], row[:, 3, :]).then_inc(S("besti"), 1)
            nc.vector.tensor_tensor(pair[:, 2:3], best[:, 1:2], best[:, 0:1], ALU.subtract).then_inc(S("gap"), 1)
            dve.wait_ge(S("ex"), 3)
            link(nc.vector.tensor_scalar(row[:, 6, 0:1], pair[:, 3:4], 1.0, None, ALU.add))
            link(nc.vector.reciprocal(pair[:, 0:1], row[:, 6, 0:1]))
            nc.vector.tensor_tensor(pair[:, 1:2], pair[:, 0:1], pair[:, 3:4], ALU.mult).then_inc(S("pair"), 1)
            dve.wait_ge(S("pcol_ps"), 1)
            link(nc.vector.tensor_copy(pcol[:, :], ps[:, 2, 0:K]))
            dve.wait_ge(S("w"), 16 * 4 * K)
            for j in range(K):
                link(nc.vector.tensor_scalar(w2s[:, j, :, :], w2[:, j, :, :], pcol[:, j:j + 1], None, ALU.mult))
            link(nc.vector.tensor_scalar(b2m[:, 0, :], b2[:, 0, :], pcol[0:1, 0:1], None, ALU.mult))
            nc.vector.tensor_scalar(b2m[:, 1, :], b2[:, 1, :], pcol[0:1, 1:2], None, ALU.mult).then_inc(S("b2m"), 1)
            dve.wait_ge(S("bias_ps"), 1)
            nc.vector.tensor_copy(bias[:, 0, :], ps[0:TB, 3, 0:D])
            for j in range(K):
                link(nc.vector.tensor_copy(w2p[:, 0, j, :, :], w2s[:, j, :, :]))
                link(nc.vector.tensor_tensor(w2p[:, 1, j, :, :], w2s[:, j, :, :], w2p[:, 0, j, :, :], ALU.subtract))

    with nc.Block() as block:
        @block.sync
        def _(sp):
            group = lambda ap, g: ap[bass.ds(g * GTOK, GTOK), :].rearrange("(t p) d -> p t d", p=TB)

            def load(g, q):
                sp.dma_start(yg[:, q, :, :], group(k.y3, g)).then_inc(S(f"in{q}"), 16)
                sp.dma_start(xg[:, q, :, :], group(k.x3, g)).then_inc(S(f"in{q}"), 16)

            def store(g, q):
                sp.wait_ge(S("out"), g + 1)
                sp.dma_start(group(a["out"], g), res[:, q, :, :]).then_inc(S(f"stored{q}"), 16)

            for q in range(2):
                load(q, q)
            with sp.Fori(0, NG // 2 - 1) as i:
                for q in range(2):
                    store(i * 2 + q, q)
                    load(i * 2 + (2 + q), q)
            store(NG - 3, 0)
            load(NG - 1, 0)
            store(NG - 2, 1)
            store(NG - 1, 0)
            for q in range(2):
                sp.wait_ge(S(f"stored{q}"), 16 * (1 + NG // 2 + (NG - q) % 2))

        @block.tensor
        def _(pe):
            pe.sem_inc(S("down"), 2)
            pe.sem_inc(S("up"), 2 * K)

            def up(g, q):
                pe.wait_ge(S("xp"), g + 1)
                for j in range(K):
                    pe.wait_ge(S("gelu"), g * K + (j + 1))
                    for c in range(KH):
                        for h in range(KD):
                            for m, (v, w) in enumerate(PASSES):
                                last = nc.tensor.matmul(psH[j][c], w1p[:, v, j, h, c * P:(c + 1) * P], xp[:, q, w, h, :],
                                                        start=(h == 0 and m == 0), stop=(h == KD - 1 and m == 2))
                    last.then_inc(S("up"), 1)

            def down(g, q):
                pe.wait_ge(S("hp"), g * K + K)
                pe.wait_ge(S("read"), g + 1)
                for tt in range(2):
                    for j in range(K):
                        for c in range(KH):
                            for m, (v, w) in enumerate(PASSES):
                                last = nc.tensor.matmul(psY[q][:, tt, :], hp[:, q, v, j, c, tt * TB:(tt + 1) * TB], w2p[:, w, j, c, :],
                                                        start=(j == 0 and c == 0 and m == 0), stop=(j == K - 1 and c == KH - 1 and m == 2))
                last.then_inc(S("down"), 1)

            up(0, 0)
            with pe.Fori(0, NG // 2) as i:
                for q in range(2):
                    up(i * 2 + (1 + q), 1 - q)
                    down(i * 2 + q, q)
            down(NG - 1, 0)

        @block.scalar
        def _(act):
            act.sem_inc(S("gelu"), 2)

            def gelu(g, q):
                act.wait_ge(S("down"), g + 1)
                for j in range(K):
                    act.wait_ge(S("up"), g * K + (j + 1 + 2 * K))
                    for c in range(KH):
                        last = nc.scalar.activation(hT[:, q, j, c, :], psH[j][c], ACT.Gelu, bias=b1[:, j, c:c + 1])
                    last.then_inc(S("gelu"), 1)
                    act.wait_ge(S("gelu"), g * K + (j + 3))
                    act.sem_inc(S("pause"), 1)
                    nc.scalar.copy(hp[:, q, 0, j, :, :], hT[:, q, j, :, :]).then_inc(S("h_high"), 1)

            gelu(0, 0)
            with act.Fori(0, NG // 2) as i:
                for q in range(2):
                    gelu(i * 2 + (1 + q), 1 - q)
                    root_step(k, "f1", act, mv[:, q, :, :], i * 2 + (1 + q))
            root_step(k, "f1", act, mv[:, 0, :, :], NG)

        @block.vector
        def _(dve):
            dve.sem_inc(S("read"), 2)
            for q in range(2):
                dve.sem_inc(S(f"stored{q}"), 16)
            both = lambda row: row[:, :, :].to_broadcast([TB, 2, D])

            def finish(g, i, q):
                n = g + 1
                dve.wait_ge(S(f"in{q}"), i * 32 + 32)
                nc.vector.tensor_tensor(yg[:, q, :, :], yg[:, q, :, :], both(bias), ALU.add).then_inc(S("biased"), 1)
                nc.vector.tensor_tensor(xg[:, q, :, :], xg[:, q, :, :], both(beta), ALU.add).then_inc(S("shifted_x"), 1)
                dve.wait_ge(S("biased"), n)
                dve.wait_ge(S("down"), n + 2)
                nc.vector.tensor_tensor(yg[:, q, :, :], psY[q], yg[:, q, :, :], ALU.add).then_inc(S("read"), 1)
                dve.wait_ge(S("read"), n + 2)
                norm_steps(k, "f1", dve, yg[:, q, :, :], st[:, q, :, :], mv[:, q, :, :], z[:, q, :, :], n).then_inc(S("normed"), 1)
                dve.wait_ge(S("normed"), n)
                nc.vector.tensor_tensor(z[:, q, :, :], z[:, q, :, :], both(gamma), ALU.mult).then_inc(S("scaled"), 1)
                dve.wait_ge(S("scaled"), n)
                dve.wait_ge(S("shifted_x"), n)
                dve.wait_ge(S(f"stored{q}"), i * 16 + 16)
                nc.vector.tensor_tensor(res[:, q, :, :], z[:, q, :, :], xg[:, q, :, :], ALU.add).then_inc(S("out"), 1)

            def split_x(g, q):
                dve.wait_ge(S("up"), g * K + K)
                dve.sem_inc(S("pause"), 1)
                mine = k.acc[:, 0:KD, bass.ds(g * GTOK, GTOK)]
                nc.vector.tensor_copy(xp[:, q, 0, :, :], mine).then_inc(S("x_high"), 1)
                dve.wait_ge(S("x_high"), g + 1)
                dve.sem_inc(S("pause"), 1)
                nc.vector.tensor_tensor(xp[:, q, 1, :, :], mine, xp[:, q, 0, :, :], ALU.subtract).then_inc(S("xp"), 1)

            def split_h(g, q):
                for j in range(K):
                    dve.wait_ge(S("h_high"), g * K + (j + 1))
                    dve.sem_inc(S("pause"), 1)
                    nc.vector.tensor_tensor(hp[:, q, 1, j, :, :], hT[:, q, j, :, :], hp[:, q, 0, j, :, :], ALU.subtract).then_inc(S("hp"), 1)

            split_x(0, 0)
            split_x(1, 1)
            split_h(0, 0)
            with dve.Fori(0, NG // 2 - 1) as i:
                for q in range(2):
                    split_x(i * 2 + (2 + q), q)
                    split_h(i * 2 + (1 + q), 1 - q)
                    finish(i * 2 + q, i, q)
            split_x(NG - 1, 0)
            split_h(NG - 2, 1)
            finish(NG - 3, NG // 2 - 1, 0)
            split_h(NG - 1, 0)
            finish(NG - 2, NG // 2 - 1, 1)
            finish(NG - 1, NG // 2, 0)


_PLAIN = ["x", "L0_gnn_W", "L1_gnn_W", "L0_ffn_Wr", "L0_ffn_W1", "L0_ffn_W2", "L0_ffn_b2",
          "L1_ffn_Wr", "L1_ffn_W1", "L1_ffn_W2", "L1_ffn_b2"]
_ROWS = ["L0_ffn_gamma", "L0_ffn_beta", "L0_ffn_br", "L1_ffn_gamma", "L1_ffn_beta", "L1_ffn_br"]


def laid_out(inputs):
    import numpy as np

    out = {n: np.ascontiguousarray(inputs[n]) for n in _PLAIN}
    out.update({n: np.ascontiguousarray(inputs[n]).reshape(1, -1) for n in _ROWS})
    for n in ("L0_ffn_b1", "L1_ffn_b1"):
        out[n] = np.ascontiguousarray(np.asarray(inputs[n]).reshape(E, KH, P).transpose(0, 2, 1))
    pad = TILES * P - NE
    src, dst = np.asarray(inputs["src"]), np.asarray(inputs["dst"])
    dist = np.asarray(inputs["edge_attr3_1x1"]).reshape(-1)
    nodest = np.full(pad, -1, dst.dtype)
    dstp = np.concatenate([dst, nodest])
    edge_major = lambda v: np.ascontiguousarray(v.reshape(TILES, P).T)
    out["src_e"] = edge_major(np.concatenate([src, np.zeros(pad, src.dtype)]))
    out["dst_e"] = edge_major(dstp)
    out["dist_e"] = edge_major(np.concatenate([dist, np.zeros(pad, dist.dtype)]))
    out["dst_t"] = dstp.reshape(TILES, P)
    out["dst_prev_t"] = np.concatenate([np.full(1, -2, dst.dtype), dstp[:-1]]).reshape(TILES, P)
    out["dst_next_t"] = np.concatenate([dstp[1:], np.full(1, -2, dst.dtype)]).reshape(TILES, P)
    out["n0"] = np.ascontiguousarray(dstp[::P]).reshape(1, TILES)
    for layer, (left, right) in enumerate([("L0_gnn_w_att_src", "L0_gnn_w_att_dst"), ("L1_gnn_attn_l", "L1_gnn_attn_r")]):
        H = HEADS[layer]
        DH = D // H
        att = np.zeros((D, 2 * H), np.float32)
        for side, name in enumerate((left, right)):
            v = np.asarray(inputs[name]).reshape(H, DH)
            for h in range(H):
                att[h * DH:(h + 1) * DH, side * H + h] = v[h]
        out[f"att{layer}"] = att
        f = np.arange(D)
        spread = np.zeros((H, KD, P), np.float32)
        spread[f // DH, f // P, f % P] = 1
        out[f"spread{layer}"] = spread
    out["ident"] = np.eye(P, dtype=np.float32)
    out["before"] = np.triu(np.ones((TB, TB), np.float32), 1)
    out["iota"] = np.tile(np.arange(P, dtype=np.float32), (P, 1))
    out["part"] = np.arange(P, dtype=np.float32).reshape(P, 1)
    return out


def kernel(**inputs):
    from concourse import bacc
    from concourse.bass_utils import run_bass_kernel_spmd as run

    nc = bacc.Bacc("TRN2", target_bir_lowering=False, num_devices=1)
    arrays = laid_out(inputs)
    aps = {n: nc.dram_tensor("in_" + n, v.shape, mybir.dt.from_np(v.dtype), kind="ExternalInput").ap() for n, v in arrays.items()}
    aps["out"] = nc.dram_tensor("out_0", (N, D), F32, kind="ExternalOutput").ap()
    emit(nc, aps)
    r = run(nc, [{"in_" + n: v for n, v in arrays.items()}], core_ids=[0])
    return r.results[0]["out_0"]
```
